# Optimizing a Trainium2 kernel written in Bass

```python
import numpy as np
import jax
import jax.numpy as jnp

def _softmax(x, axis=-1):
    return jax.nn.softmax(x, axis=axis)

def _gelu(x):
    return jax.nn.gelu(x, approximate=True)

def _silu(x):
    return jax.nn.silu(x)

def _sigmoid(x):
    return jax.nn.sigmoid(x)

def _layernorm(x, axis=-1, eps=1e-05):
    m = jnp.mean(x, axis=axis, keepdims=True)
    v = jnp.var(x, axis=axis, keepdims=True)
    return (x - m) / jnp.sqrt(v + eps)

def _scatter_add(tgt, idx, src, axis=0):
    return tgt.at[idx].add(src)

def _segment_sum(src, seg, n):
    return jax.ops.segment_sum(src, seg, n)
kernel_name = 'mk_cond_resid_d2_seqx_r8_4f1b1a'

def setup_inputs(seed: int=0):
    np.random.seed(seed)
    _w = jnp.asarray

    def _rec_inputs():
        import jax
        import jax.numpy as jnp
        _rk = jax.random.key(seed)
        x = -0.0002928 + 1 * jax.random.normal(jax.random.fold_in(_rk, 1), (16, 128, 128), jnp.float32)
        _lenS = 128 - jax.random.randint(jax.random.fold_in(_rk, 7), (16,), 0, max(1, 128 // 4) + 1, jnp.int32)
        _lenS2 = 128 - jax.random.randint(jax.random.fold_in(_rk, 8), (16,), 0, max(1, 128 // 4) + 1, jnp.int32)
        fside_BxS_0 = 0.0061147 + 1.02565 * jax.random.normal(jax.random.fold_in(_rk, 12), (16, 128), jnp.float32)
        itok_BxSxS_0_4 = jax.random.randint(jax.random.fold_in(_rk, 13), (16, 128, 128), 0, 5, jnp.int32)
        fside_BxSxS_0 = -3.24666e-05 + 0.0312493 * jax.random.normal(jax.random.fold_in(_rk, 14), (16, 128, 128), jnp.float32)
        cond_2048 = -4.62462e-05 + 0.0441849 * jax.random.normal(jax.random.fold_in(_rk, 16), (16, 256), jnp.float32)
        _validS = jnp.arange(128)[None, :] < _lenS[:, None]
        _validS2 = jnp.arange(128)[None, :] < _lenS2[:, None]
        _causal = jnp.tril(jnp.ones((128, 128), dtype=bool))
        mask_BxS_ff1 = jnp.where(jnp.ones((16, 128), dtype=bool), 1.0, 0.0).astype(jnp.float32)
        mask_BxS_ff0 = jnp.where(jnp.ones((16, 128), dtype=bool), 0.0, -1000000000.0).astype(jnp.float32)
        return (x, fside_BxS_0, itok_BxSxS_0_4, fside_BxSxS_0, cond_2048, mask_BxS_ff1, mask_BxS_ff0)
    x, fside_BxS_0, itok_BxSxS_0_4, fside_BxSxS_0, cond_2048, mask_BxS_ff1, mask_BxS_ff0 = _rec_inputs()

    def _L0_cond_setup():
        import jax, jax.numpy as jnp
        import numpy as np
        B, N, D = (4, 128, 128)
        T_ITER = 4
        E_TYPES = 4
        ALPHA = 0.2

        def _lin_w(key, out_f, in_f):
            bound = float(np.sqrt(3.0 / ((in_f + out_f) / 2.0)))
            return jax.random.uniform(key, (out_f, in_f), minval=-bound, maxval=bound, dtype=jnp.float32)

        def _lin(x, w, b):
            return x @ w.T + b

        def _qdgat_forward(ents, ent_mask, q_encoding, adj, types, init_mem, w_qin, b_qin, w_qt, b_qt, w_pl, b_pl, w_pc, b_pc, w_q, b_q, w_k, b_k, w_v, b_v, w_pk, b_pk, w_pv, b_pv, wes, w_mu, b_mu, w_cb, b_cb):
            d = ents.shape[-1]
            x_loc = ents
            x_ctx = jnp.broadcast_to(init_mem, ents.shape)
            var_drop = ent_mask[:, :, None]
            adj_pos = adj > 0
            q_base = jax.nn.elu(_lin(q_encoding, w_qin, b_qin))
            n_types = wes.shape[0] + 1
            for t in range(T_ITER):
                cmd = _lin(q_base, w_qt[t], b_qt[t])
                xc = x_ctx * var_drop
                pl = _lin(x_loc, w_pl, b_pl)
                pc = _lin(xc, w_pc, b_pc)
                x_joint = jnp.concatenate([x_loc, xc, pl * pc], axis=-1)
                q = _lin(x_joint, w_q, b_q)
                k = _lin(x_joint, w_k, b_k) * _lin(cmd, w_pk, b_pk)[:, None, :]
                v = _lin(x_joint, w_v, b_v) * _lin(cmd, w_pv, b_pv)[:, None, :]
                edge_score = jnp.zeros(adj.shape, jnp.float32)
                for i in range(n_types):
                    if types >> i & 1 == 1:
                        w1, w2 = (wes[i - 1, :d], wes[i - 1, d:])
                        s = (q @ w1)[:, :, None] + (k @ w2)[:, None, :]
                        edge_score = edge_score + jnp.where(adj == i, s, 0.0)
                e = jnp.where(edge_score > 0, edge_score, ALPHA * edge_score)
                logits = jnp.where(adj_pos, e, jnp.float32(-9000000000000000.0))
                prob = jax.nn.softmax(logits, axis=-1)
                message = jnp.einsum('bij,bjd->bid', prob, v)
                x_ctx = _lin(jnp.concatenate([xc, message], axis=-1), w_mu, b_mu)
            return _lin(jnp.concatenate([x_loc, x_ctx], axis=-1), w_cb, b_cb)
        key = jax.random.key(seed)
        ks = jax.random.split(key, 32)
        inp = {}
        inp['ents'] = jax.random.normal(ks[0], (B, N, D), jnp.float32)
        inp['ent_mask'] = jnp.ones((B, N), jnp.float32)
        inp['q_encoding'] = jax.random.normal(ks[1], (B, D), jnp.float32)
        inp['adj'] = jax.random.randint(ks[2], (B, N, N), 0, E_TYPES + 1, dtype=jnp.int32)
        inp['types'] = 30
        inp['init_mem'] = jax.random.normal(ks[3], (1, D), jnp.float32)
        inp['w_qin'] = _lin_w(ks[4], D, D)
        inp['b_qin'] = jnp.zeros((D,), jnp.float32)
        inp['w_qt'] = jnp.stack([_lin_w(ks[5 + t], D, D) for t in range(T_ITER)])
        inp['b_qt'] = jnp.zeros((T_ITER, D), jnp.float32)
        inp['w_pl'] = _lin_w(ks[9], D, D)
        inp['b_pl'] = jnp.zeros((D,), jnp.float32)
        inp['w_pc'] = _lin_w(ks[10], D, D)
        inp['b_pc'] = jnp.zeros((D,), jnp.float32)
        inp['w_q'] = _lin_w(ks[11], D, 3 * D)
        inp['b_q'] = jnp.zeros((D,), jnp.float32)
        inp['w_k'] = _lin_w(ks[12], D, 3 * D)
        inp['b_k'] = jnp.zeros((D,), jnp.float32)
        inp['w_v'] = _lin_w(ks[13], D, 3 * D)
        inp['b_v'] = jnp.zeros((D,), jnp.float32)
        inp['w_pk'] = _lin_w(ks[14], D, D)
        inp['b_pk'] = jnp.zeros((D,), jnp.float32)
        inp['w_pv'] = _lin_w(ks[15], D, D)
        inp['b_pv'] = jnp.zeros((D,), jnp.float32)
        wb = 1.414 * float(np.sqrt(6.0 / (2 * D + 1)))
        inp['wes'] = jax.random.uniform(ks[16], (E_TYPES, 2 * D), minval=-wb, maxval=wb, dtype=jnp.float32)
        inp['w_mu'] = _lin_w(ks[17], D, 2 * D)
        inp['b_mu'] = jnp.zeros((D,), jnp.float32)
        inp['w_cb'] = _lin_w(ks[18], D, 2 * D)
        inp['b_cb'] = jnp.zeros((D,), jnp.float32)
        return inp
    _L0_cond_all = _L0_cond_setup()
    _L0_cond_in = {k: v for k, v in _L0_cond_all.items() if k in ('init_mem', 'w_qin', 'b_qin', 'w_pl', 'b_pl', 'w_pc', 'b_pc', 'w_q', 'b_q', 'w_k', 'b_k', 'w_v', 'b_v', 'w_pk', 'b_pk', 'w_pv', 'b_pv', 'w_mu', 'b_mu', 'w_cb', 'b_cb')}
    del _L0_cond_all

    def _L1_cond_setup():
        import jax, jax.numpy as jnp
        import numpy as np
        B, S, D_MODEL, D_INNER, D_STATE = (4, 512, 128, 256, 16)
        key = jax.random.key(seed)
        ks = jax.random.split(key, 12)
        inp = {'x': jax.random.normal(ks[0], (B, S, D_MODEL), jnp.float32), 't_emb': jax.random.normal(ks[1], (B, D_INNER), jnp.float32), 'W_in': jax.random.normal(ks[2], (2 * D_INNER, D_MODEL), jnp.float32) * 0.02, 'W_conv': jax.random.normal(ks[3], (D_INNER, 1, 4), jnp.float32) * 0.1, 'b_conv': jnp.zeros((D_INNER,), jnp.float32), 'ln_g': jnp.ones((D_INNER,), jnp.float32), 'ln_b': jnp.zeros((D_INNER,), jnp.float32), 'W_xproj': jax.random.normal(ks[4], (3 * D_STATE, D_INNER), jnp.float32) * 0.02, 'W_dt': jax.random.normal(ks[5], (D_STATE, D_STATE), jnp.float32) * 0.01, 'b_dt': jax.random.uniform(ks[6], (D_STATE,), jnp.float32) * 0.1, 'A_log': jax.random.normal(ks[7], (D_STATE,), jnp.float32) * 0.1, 'D': jnp.ones((D_INNER,), jnp.float32) * 0.1, 'W_out': jax.random.normal(ks[8], (D_MODEL, D_INNER), jnp.float32) * 0.02}
        return inp
    _L1_cond_all = _L1_cond_setup()
    _L1_cond_in = {k: v for k, v in _L1_cond_all.items() if k in ('W_in', 'W_conv', 'b_conv', 'ln_g', 'ln_b', 'W_xproj', 'W_dt', 'b_dt', 'A_log', 'D', 'W_out')}
    del _L1_cond_all
    return {'x': x, 'fside_BxS_0': fside_BxS_0, 'itok_BxSxS_0_4': itok_BxSxS_0_4, 'fside_BxSxS_0': fside_BxSxS_0, 'cond_2048': cond_2048, 'mask_BxS_ff1': mask_BxS_ff1, 'mask_BxS_ff0': mask_BxS_ff0, 'L0_cond_init_mem': _L0_cond_in['init_mem'], 'L0_cond_w_qin': _L0_cond_in['w_qin'], 'L0_cond_b_qin': _L0_cond_in['b_qin'], 'L0_cond_w_pl': _L0_cond_in['w_pl'], 'L0_cond_b_pl': _L0_cond_in['b_pl'], 'L0_cond_w_pc': _L0_cond_in['w_pc'], 'L0_cond_b_pc': _L0_cond_in['b_pc'], 'L0_cond_w_q': _L0_cond_in['w_q'], 'L0_cond_b_q': _L0_cond_in['b_q'], 'L0_cond_w_k': _L0_cond_in['w_k'], 'L0_cond_b_k': _L0_cond_in['b_k'], 'L0_cond_w_v': _L0_cond_in['w_v'], 'L0_cond_b_v': _L0_cond_in['b_v'], 'L0_cond_w_pk': _L0_cond_in['w_pk'], 'L0_cond_b_pk': _L0_cond_in['b_pk'], 'L0_cond_w_pv': _L0_cond_in['w_pv'], 'L0_cond_b_pv': _L0_cond_in['b_pv'], 'L0_cond_w_mu': _L0_cond_in['w_mu'], 'L0_cond_b_mu': _L0_cond_in['b_mu'], 'L0_cond_w_cb': _L0_cond_in['w_cb'], 'L0_cond_b_cb': _L0_cond_in['b_cb'], 'L1_cond_W_in': _L1_cond_in['W_in'], 'L1_cond_W_conv': _L1_cond_in['W_conv'], 'L1_cond_b_conv': _L1_cond_in['b_conv'], 'L1_cond_ln_g': _L1_cond_in['ln_g'], 'L1_cond_ln_b': _L1_cond_in['ln_b'], 'L1_cond_W_xproj': _L1_cond_in['W_xproj'], 'L1_cond_W_dt': _L1_cond_in['W_dt'], 'L1_cond_b_dt': _L1_cond_in['b_dt'], 'L1_cond_A_log': _L1_cond_in['A_log'], 'L1_cond_D': _L1_cond_in['D'], 'L1_cond_W_out': _L1_cond_in['W_out']}

def reference(x, fside_BxS_0, itok_BxSxS_0_4, fside_BxSxS_0, cond_2048, mask_BxS_ff1, mask_BxS_ff0, L0_cond_init_mem, L0_cond_w_qin, L0_cond_b_qin, L0_cond_w_pl, L0_cond_b_pl, L0_cond_w_pc, L0_cond_b_pc, L0_cond_w_q, L0_cond_b_q, L0_cond_w_k, L0_cond_b_k, L0_cond_w_v, L0_cond_b_v, L0_cond_w_pk, L0_cond_b_pk, L0_cond_w_pv, L0_cond_b_pv, L0_cond_w_mu, L0_cond_b_mu, L0_cond_w_cb, L0_cond_b_cb, L1_cond_W_in, L1_cond_W_conv, L1_cond_b_conv, L1_cond_ln_g, L1_cond_ln_b, L1_cond_W_xproj, L1_cond_W_dt, L1_cond_b_dt, L1_cond_A_log, L1_cond_D, L1_cond_W_out):
    import jax
    import jax.numpy as jnp

    def _L0_cond_ref(ents, ent_mask, q_encoding, adj, types, init_mem, w_qin, b_qin, w_qt, b_qt, w_pl, b_pl, w_pc, b_pc, w_q, b_q, w_k, b_k, w_v, b_v, w_pk, b_pk, w_pv, b_pv, wes, w_mu, b_mu, w_cb, b_cb):
        import jax, jax.numpy as jnp
        import numpy as np
        B, N, D = (4, 128, 128)
        T_ITER = 4
        E_TYPES = 4
        ALPHA = 0.2

        def _lin_w(key, out_f, in_f):
            bound = float(np.sqrt(3.0 / ((in_f + out_f) / 2.0)))
            return jax.random.uniform(key, (out_f, in_f), minval=-bound, maxval=bound, dtype=jnp.float32)

        def _lin(x, w, b):
            return x @ w.T + b

        def _qdgat_forward(ents, ent_mask, q_encoding, adj, types, init_mem, w_qin, b_qin, w_qt, b_qt, w_pl, b_pl, w_pc, b_pc, w_q, b_q, w_k, b_k, w_v, b_v, w_pk, b_pk, w_pv, b_pv, wes, w_mu, b_mu, w_cb, b_cb):
            d = ents.shape[-1]
            x_loc = ents
            x_ctx = jnp.broadcast_to(init_mem, ents.shape)
            var_drop = ent_mask[:, :, None]
            adj_pos = adj > 0
            q_base = jax.nn.elu(_lin(q_encoding, w_qin, b_qin))
            n_types = wes.shape[0] + 1
            for t in range(T_ITER):
                cmd = _lin(q_base, w_qt[t], b_qt[t])
                xc = x_ctx * var_drop
                pl = _lin(x_loc, w_pl, b_pl)
                pc = _lin(xc, w_pc, b_pc)
                x_joint = jnp.concatenate([x_loc, xc, pl * pc], axis=-1)
                q = _lin(x_joint, w_q, b_q)
                k = _lin(x_joint, w_k, b_k) * _lin(cmd, w_pk, b_pk)[:, None, :]
                v = _lin(x_joint, w_v, b_v) * _lin(cmd, w_pv, b_pv)[:, None, :]
                edge_score = jnp.zeros(adj.shape, jnp.float32)
                for i in range(n_types):
                    if types >> i & 1 == 1:
                        w1, w2 = (wes[i - 1, :d], wes[i - 1, d:])
                        s = (q @ w1)[:, :, None] + (k @ w2)[:, None, :]
                        edge_score = edge_score + jnp.where(adj == i, s, 0.0)
                e = jnp.where(edge_score > 0, edge_score, ALPHA * edge_score)
                logits = jnp.where(adj_pos, e, jnp.float32(-9000000000000000.0))
                prob = jax.nn.softmax(logits, axis=-1)
                message = jnp.einsum('bij,bjd->bid', prob, v)
                x_ctx = _lin(jnp.concatenate([xc, message], axis=-1), w_mu, b_mu)
            return _lin(jnp.concatenate([x_loc, x_ctx], axis=-1), w_cb, b_cb)
        return _qdgat_forward(ents, ent_mask, q_encoding, adj, types, init_mem, w_qin, b_qin, w_qt, b_qt, w_pl, b_pl, w_pc, b_pc, w_q, b_q, w_k, b_k, w_v, b_v, w_pk, b_pk, w_pv, b_pv, wes, w_mu, b_mu, w_cb, b_cb)

    def _L1_cond_ref(x, t_emb, W_in, W_conv, b_conv, ln_g, ln_b, W_xproj, W_dt, b_dt, A_log, D, W_out):
        import jax, jax.numpy as jnp
        import numpy as np
        B, S, D_MODEL, D_INNER, D_STATE = (4, 512, 128, 256, 16)
        d_inner = W_conv.shape[0]
        d_state = A_log.shape[0]
        xr, gate = jnp.split(x @ W_in.T, 2, axis=-1)
        xr = xr + t_emb[:, None, :]
        xc = jax.lax.conv_general_dilated(xr.transpose(0, 2, 1), W_conv, (1,), [(3, 0)], feature_group_count=d_inner, dimension_numbers=('NCH', 'OIH', 'NCH')) + b_conv[None, :, None]
        xc = jax.nn.silu(xc).transpose(0, 2, 1)
        mu = xc.mean(-1, keepdims=True)
        var = xc.var(-1, keepdims=True)
        xn = (xc - mu) / jnp.sqrt(var + 1e-05) * ln_g + ln_b
        Bm, Cm, dt = jnp.split(xn @ W_xproj.T, 3, axis=-1)
        dt = jnp.tanh(dt @ W_dt.T + b_dt) * 0.01
        A = -jnp.tanh(A_log)
        Ad = 1.0 + dt * A
        Bd = Bm * jnp.minimum(jnp.linalg.norm(xn, axis=-1, keepdims=True), 1.0)
        h0 = jnp.zeros((xn.shape[0], d_state, d_inner), xn.dtype)

        def step(h, inputs):
            ad, bd, xt, ct = inputs
            h = jnp.clip(h * ad[:, :, None] + bd[:, :, None] * xt[:, None, :], -10.0, 10.0)
            yt = jnp.einsum('bd,bdh->bh', ct, h)
            return (h, yt)
        _, ys = jax.lax.scan(step, h0, (Ad.transpose(1, 0, 2), Bd.transpose(1, 0, 2), xn.transpose(1, 0, 2), Cm.transpose(1, 0, 2)))
        y = ys.transpose(1, 0, 2) + D * xn
        return y * jax.nn.silu(gate) @ W_out.T
    x = x + _L0_cond_ref(x, mask_BxS_ff1, fside_BxS_0, itok_BxSxS_0_4, 30, L0_cond_init_mem, L0_cond_w_qin, L0_cond_b_qin, fside_BxSxS_0, mask_BxS_ff0, L0_cond_w_pl, L0_cond_b_pl, L0_cond_w_pc, L0_cond_b_pc, L0_cond_w_q, L0_cond_b_q, L0_cond_w_k, L0_cond_b_k, L0_cond_w_v, L0_cond_b_v, L0_cond_w_pk, L0_cond_b_pk, L0_cond_w_pv, L0_cond_b_pv, cond_2048, L0_cond_w_mu, L0_cond_b_mu, L0_cond_w_cb, L0_cond_b_cb)
    x = x + _L1_cond_ref(x, cond_2048, L1_cond_W_in, L1_cond_W_conv, L1_cond_b_conv, L1_cond_ln_g, L1_cond_ln_b, L1_cond_W_xproj, L1_cond_W_dt, L1_cond_b_dt, L1_cond_A_log, L1_cond_D, L1_cond_W_out)
    return x

_drawn_inputs = setup_inputs


def setup_inputs(seed=0):
    import zlib

    import numpy as np

    out = dict(_drawn_inputs(seed))
    spreads = {'L0_cond_b_qin': (0.0, 0.558),
     'L0_cond_b_pl': (0.0, 0.639),
     'L0_cond_b_pc': (0.0, 0.8),
     'L0_cond_b_q': (0.0, 0.8),
     'L0_cond_b_k': (0.0, 0.8),
     'L0_cond_b_v': (0.0, 0.317),
     'L0_cond_b_pk': (0.0, 0.8),
     'L0_cond_b_pv': (0.0, 0.1),
     'L0_cond_b_mu': (0.0, 0.1),
     'L0_cond_b_cb': (0.0, 0.8),
     'L1_cond_b_conv': (0.0, 0.369),
     'L1_cond_ln_g': (1.0, 0.2),
     'L1_cond_ln_b': (0.0, 0.1),
     'L1_cond_D': (0.10000000149011612, 0.6)}
    factors = {'L0_cond_w_pl': 4.236,
     'L0_cond_w_pc': 3.085,
     'L0_cond_w_q': 8.0,
     'L0_cond_w_k': 8.0,
     'L0_cond_w_pk': 8.0,
     'L1_cond_W_dt': 64.0,
     'L1_cond_b_dt': 39.323,
     'L1_cond_A_log': 21.73}
    for name, (base, spread) in spreads.items():
        noise = np.random.default_rng([zlib.crc32(name.encode()), seed]).standard_normal(out[name].shape)
        drawn = base * np.exp(spread * noise) if base else spread * noise
        out[name] = jnp.asarray(drawn.astype(out[name].dtype))
    for name, factor in factors.items():
        out[name] = (out[name] * factor).astype(out[name].dtype)
    return out
```

```python
from contextlib import ExitStack

import concourse.bass as bass
from concourse import mybir

F32 = mybir.dt.float32
BF16 = mybir.dt.bfloat16
I32 = mybir.dt.int32
U8 = mybir.dt.uint8
U16 = mybir.dt.uint16
ALU = mybir.AluOpType
ACT = mybir.ActivationFunctionType
AX = mybir.AxisListType

P = 128
B, S, D = 16, 128, 128
TOK = B * S
T_ITER, TYPES = 4, 4
NG, GB = 4, 4
GT = GB * S
OC = 2
DI = OC * P
NST = 16
HB = B // 2
TB = 8
NBLK = S // TB
XCH = 4
TAPS = 4
PARTS = 3
MASKED = -9000000000000000.0
ALPHA = 0.2

COLS = [("ident", P), ("wqin", D), ("wqt", T_ITER * D), ("wpl", D), ("wpc", D), ("wq", 3 * D),
        ("wk", 3 * D), ("wv", 3 * D), ("wpk", D), ("wpv", D), ("wmu", 2 * D), ("wcb", 2 * D),
        ("win", 2 * DI), ("wxp", OC * 32), ("wout", OC * D), ("cond", OC * B), ("qenc", B),
        ("bqin", 1), ("bqt", T_ITER), ("bpl", 1), ("bpc", 1), ("bq", 1), ("bk", 1), ("bv", 1),
        ("bpk", 1), ("bpv", 1), ("bmu", 1), ("bcb", 1), ("init", 1), ("conv", OC * TAPS),
        ("bconv", OC), ("lng", OC), ("lnb", OC), ("dskip", OC), ("bdt", 1), ("alog", 1),
        ("nm12", 1), ("nm3", 1), ("half8", HB)]
COLS16 = [("wxdt", DI), ("wdt", NST)]
ROWS_OF = GB * TYPES


def places(cols):
    at, out = 0, {}
    for name, n in cols:
        out[name] = (at, at + n)
        at += n
    return out, at


AT, WIDE = places(COLS)
AT16, WIDE16 = places(COLS16)


def build_program(nc, xT, adj, w128, w16, mask, rows, sel, spread, out):
    with ExitStack() as ctx:
        def sb(name, shape, dt=F32):
            return ctx.enter_context(nc.sbuf_tensor(name, shape, dt))

        def sem(name):
            return ctx.enter_context(nc.semaphore(name))

        bank = [ctx.enter_context(nc.psum_tensor(f"bank{i}", [P, 512], F32)) for i in range(8)]

        W = sb("W", [P, WIDE])
        W16 = sb("W16", [NST, WIDE16])
        XT = sb("XT", [P, B, S])
        arena = sb("arena", [P, 16384])
        XC = arena[:, 0:2048].rearrange("p (b t) -> p b t", b=B)
        PL = arena[:, 2048:4096].rearrange("p (b t) -> p b t", b=B)
        VL = arena[:, 4096:6144].rearrange("p (b d) -> p b d", b=B)
        BASE = arena[:, 6144:8192]
        MB = arena[:, 8192:10240].rearrange("p (b t) -> p b t", b=B)
        MK = arena[:, 10240:12288].bitcast(U8).rearrange("p (k n) -> p k n", k=TYPES)
        ADJ = arena[:, 12288:14336].bitcast(I32)
        XR = arena[:, :].bitcast(BF16).rearrange("p (t c) -> p t c", c=DI)

        spread_sb = sb("spread_sb", [PARTS * B, 2, P], BF16)
        rows_sb = sb("rows_sb", [P, 2, DI])

        qb = sb("qb", [P, B])
        qneg = sb("qneg", [P, B])
        qexp = sb("qexp", [P, B])
        cmd = sb("cmd", [P, T_ITER, B])
        pk = sb("pk", [P, T_ITER, B])
        pv = sb("pv", [P, T_ITER, B])
        gk = sb("gk", [P, T_ITER, B, TYPES])
        grep = sb("grep", [P, P])
        aq = sb("aq", [P, 3, TYPES])
        cb = sb("cb", [P, T_ITER * NG])

        work = sb("work", [P, 6656])
        PP, vrow, rrow, ES, E, Pr, PTs, MS = [work[:, i * GT:(i + 1) * GT] for i in range(8)]
        Vs = work[:, 4096:5120].rearrange("p (q b d) -> p q b d", q=2, b=GB)
        arep = work[:, 5120:6656].rearrange("p (c g n) -> p c g n", c=3, g=NG)
        XP = work[:, 0:6144].bitcast(BF16).rearrange("p (q b c) -> p q b c", q=PARTS, b=B)
        p1 = sb("p1", [P, GT], BF16)
        p2 = sb("p2", [P, GT], BF16)
        Y = sb("Y", [P, GT], BF16)
        nmax = sb("nmax", [P, GB])
        sums = sb("sums", [P, GB])
        rsum = sb("rsum", [P, GB])

        X1 = sb("X1", [P, B, S])
        GATE = sb("GATE", [P, OC, B, S])
        XNT = sb("XNT", [P, OC, B, S])
        PAD = TAPS - 1
        xpad = sb("xpad", [P, OC, GB, PAD + S])
        st = sb("st", [P, GB, 6])
        mv = sb("mv", [P, GB, 2])
        sd = sb("sd", [P, GB])
        rstd = sb("rstd", [P, GB])
        ssq = sb("ssq", [P, GB])
        nrm = sb("nrm", [P, GB])
        nf = sb("nf", [P, GB])
        wx = sb("wx", [P, OC, 48])
        eps = sb("eps", [P, 1])
        ABC = sb("ABC", [P, 2, 3, S])
        work2 = sb("work2", [P, 6144])
        ak = work2[:, 0:768].rearrange("p (c t n) -> p c t n", c=3, t=T_ITER)
        sel_sb = work2[:, 1024:3072].bitcast(BF16).rearrange("p (q a b) -> p q a b", q=2, a=ROWS_OF)
        cv = work2[:, 0:1024].rearrange("p (c n) -> p c n", c=OC)
        XS = work2[:, 1024:2048].rearrange("p (c n) -> p c n", c=OC)
        N0 = work2[:, 2048:3072].rearrange("p (b c) -> p b c", b=GB)
        XN = work2[:, 3072:4096].rearrange("p (b c) -> p b c", b=GB)
        PR = work2[0:48, 4096:6144]
        Dt = work2[:, 0:2048].rearrange("p (q h c) -> p q h c", q=4, h=2)
        H = work2[:, 2048:4096].rearrange("p (q h c) -> p q h c", q=4, h=2)
        U = work2[:, 4096:4608].rearrange("p (h c) -> p h c", h=2)
        YS = work2[:, 4608:5120].rearrange("p (h c) -> p h c", h=2)
        z = work2[:, 5120:5120 + OC * TB * B].rearrange("p (c t b) -> p c t b", c=OC, t=TB)
        cmat = sb("cmat", [P, 2, 2, TB * (TB + 1) * HB])
        nA = sb("nA", [P, 1])

        def w(name, a=0, b=None):
            lo, hi = AT[name]
            return W[:, lo + a:(lo + b if b is not None else hi)]

        scrx = nc.dram_tensor("rows_scratch", (PARTS * B, S, DI), BF16, kind="Internal").ap()
        scr = nc.dram_tensor("proj_scratch", (48, TOK), F32, kind="Internal").ap()

        names = ("ld0 ld1 ld2 ld3 ld4 ld5 s_qb s_qn s_qe s_qd s_qbase s_cmd s_cmde s_pk s_pke s_gk s_ak s_ake s_aq "
                 "s_grep s_cb s_cbe s_ar s_zero s_pl s_ple s_vl s_vle s_mask s_xc0 "
                 "s_pc s_pp s_row s_v s_p1 s_r s_p2 s_y s_V s_Ve s_S s_es s_pred s_leak s_max s_exp s_rcp "
                 "s_sc s_pt s_ptc s_ms s_mse s_cx s_xc "
                 "s_cbo s_x1 s_in s_xr s_gate s_conv s_xs s_tr s_st s_mv s_sd s_rs s_n0 s_xg s_xn s_sq s_nr s_nf "
                 "s_q1 s_rr s_q2 s_q3 s_tb s_xnt s_pj s_pje s_wx s_wxe s_eps "
                 "s_scr s_xg4 s_abc s_th s_nA s_nAm s_a s_xrow s_X s_D s_U s_H s_yt s_yb s_Z s_z0 s_ys s_yT s_zz s_zg s_o s_oe s_out passed_dve passed_pe passed_pool").split()
        s = {n: sem(n) for n in names}

        block = ctx.enter_context(nc.Block())
        GC = [slice(g * GT, (g + 1) * GT) for g in range(NG)]

        def grp(t3, g):
            return t3[:, g * GB:(g + 1) * GB, :].rearrange("p b t -> p (b t)")

        def passed(eng, signal):
            eng.sem_inc(s[signal], 1)

        @block.sync
        def _(sp):
            sp.dma_start(W[:], w128).then_inc(s["ld0"], 16)
            sp.dma_start(XT[:].rearrange("p b t -> p (b t)"), xT).then_inc(s["ld1"], 16)
            sp.dma_start(ADJ, adj).then_inc(s["ld2"], 16)
            sp.dma_start(MB.rearrange("p b t -> p (b t)"), mask.broadcast_to((P, TOK))).then_inc(s["ld3"], 16)
            sp.dma_start(sel_sb.rearrange("p q a b -> p (q a b)").bitcast(U16), sel).then_inc(s["ld4"], 16)
            sp.dma_start(spread_sb[:].rearrange("p a b -> p (a b)").bitcast(U16), spread).then_inc(s["ld5"], 16)
            sp.dma_start(W16[:], w16).then_inc(s["ld5"], 16)
            sp.dma_start(rows_sb[:].rearrange("p a b -> p (a b)"), rows.broadcast_to((P, 2 * DI))).then_inc(s["ld5"], 16)
            for g in range(NG):
                sp.wait_ge(s["s_q3"], g + 1)
                for q in range(PARTS):
                    r0 = q * B + g * GB
                    sp.dma_start(scrx[r0:r0 + GB, :, :].rearrange("r t c -> t r c"),
                                 XP[:, q, g * GB:(g + 1) * GB, :]).then_inc(s["s_xg4"], 16)
            sp.wait_ge(s["s_pje"], NG)
            sp.dma_start(scr, PR[:]).then_inc(s["s_scr"], 16)
            sp.wait_ge(s["s_scr"], 16)
            for k in range(3):
                for h in range(2):
                    src = scr[k * NST:(k + 1) * NST, h * HB * S:(h + 1) * HB * S].rearrange("s (b t) -> b s t", b=HB)
                    for b in range(HB):
                        sp.dma_start(ABC[b * NST:(b + 1) * NST, h, k, :], src[b]).then_inc(s["s_abc"], 16)
            sp.wait_ge(s["s_cbo"], NG)
            sp.wait_ge(s["s_xg4"], 16 * NG * PARTS)
            for c in range(XCH):
                tc = slice(c * S // XCH, (c + 1) * S // XCH)
                sp.dma_start(XR[0:PARTS * B, tc, :], scrx[:, tc, :]).then_inc(s["s_xrow"], 16)
            sp.wait_ge(s["s_oe"], NBLK)
            sp.dma_start(out, X1[:].rearrange("p b t -> p (b t)")).then_inc(s["s_out"], 16)
            sp.wait_ge(s["s_out"], 16)


        @block.tensor
        def _(pe):
            def mm(o, a, b, start=True, stop=True):
                return nc.tensor.matmul(o, a, b, start=start, stop=stop)

            ident = w("ident")
            pe.wait_ge(s["ld0"], 16)
            mm(bank[0][:, 0:B], w("wqin"), w("qenc")).then_inc(s["s_qb"], 1)
            pe.wait_ge(s["s_qbase"], 1)
            for t in range(T_ITER):
                x = mm(bank[1][:, t * B:(t + 1) * B], w("wqt", t * D, (t + 1) * D), qb[:])
            x.then_inc(s["s_cmd"], 1)
            pe.wait_ge(s["ld1"], 16)
            for g in range(NG):
                mm(bank[3 + g][:], w("wpl"), grp(XT, g)).then_inc(s["s_pl"], 1)
            pe.wait_ge(s["s_cmde"], 1)
            cf = cmd[:].rearrange("p t b -> p (t b)")
            mm(bank[0][:, 0:64], w("wpk"), cf)
            mm(bank[0][:, 64:128], w("wpv"), cf).then_inc(s["s_pk"], 1)
            for c in range(3):
                x = mm(bank[2][:, c * TYPES:(c + 1) * TYPES], w("wq", c * D, (c + 1) * D), w("cond", 0, TYPES))
            x.then_inc(s["s_aq"], 1)
            for g in range(NG):
                pe.wait_ge(s["s_ple"], g + 1)
                for b in range(GB):
                    x = mm(bank[3 + g][:, b * D:(b + 1) * D], XT[:, g * GB + b, :], w("wv", 0, D))
                x.then_inc(s["s_vl"], 1)
            pe.wait_ge(s["s_gk"], 1)
            gkf = gk[:].rearrange("p t b k -> p (t b k)")
            for c in range(3):
                if c == 2:
                    pe.wait_ge(s["s_pke"], 2)
                mm(bank[[1, 7, 0][c]][:, 0:256], w("wk", c * D, (c + 1) * D), gkf).then_inc(s["s_ak"], 1)
            pe.wait_ge(s["s_aq"], 2)
            for n in range(T_ITER * NG):
                pe.wait_ge(s["s_grep"], n + 1)
                x = mm(bank[2][:, 16 + 2 * n:18 + 2 * n], grep[:], W[:, AT["bq"][0]:AT["bk"][1]])
                x.then_inc(s["s_cb"], 1)
            pe.wait_ge(s["s_cbe"], 2)
            pe.wait_ge(s["ld4"], 16)
            for g in range(NG):
                pe.wait_ge(s["s_vle"], g + 1)
            pe.wait_ge(s["s_ake"], 3)
            pe.wait_ge(s["s_xc0"], 1)

            def pc(n, g):
                mm(bank[0][:], w("wpc"), grp(XC, g)).then_inc(s["s_pc"], 1)

            def slot(n, g, first, last, more):
                pg = (g - 1) % NG
                if more:
                    pe.wait_ge(s["s_pp"], n + 1)
                    pe.wait_ge(s["s_ar"], n + 1)
                    mm(bank[1][:], arep[:, 0, g, :], grp(XT, g), True, False)
                    mm(bank[1][:], arep[:, 1, g, :], grp(XC, g), False, False)
                    mm(bank[1][:], arep[:, 2, g, :], PP[:], False, True).then_inc(s["s_row"], 1)
                if not first:
                    pe.wait_ge(s["s_sc"], n)
                    if not (isinstance(n, int) and n == 1):
                        pe.wait_ge(s["s_xc"], n - 1)
                    for b in range(GB):
                        x = nc.tensor.transpose(bank[7][:, b * S:(b + 1) * S], Pr[:, b * S:(b + 1) * S], ident)
                    x.then_inc(s["s_pt"], 1)
                if more:
                    pe.wait_ge(s["s_Ve"], n)
                    for b in range(GB):
                        o = bank[2][:, b * D:(b + 1) * D]
                        mm(o, XC[:, g * GB + b, :], w("wv", D, 2 * D), True, False)
                        x = mm(o, PP[:, b * S:(b + 1) * S], w("wv", 2 * D, 3 * D), False, True)
                    x.then_inc(s["s_V"], 1)
                if not first:
                    pe.wait_ge(s["s_ptc"], n)
                    pe.wait_ge(s["s_Ve"], n)
                    for b in range(GB):
                        x = mm(bank[0][:, b * S:(b + 1) * S], Vs[:, pg % 2, b, :], PTs[:, b * S:(b + 1) * S])
                    x.then_inc(s["s_ms"], 1)
                if more:
                    pe.wait_ge(s["s_y"], n + 1)
                    for k in range(TYPES):
                        pe.wait_ge(s["s_pred"], n * TYPES)
                        for b in range(GB):
                            o = bank[3 + k][:, b * S:(b + 1) * S]
                            row = b * TYPES + k
                            mm(o, Y[:, b * S:(b + 1) * S], sel_sb[:, 0, row, :], True, False)
                            x = mm(o, sel_sb[:, 1, row, :], Y[:, b * S:(b + 1) * S], False, True)
                        x.then_inc(s["s_S"], 1)
                    if not last:
                        if not first:
                            pe.wait_ge(s["s_mse"], n)
                        if not (isinstance(n, int) and n < 3):
                            pe.wait_ge(s["s_xc"], n - 2)
                        pc(n + 1, (g + 1) % NG)
                if not first:
                    pe.wait_ge(s["s_mse"], n)
                    mm(bank[7][:], w("wmu", 0, D), grp(XC, pg), True, False)
                    mm(bank[7][:], w("wmu", D, 2 * D), MS[:], False, True).then_inc(s["s_cx"], 1)

            pc(0, 0)
            for g in range(NG):
                slot(g, g, g == 0, False, True)
            with pe.Fori(1, T_ITER - 1) as t:
                for g in range(NG):
                    slot(t * NG + g, g, False, False, True)
            for g in range(NG):
                slot((T_ITER - 1) * NG + g, g, False, g == NG - 1, True)
            slot(T_ITER * NG, 0, False, True, False)

            pe.wait_ge(s["ld5"], 48)
            pe.wait_ge(s["s_xc"], T_ITER * NG)
            for c in range(OC):
                x = mm(bank[6][:, c * NST:(c + 1) * NST], W16[:, c * P:(c + 1) * P], W16[:, AT16["wdt"][0]:AT16["wdt"][1]])
            x.then_inc(s["s_wx"], 1)

            def front_a(g):
                if g:
                    pe.wait_ge(s["s_x1"], g)
                mm(bank[7][:], w("wcb", 0, D), grp(XT, g), True, False)
                mm(bank[7][:], w("wcb", D, 2 * D), grp(XC, g), False, True).then_inc(s["s_cbo"], 1)
                pe.wait_ge(s["s_x1"], g + 1)
                for c in range(4):
                    if g:
                        pe.wait_ge(s["s_xr"] if c < 2 else s["s_gate"], 2 * g)
                    mm(bank[c][:], w("win", c * P, (c + 1) * P), grp(X1, g)).then_inc(s["s_in"], 1)

            def front_b(g):
                pe.wait_ge(s["s_xs"], 2 * (g + 1))
                if g:
                    pe.wait_ge(s["s_n0"], g)
                    pe.wait_ge(s["s_pje"], g)
                for b in range(GB):
                    for c in range(OC):
                        at = (b * OC + c) * P
                        x = nc.tensor.transpose(bank[4 + at // 512][:, at % 512:at % 512 + P],
                                                XS[:, c, b * S:(b + 1) * S], ident)
                x.then_inc(s["s_tr"], 1)

            def front_c(g):
                pe.wait_ge(s["s_n0"], g + 1)
                for c in range(OC):
                    for b in range(GB):
                        x = nc.tensor.transpose(bank[4 + c][:, b * S:(b + 1) * S], N0[:, b, c * P:(c + 1) * P], ident)
                    x.then_inc(s["s_tb"], 1)
                pe.wait_ge(s["s_xnt"], 2 * (g + 1))
                pe.wait_ge(s["s_wxe"], 2)
                if g:
                    pe.wait_ge(s["s_pje"], g)
                for c in range(OC):
                    x = mm(bank[6][0:48, :], wx[:, c, :], grp(XNT[:, c], g), c == 0, c == OC - 1)
                x.then_inc(s["s_pj"], 1)

            front_a(0)
            for g in range(NG):
                front_b(g)
                if g + 1 < NG:
                    front_a(g + 1)
                front_c(g)

            pe.wait_ge(s["s_pje"], NG)

            def spread_x(t, slot_):
                for h in range(2):
                    x = mm(bank[slot_][:, h * DI:(h + 1) * DI], spread_sb[:, h, :],
                           XR[0:PARTS * B, bass.ds(t, 1), :].rearrange("p a c -> p (a c)"))
                x.then_inc(s["s_X"], 1)

            def blk(nb, j, tail, warm):
                t0 = nb * TB
                for k in range(2):
                    if not warm:
                        pe.wait_ge(s["s_D"], 2 * (t0 + k) - 2)
                    spread_x(t0 + k, k)
                pe.wait_ge(s["s_Z"], 2 * (nb + 1))
                for k in range(TB):
                    t = t0 + k
                    pe.wait_ge(s["s_H"], t + 1)
                    for h in range(2):
                        x = mm(bank[2 + 2 * j + h][0:TB * HB, 0:DI], cmat[:, h, j, k * TB * HB:(k + 1) * TB * HB], H[:, k % 4, h, :], k == 0, k == TB - 1)
                    x.then_inc(s["s_yt"], 1)
                    if k + 2 < TB:
                        pe.wait_ge(s["s_D"], 2 * (t + 1))
                        spread_x(t + 2, k % 2)
                    if tail and k == 3:
                        tail_a(nb - 1)
                    if tail and k == 6:
                        tail_b(nb - 1)

            def tail_a(nb):
                pe.wait_ge(s["s_ys"], 2 * (nb + 1))
                if not (isinstance(nb, int) and nb == 0):
                    pe.wait_ge(s["s_zz"], nb)
                passed(pe, "passed_pe")
                for c in range(OC):
                    for h in range(2):
                        o = bank[6][:, c * TB * B:(c + 1) * TB * B].rearrange("p (t b) -> p t b", b=B)[:, :, h * HB:(h + 1) * HB]
                        x = nc.tensor.transpose(o, YS[0:TB * HB, h, c * P:(c + 1) * P], ident[0:TB * HB, 0:TB * HB])
                x.then_inc(s["s_yT"], 1)

            def tail_b(nb):
                pe.wait_ge(s["s_zg"], nb + 1)
                if not (isinstance(nb, int) and nb == 0):
                    pe.wait_ge(s["s_oe"], nb)
                for c in range(OC):
                    x = mm(bank[7][:, 0:TB * B], w("wout", c * D, (c + 1) * D), z[:, c].rearrange("p t b -> p (t b)"),
                           c == 0, c == OC - 1)
                x.then_inc(s["s_o"], 1)

            pe.wait_ge(s["s_xrow"], 16 * XCH)
            blk(0, 0, False, True)
            blk(1, 1, True, False)
            with pe.Fori(1, NBLK // 2) as it:
                blk(it * 2, 0, True, False)
                blk(it * 2 + 1, 1, True, False)
            tail_a(NBLK - 1)
            tail_b(NBLK - 1)

        @block.vector
        def _(v):
            def tt(o, a, b, op):
                return nc.vector.tensor_tensor(o, a, b, op)

            def stt(o, a, sc, b, op0, op1):
                return nc.vector.scalar_tensor_tensor(out=o, in0=a, scalar=sc, in1=b, op0=op0, op1=op1)

            nc.vector.memset(grep[:], 0.0).then_inc(s["s_zero"], 1)
            nc.vector.memset(arep[:], 0.0).then_inc(s["s_zero"], 1)
            nc.vector.memset(eps[:], 1e-5).then_inc(s["s_eps"], 1)
            nc.vector.memset(xpad[:], 0.0).then_inc(s["s_zero"], 1)
            nc.vector.memset(cmat[:], 0.0).then_inc(s["s_z0"], 1)
            v.wait_ge(s["ld0"], 16)
            v.wait_ge(s["s_qb"], 1)
            nc.vector.tensor_scalar(qb[:], bank[0][:, 0:B], w("bqin"), 0.0, ALU.add, ALU.max).then_inc(s["s_qd"], 1)
            nc.vector.tensor_scalar(qneg[:], bank[0][:, 0:B], w("bqin"), 0.0, ALU.add, ALU.min).then_inc(s["s_qn"], 1)
            v.wait_ge(s["s_qe"], 1)
            v.wait_ge(s["s_qd"], 1)
            stt(qb[:], qexp[:], -1.0, qb[:], ALU.add, ALU.add).then_inc(s["s_qbase"], 1)
            v.wait_ge(s["s_cmd"], 1)
            for t in range(T_ITER):
                x = nc.vector.tensor_scalar(cmd[:, t, :], bank[1][:, t * B:(t + 1) * B], w("bqt", t, t + 1), None, ALU.add)
            x.then_inc(s["s_cmde"], 1)
            for g in range(NG):
                v.wait_ge(s["s_pl"], g + 1)
                nc.vector.tensor_scalar(grp(PL, g), bank[3 + g][:], w("bpl"), None, ALU.add).then_inc(s["s_ple"], 1)
            v.wait_ge(s["s_pk"], 1)
            nc.vector.tensor_scalar(pk[:].rearrange("p t b -> p (t b)"), bank[0][:, 0:64], w("bpk"), None, ALU.add).then_inc(s["s_pke"], 1)
            nc.vector.tensor_scalar(pv[:].rearrange("p t b -> p (t b)"), bank[0][:, 64:128], w("bpv"), None, ALU.add).then_inc(s["s_pke"], 1)
            v.wait_ge(s["s_pke"], 2)
            w2 = w("cond", B, B + TYPES)
            tt(gk[:].rearrange("p t b k -> p (t b) k"),
               pk[:].rearrange("p t (b o) -> p (t b) o", o=1).broadcast_to((P, T_ITER * B, TYPES)),
               w2.rearrange("p (o k) -> p o k", o=1).broadcast_to((P, T_ITER * B, TYPES)), ALU.mult).then_inc(s["s_gk"], 1)
            v.wait_ge(s["s_aq"], 1)
            nc.vector.tensor_copy(aq[:].rearrange("p c k -> p (c k)"), bank[2][:, 0:12]).then_inc(s["s_aq"], 1)
            for g in range(NG):
                v.wait_ge(s["s_vl"], g + 1)
                nc.vector.tensor_copy(VL[:, g * GB:(g + 1) * GB, :].rearrange("p b d -> p (b d)"), bank[3 + g][:]).then_inc(s["s_vle"], 1)
            for c in range(3):
                v.wait_ge(s["s_ak"], c + 1)
                nc.vector.tensor_copy(ak[:, c].rearrange("p t n -> p (t n)"), bank[[1, 7, 0][c]][:, 0:256]).then_inc(s["s_ake"], 1)
            v.wait_ge(s["ld2"], 16)
            for k in range(TYPES):
                nc.vector.tensor_scalar(MK[:, k, :], ADJ, float(k + 1), None, ALU.is_equal).then_inc(s["s_mask"], 1)
            nc.vector.tensor_scalar(BASE, ADJ, 0.0, MASKED / ALPHA, ALU.is_le, ALU.mult).then_inc(s["s_mask"], 1)
            v.wait_ge(s["ld3"], 16)
            nc.vector.tensor_scalar(XC.rearrange("p b t -> p (b t)"), MB.rearrange("p b t -> p (b t)"), w("init"), None,
                                    ALU.mult).then_inc(s["s_xc0"], 1)
            v.wait_ge(s["s_cb"], T_ITER * NG)
            cbp = bank[2][:, 16:16 + 2 * T_ITER * NG].rearrange("p (n k) -> p n k", k=2)
            nc.vector.tensor_copy(cb[0:64, :], cbp[0:64, :, 0]).then_inc(s["s_cbe"], 1)
            nc.vector.tensor_copy(cb[64:128, :], cbp[64:128, :, 1]).then_inc(s["s_cbe"], 1)
            v.wait_ge(s["s_mask"], TYPES + 1)
            v.wait_ge(s["s_vle"], NG)
            v.wait_ge(s["s_ple"], NG)

            def pp(n, g):
                v.wait_ge(s["s_pc"], n + 1)
                stt(PP[:], bank[0][:], w("bpc"), grp(PL, g), ALU.add, ALU.mult).then_inc(s["s_pp"], 1)

            def slot(n, t, g, first, last, more, final):
                pg = (g - 1) % NG
                if more:
                    v.wait_ge(s["s_v"], n + 1)
                    v.wait_ge(s["s_p1"], n + 1)
                    stt(rrow[:], p1[:], w("nm12"), vrow[:], ALU.mult, ALU.add).then_inc(s["s_r"], 1)
                    v.wait_ge(s["s_p2"], n + 1)
                    v.wait_ge(s["s_r"], n + 1)
                    v.wait_ge(s["s_S"], n * TYPES)
                    stt(Y[:], p2[:], w("nm3"), rrow[:], ALU.mult, ALU.add).then_inc(s["s_y"], 1)
                    v.wait_ge(s["s_V"], n + 1)
                    tt(Vs[:, g % 2].rearrange("p b d -> p (b d)"), bank[2][:],
                       VL[:, g * GB:(g + 1) * GB, :].rearrange("p b d -> p (b d)"), ALU.add).then_inc(s["s_Ve"], 1)
                if not first:
                    v.wait_ge(s["s_ms"], n)
                    pt = (t if g else t - 1)
                    stt(MS[:].rearrange("p (b t) -> p b t", b=GB), bank[0][:].rearrange("p (b t) -> p b t", b=GB), w("bv"),
                        pv[:, bass.ds(pt, 1), pg * GB:(pg + 1) * GB].rearrange("p o b -> p b o").broadcast_to((P, GB, S)),
                        ALU.add, ALU.mult).then_inc(s["s_mse"], 1)
                if more:
                    for k in range(TYPES):
                        if k == 0:
                            v.wait_ge(s["s_es"], n + 1)
                        v.wait_ge(s["s_S"], n * TYPES + k + 1)
                        v.wait_ge(s["s_pred"], n * TYPES + k)
                        passed(v, "passed_dve")
                        nc.vector.copy_predicated(ES[:], MK[:, k, GC[g]], bank[3 + k][:]).then_inc(s["s_pred"], 1)
                    v.wait_ge(s["s_pred"], n * TYPES + TYPES)
                    stt(E[:], ES[:], ALPHA, ES[:], ALU.mult, ALU.max).then_inc(s["s_leak"], 1)
                    v.wait_ge(s["s_leak"], n + 1)
                    nc.vector.tensor_reduce(nmax[:], E[:].rearrange("p (b t) -> p b t", b=GB), AX.X, ALU.max,
                                            negate=True).then_inc(s["s_max"], 1)
                    if not last:
                        pp(n + 1, (g + 1) % NG)
                if not first:
                    v.wait_ge(s["s_cx"], n)
                    if final:
                        nc.vector.tensor_scalar(grp(XC, pg), bank[7][:], w("bmu"), None, ALU.add).then_inc(s["s_xc"], 1)
                    else:
                        stt(grp(XC, pg), bank[7][:], w("bmu"), grp(MB, pg), ALU.add, ALU.mult).then_inc(s["s_xc"], 1)
                if more:
                    v.wait_ge(s["s_exp"], (n + 1) * GB)
                    v.wait_ge(s["s_sc"], n)
                    nc.vector.reciprocal(rsum[:], sums[:]).then_inc(s["s_rcp"], 1)

            pp(0, 0)
            for g in range(NG):
                slot(g, 0, g, g == 0, False, True, False)
            with v.Fori(1, T_ITER - 1) as t:
                for g in range(NG):
                    slot(t * NG + g, t, g, False, False, True, False)
            t = T_ITER - 1
            for g in range(NG):
                slot(t * NG + g, t, g, False, g == NG - 1, True, g > 0)
            slot(T_ITER * NG, T_ITER, 0, False, True, False, True)

            v.wait_ge(s["s_wx"], 1)
            nc.vector.tensor_copy(wx[:, :, 0:32], w("wxp").rearrange("p (c n) -> p c n", c=OC)).then_inc(s["s_wxe"], 1)
            nc.vector.tensor_copy(wx[:, :, 32:48], bank[6][:, 0:2 * NST].rearrange("p (c n) -> p c n", c=OC)).then_inc(s["s_wxe"], 1)

            v.wait_ge(s["s_zero"], 3)

            def front_a(g):
                v.wait_ge(s["s_cbo"], g + 1)
                stt(grp(X1, g), bank[7][:], w("bcb"), grp(XT, g), ALU.add, ALU.add).then_inc(s["s_x1"], 1)
                for c in range(OC):
                    v.wait_ge(s["s_in"], 4 * g + c + 1)
                    tt(xpad[:, c, :, PAD:], bank[c][:].rearrange("p (b t) -> p b t", b=GB),
                       w("cond", c * B + g * GB, c * B + (g + 1) * GB).rearrange("p (b o) -> p b o", o=1).broadcast_to((P, GB, S)),
                       ALU.add).then_inc(s["s_xr"], 1)
                for c in range(OC):
                    o = cv[:, c, :].rearrange("p (b t) -> p b t", b=GB)
                    v.wait_ge(s["s_xr"], 2 * g + c + 1)
                    v.wait_ge(s["s_xs"], 2 * g)
                    for k in range(TAPS):
                        m = TAPS * (OC * g + c) + k
                        wk = w("conv", c * TAPS + k, c * TAPS + k + 1)
                        src = xpad[:, c, :, k:k + S]
                        if k == 0:
                            x = nc.vector.tensor_scalar(o, src, wk, w("bconv", c, c + 1), ALU.mult, ALU.add)
                        else:
                            v.wait_ge(s["s_conv"], m)
                            x = stt(o, src, wk, o, ALU.mult, ALU.add)
                        x.then_inc(s["s_conv"], 1)

            def front_b(g):
                v.wait_ge(s["s_tr"], g + 1)
                tr = [bank[4 + b // 2][:, (b % 2) * DI:(b % 2 + 1) * DI] for b in range(GB)]
                for b in range(GB):
                    nc.vector.bn_stats(st[:, b, :], tr[b]).then_inc(s["s_st"], 1)
                for b in range(GB):
                    v.wait_ge(s["s_st"], GB * g + b + 1)
                    nc.vector.bn_aggr(mv[:, b, :], st[:, b, :]).then_inc(s["s_mv"], 1)
                v.wait_ge(s["s_sd"], g + 1)
                nc.vector.reciprocal(rstd[:], sd[:]).then_inc(s["s_rs"], 1)
                v.wait_ge(s["s_rs"], g + 1)
                if g:
                    v.wait_ge(s["s_tb"], 2 * g)
                    v.wait_ge(s["s_xg"], g)
                for b in range(GB):
                    x = nc.vector.tensor_scalar(N0[:, b, :], tr[b], mv[:, b, 0:1], rstd[:, b:b + 1], ALU.subtract, ALU.mult)
                x.then_inc(s["s_n0"], 1)

            def front_c(g):
                v.wait_ge(s["s_nr"], g + 1)
                nc.vector.tensor_scalar(nf[:], nrm[:], 1.0, None, ALU.min).then_inc(s["s_nf"], 1)
                v.wait_ge(s["s_q1"], g + 1)
                bs = slice(g * GB, (g + 1) * GB)
                for b in range(GB):
                    x = stt(XN[:, b, :], XN[:, b, :], nf[:, b:b + 1], XP[:, 0, g * GB + b, :], ALU.mult, ALU.subtract)
                x.then_inc(s["s_rr"], 1)
                v.wait_ge(s["s_q2"], g + 1)
                v.wait_ge(s["s_rr"], g + 1)
                tt(XP[:, 2, bs, :], XN[:], XP[:, 1, bs, :], ALU.subtract).then_inc(s["s_q3"], 1)

            v.wait_ge(s["s_eps"], 1)
            front_a(0)
            for g in range(NG):
                front_b(g)
                if g + 1 < NG:
                    front_a(g + 1)
                front_c(g)

            v.wait_ge(s["s_nA"], 1)
            nc.vector.tensor_scalar(nA[:], nA[:], -0.01, None, ALU.mult).then_inc(s["s_nAm"], 1)
            v.wait_ge(s["s_th"], 1)
            v.wait_ge(s["s_nAm"], 1)
            nc.vector.tensor_scalar(ABC[:, :, 2, :], ABC[:, :, 2, :], nA[:], 1.0, ALU.mult, ALU.add).then_inc(s["s_a"], 1)
            v.wait_ge(s["s_abc"], 16 * 6 * HB)
            v.wait_ge(s["s_q3"], NG)
            nc.vector.memset(H[:, 3], 0.0).then_inc(s["s_a"], 1)
            v.wait_ge(s["s_a"], 2)

            def blk(nb, tail, warm):
                t0 = nb * TB
                for k in range(TB):
                    t = t0 + k
                    for h in range(2):
                        v.wait_ge(s["s_D"], 2 * t + h + 1)
                        if not (warm and k == 0):
                            v.wait_ge(s["s_H"], t)
                        stt(U[:, h, :], H[:, (k + 3) % 4, h, :], ABC[:, h, 2, bass.ds(t, 1)], Dt[:, k % 4, h, :],
                            ALU.mult, ALU.add).then_inc(s["s_U"], 1)
                    v.wait_ge(s["s_U"], 2 * t + 2)
                    if not (warm and k < 4):
                        v.wait_ge(s["s_yt"], t - 3)
                    nc.vector.tensor_scalar(H[:, k % 4], U[:], 10.0, -10.0, ALU.min, ALU.max).then_inc(s["s_H"], 1)
                    if tail and k == 4:
                        tail_a(nb - 1)
                    if tail and k == 7:
                        tail_b(nb - 1)

            def view(t4, nb):
                return t4[:, :, bass.ds(nb * TB, TB)].rearrange("p b t -> p t b")

            def tail_a(nb):
                v.wait_ge(s["s_yT"], nb + 1)
                if not (isinstance(nb, int) and nb == 0):
                    v.wait_ge(s["s_o"], nb)
                for c in range(OC):
                    x = stt(z[:, c], view(XNT[:, c], nb), w("dskip", c, c + 1),
                            bank[6][:, c * TB * B:(c + 1) * TB * B].rearrange("p (t b) -> p t b", b=B), ALU.mult, ALU.add)
                x.then_inc(s["s_zz"], 1)

            def tail_b(nb):
                v.wait_ge(s["s_o"], nb + 1)
                tt(view(X1, nb), view(X1, nb), bank[7][:, 0:TB * B].rearrange("p (t b) -> p t b", b=B),
                   ALU.add).then_inc(s["s_oe"], 1)

            blk(0, False, True)
            blk(1, True, False)
            with v.Fori(1, NBLK // 2) as it:
                blk(it * 2, True, False)
                blk(it * 2 + 1, True, False)
            tail_a(NBLK - 1)
            tail_b(NBLK - 1)

        @block.scalar
        def _(act):
            def a_(o, i, f, bias=0.0, scale=1.0, **k):
                return nc.scalar.activation(o, i, f, bias=bias, scale=scale, **k)

            act.wait_ge(s["s_qn"], 1)
            a_(qexp[:], qneg[:], ACT.Exp).then_inc(s["s_qe"], 1)
            act.wait_ge(s["s_cbe"], 2)

            def slot(n, g, first, more):
                if more:
                    act.wait_ge(s["s_row"], n + 1)
                    act.wait_ge(s["s_r"], n)
                    bias = cb[:, bass.ds(n, 1)]
                    a_(vrow[:], bank[1][:], ACT.Identity, bias=bias).then_inc(s["s_v"], 1)
                    a_(p1[:], bank[1][:], ACT.Identity, bias=bias).then_inc(s["s_p1"], 1)
                if not first:
                    act.wait_ge(s["s_pt"], n)
                    if not (isinstance(n, int) and n == 1):
                        act.wait_ge(s["s_ms"], n - 1)
                    a_(PTs[:], bank[7][:], ACT.Copy).then_inc(s["s_ptc"], 1)
                if more:
                    act.wait_ge(s["s_max"], n + 1)
                    act.wait_ge(s["s_rcp"], n)
                    for b in range(GB):
                        cs = slice(b * S, (b + 1) * S)
                        a_(Pr[:, cs], E[:, cs], ACT.Exp, bias=nmax[:, b:b + 1], accum_out=sums[:, b:b + 1]).then_inc(s["s_exp"], 1)

            for g in range(NG):
                slot(g, g, g == 0, True)
            with act.Fori(1, T_ITER - 1) as t:
                for g in range(NG):
                    slot(t * NG + g, g, False, True)
            for g in range(NG):
                slot((T_ITER - 1) * NG + g, g, False, True)
            slot(T_ITER * NG, 0, False, False)

            def front_a(g):
                for c in range(OC):
                    act.wait_ge(s["s_in"], 4 * g + 2 + c + 1)
                    a_(grp(GATE[:, c], g), bank[2 + c][:], ACT.Silu).then_inc(s["s_gate"], 1)
                for c in range(OC):
                    act.wait_ge(s["s_conv"], TAPS * (OC * g + c + 1))
                    if g:
                        act.wait_ge(s["s_tr"], g)
                    a_(XS[:, c, :], cv[:, c, :], ACT.Silu).then_inc(s["s_xs"], 1)

            def front_b(g):
                act.wait_ge(s["s_eps"], 1)
                act.wait_ge(s["s_mv"], GB * (g + 1))
                act.wait_ge(s["s_rs"], g)
                a_(sd[:], mv[:, :, 1], ACT.Sqrt, bias=eps[:]).then_inc(s["s_sd"], 1)

            def front_c(g):
                act.wait_ge(s["s_xn"], g + 1)
                if g:
                    act.wait_ge(s["s_nf"], g)
                for b in range(GB):
                    a_(XP[:, 1, g * GB + b, :], XN[:, b, :], ACT.Square, accum_out=ssq[:, b:b + 1]).then_inc(s["s_sq"], 1)
                act.wait_ge(s["s_sq"], GB * (g + 1))
                a_(nrm[:], ssq[:], ACT.Sqrt).then_inc(s["s_nr"], 1)
                for c in range(OC):
                    act.wait_ge(s["s_tb"], 2 * g + c + 1)
                    a_(grp(XNT[:, c], g), bank[4 + c][:], ACT.Identity, bias=w("lnb", c, c + 1), scale=w("lng", c, c + 1)).then_inc(s["s_xnt"], 1)
                act.wait_ge(s["s_nf"], g + 1)
                for b in range(GB):
                    x = a_(XP[:, 0, g * GB + b, :], XN[:, b, :], ACT.Copy, scale=nf[:, b:b + 1])
                x.then_inc(s["s_q1"], 1)
                act.wait_ge(s["s_pj"], g + 1)
                a_(PR[:, GC[g]], bank[6][0:48, :], ACT.Copy).then_inc(s["s_pje"], 1)

            front_a(0)
            for g in range(NG):
                front_b(g)
                if g + 1 < NG:
                    front_a(g + 1)
                front_c(g)

            a_(nA[:], w("alog"), ACT.Tanh).then_inc(s["s_nA"], 1)
            act.wait_ge(s["s_abc"], 16 * 6 * HB)
            a_(ABC[:, :, 2, :], ABC[:, :, 2, :], ACT.Tanh, bias=w("bdt")).then_inc(s["s_th"], 1)

            def blk(nb, j, tail, warm):
                t0 = nb * TB
                for k in range(TB):
                    t = t0 + k
                    act.wait_ge(s["s_X"], t + 1)
                    if not (warm and k < 4):
                        act.wait_ge(s["s_U"], 2 * (t - 3))
                    for h in range(2):
                        a_(Dt[:, k % 4, h, :], bank[k % 2][:, h * DI:(h + 1) * DI], ACT.Copy,
                           scale=ABC[:, h, 0, bass.ds(t, 1)]).then_inc(s["s_D"], 1)
                    if tail and k == 1:
                        copy_y(nb - 1, 1 - j)

            def copy_y(nb, j):
                for h in range(2):
                    act.wait_ge(s["s_yt"], (nb + 1) * TB)
                    if not (isinstance(nb, int) and nb == 0):
                        act.wait_ge(s["s_yT"], nb)
                    yb = bank[2 + 2 * j + h][0:TB * HB, 0:DI]
                    a_(YS[0:TB * HB, h, :], yb, ACT.Copy).then_inc(s["s_ys"], 1)

            blk(0, 0, False, True)
            blk(1, 1, True, False)
            with act.Fori(1, NBLK // 2) as it:
                blk(it * 2, 0, True, False)
                blk(it * 2 + 1, 1, True, False)
            copy_y(NBLK - 1, 1)

        @block.gpsimd
        def _(pool):
            cp = nc.gpsimd.tensor_copy
            pool.wait_ge(s["s_zero"], 2)
            pool.wait_ge(s["ld0"], 16)
            w1 = w("cond", 0, TYPES).rearrange("p (o k) -> p o k", o=1)
            x = cp(grep[:, 0:48].rearrange("p (a k) -> p a k", k=TYPES), w1.broadcast_to((P, 12, TYPES)))
            pool.wait_ge(s["s_gk"], 1)
            for n in range(T_ITER * NG):
                t, g = divmod(n, NG)
                if n:
                    pool.wait_ge(s["s_cb"], n)
                src = gk[:, t, g * GB:(g + 1) * GB, :].rearrange("p (o b) k -> p o (b k)", o=1)
                cp(grep[:, 64:112].rearrange("p (a n) -> p a n", n=ROWS_OF), src.broadcast_to((P, PARTS, ROWS_OF))).then_inc(s["s_grep"], 1)
            pool.wait_ge(s["s_aq"], 2)
            for g in range(NG):
                for c in range(3):
                    x = cp(arep[:, c, g, 0:48].rearrange("p (a k) -> p a k", k=TYPES),
                           aq[:, c, :].rearrange("p (o k) -> p o k", o=1).broadcast_to((P, 12, TYPES)))
            pool.wait_ge(s["s_ake"], 3)

            def key_cols(t, g):
                src = ak[:, :, bass.ds(t, 1), g * ROWS_OF:(g + 1) * ROWS_OF]
                o = arep[:, :, g, 64:112].rearrange("p c (a n) -> p c a n", n=ROWS_OF)
                return cp(o, src.broadcast_to((P, 3, PARTS, ROWS_OF)))

            for g in range(NG):
                key_cols(0, g).then_inc(s["s_ar"], 1)

            pool.wait_ge(s["s_mask"], TYPES + 1)

            def slot(n, t, g, final):
                pool.wait_ge(s["s_leak"], n)
                passed(pool, "passed_pool")
                cp(ES[:], BASE[:, GC[g]]).then_inc(s["s_es"], 1)
                pool.wait_ge(s["s_r"], n + 1)
                pool.wait_ge(s["s_y"], n)
                passed(pool, "passed_pool")
                cp(p2[:], rrow[:]).then_inc(s["s_p2"], 1)
                if not final:
                    pool.wait_ge(s["s_row"], n + 1)
                    passed(pool, "passed_pool")
                    key_cols(t + 1, g).then_inc(s["s_ar"], 1)
                pool.wait_ge(s["s_rcp"], n + 1)
                p3 = Pr[:].rearrange("p (b t) -> p b t", b=GB)
                nc.gpsimd.tensor_tensor(p3, p3, rsum[:].rearrange("p (b o) -> p b o", o=1).broadcast_to((P, GB, S)),
                                        ALU.mult).then_inc(s["s_sc"], 1)

            for g in range(NG):
                slot(g, 0, g, False)
            with pool.Fori(1, T_ITER - 1) as t:
                for g in range(NG):
                    slot(t * NG + g, t, g, False)
            for g in range(NG):
                slot((T_ITER - 1) * NG + g, T_ITER - 1, g, True)

            pool.wait_ge(s["ld5"], 48)
            for g in range(NG):
                pool.wait_ge(s["s_n0"], g + 1)
                if g:
                    pool.wait_ge(s["s_q3"], g)
                gb = rows_sb[:, 0:1, :].broadcast_to((P, GB, DI))
                bb = rows_sb[:, 1:2, :].broadcast_to((P, GB, DI))
                nc.gpsimd.tensor_tensor(XN[:], N0[:], gb, ALU.mult).then_inc(s["s_xg"], 1)
                pool.wait_ge(s["s_xg"], g + 1)
                nc.gpsimd.tensor_tensor(XN[:], XN[:], bb, ALU.add).then_inc(s["s_xn"], 1)
                pool.wait_ge(s["s_rr"], g + 1)
                pool.wait_ge(s["s_sq"], GB * (g + 1))
                cp(XP[:, 1, g * GB:(g + 1) * GB, :], XN[:]).then_inc(s["s_q2"], 1)

            pool.wait_ge(s["s_z0"], 1)
            pool.wait_ge(s["s_abc"], 16 * 6 * HB)

            def fill(nb, j):
                for h in range(2):
                    o = cmat[:, h, j, :].rearrange("p (k n) -> p k n", k=TB)[:, :, 0:HB]
                    c3 = ABC[:, h, 1, bass.ds(nb * TB, TB)].rearrange("p (t o) -> p t o", o=1).broadcast_to((P, TB, HB))
                    m3 = w("half8").rearrange("p (o b) -> p o b", o=1).broadcast_to((P, TB, HB))
                    nc.gpsimd.tensor_tensor(o, c3, m3, ALU.mult).then_inc(s["s_Z"], 1)

            fill(0, 0)
            fill(1, 1)

            def gate(nb):
                pool.wait_ge(s["s_zz"], nb + 1)
                for c in range(OC):
                    gv = GATE[:, c, :, bass.ds(nb * TB, TB)].rearrange("p b t -> p t b")
                    x = nc.gpsimd.tensor_tensor(z[:, c], z[:, c], gv, ALU.mult)
                x.then_inc(s["s_zg"], 1)

            with pool.Fori(0, NBLK // 2 - 1) as it:
                for j in range(2):
                    nb = it * 2 + j
                    pool.wait_ge(s["s_yt"], (nb + 1) * TB)
                    fill(nb + 2, j)
                    gate(nb)
            gate(NBLK - 2)
            gate(NBLK - 1)


def _sel_constants():
    import numpy as np
    one = 0x3F80
    sel = np.zeros((P, 2, ROWS_OF, P), np.uint16)
    for p in range(P):
        if p % 64 < PARTS * ROWS_OF:
            sel[p, p // 64, p % 64 % ROWS_OF, :] = one
    spread = np.zeros((PARTS * B, 2, P), np.uint16)
    for p in range(PARTS * B):
        b = p % B
        spread[p, b // HB, (b % HB) * NST:(b % HB + 1) * NST] = one
    return sel.reshape(P, -1), spread.reshape(PARTS * B, -1)


def kernel(**inputs):
    import numpy as np
    import concourse.bacc as bacc
    from concourse.bass_utils import run_bass_kernel_spmd

    i = {k: np.asarray(v) for k, v in inputs.items()}
    L0 = {k[8:]: v for k, v in i.items() if k.startswith("L0_cond_")}
    L1 = {k[8:]: v for k, v in i.items() if k.startswith("L1_cond_")}

    def chunks(a):
        return a.reshape(-1, P, a.shape[-1]).transpose(1, 0, 2).reshape(P, -1)

    part = np.arange(P) % 64 // ROWS_OF
    col = lambda a: a.reshape(-1, 1)
    f = {
        "ident": np.eye(P, dtype=np.float32), "wqin": L0["w_qin"].T,
        "wqt": i["fside_BxSxS_0"][:T_ITER].transpose(2, 0, 1).reshape(P, -1),
        "wpl": L0["w_pl"].T, "wpc": L0["w_pc"].T, "wq": L0["w_q"], "wk": L0["w_k"],
        "wv": chunks(L0["w_v"].T), "wpk": L0["w_pk"].T, "wpv": L0["w_pv"].T,
        "wmu": chunks(L0["w_mu"].T), "wcb": chunks(L0["w_cb"].T), "win": L1["W_in"].T,
        "wxp": chunks(L1["W_xproj"].T[:, 0:32]), "wout": chunks(L1["W_out"].T),
        "cond": chunks(i["cond_2048"].T), "qenc": i["fside_BxS_0"].T,
        "bqin": col(L0["b_qin"]), "bqt": i["mask_BxS_ff0"][:T_ITER].T, "bpl": col(L0["b_pl"]),
        "bpc": col(L0["b_pc"]), "bq": col(L0["b_q"]), "bk": col(L0["b_k"]), "bv": col(L0["b_v"]),
        "bpk": col(L0["b_pk"]), "bpv": col(L0["b_pv"]), "bmu": col(L0["b_mu"]), "bcb": col(L0["b_cb"]),
        "init": L0["init_mem"].T, "conv": chunks(L1["W_conv"][:, 0, :]), "bconv": chunks(col(L1["b_conv"])),
        "lng": chunks(col(L1["ln_g"])), "lnb": chunks(col(L1["ln_b"])), "dskip": chunks(col(L1["D"])),
        "bdt": col(np.tile(L1["b_dt"], HB)), "alog": col(np.tile(L1["A_log"], HB)),
        "nm12": col(np.where(part >= 1, -1.0, 0.0).astype(np.float32)),
        "nm3": col(np.where(part >= 2, -1.0, 0.0).astype(np.float32)),
        "half8": np.repeat(np.eye(HB, dtype=np.float32), NST, axis=0),
    }
    w128 = np.concatenate([f[n] for n, _ in COLS], axis=1)
    w16 = np.concatenate([L1["W_xproj"][32:48], L1["W_dt"].T], axis=1)
    sel, spread = _sel_constants()
    arrays = {
        "xT": i["x"].transpose(2, 0, 1).reshape(P, TOK), "adj": i["itok_BxSxS_0_4"].transpose(1, 0, 2).reshape(P, TOK),
        "w128": w128, "w16": w16, "mask": i["mask_BxS_ff1"].reshape(1, TOK),
        "rows": np.concatenate([L1["ln_g"], L1["ln_b"]]).reshape(1, 2 * DI), "sel": sel, "spread": spread,
    }
    arrays = {k: np.ascontiguousarray(v) for k, v in arrays.items()}
    nc = bacc.Bacc("TRN2", target_bir_lowering=False, num_devices=1)
    args = [nc.dram_tensor(k, a.shape, mybir.dt.from_np(a.dtype), kind="ExternalInput").ap() for k, a in arrays.items()]
    out = nc.dram_tensor("outT", (P, TOK), F32, kind="ExternalOutput").ap()
    build_program(nc, *args, out)
    r = run_bass_kernel_spmd(nc, [arrays], core_ids=[0])
    y = np.asarray(r.results[0]["outT"])
    return np.ascontiguousarray(y.reshape(D, B, S).transpose(1, 2, 0))
```

```python
from contextlib import ExitStack

import concourse.bass as bass
from concourse import mybir

F32 = mybir.dt.float32
BF16 = mybir.dt.bfloat16
I32 = mybir.dt.int32
U8 = mybir.dt.uint8
U16 = mybir.dt.uint16
ALU = mybir.AluOpType
ACT = mybir.ActivationFunctionType
AX = mybir.AxisListType

P = 128
B, S, D = 16, 128, 128
TOK = B * S
T_ITER, TYPES = 4, 4
NG, GB = 4, 4
GT = GB * S
OC = 2
DI = OC * P
NST = 16
HB = B // 2
TB = 8
NBLK = S // TB
FIRST = 4 * TB
OUT_PARTS = [(0, 8), (8, 12), (12, 15), (15, 16)]
TAPS = 4
PARTS = 3
MASKED = -9000000000000000.0
ALPHA = 0.2

COLS = [("wqin", D), ("wqt", T_ITER * D), ("qenc", B), ("cond", OC * B),
        ("bqin", 1), ("bqt", T_ITER), ("bpl", 1), ("bpc", 1), ("bq", 1), ("bk", 1), ("bv", 1),
        ("bpk", 1), ("bpv", 1), ("bmu", 1), ("bcb", 1), ("init", 1), ("conv", OC * TAPS),
        ("bconv", OC), ("dskip", OC), ("bdt", 1), ("alog", 1), ("nm12", 1), ("nm3", 1), ("half8", HB),
        ("wpl", D), ("wpk", D), ("wpv", D), ("wq", 3 * D), ("wv", 3 * D), ("wk", 3 * D), ("wpc", D),
        ("ident", P), ("wmu", 2 * D), ("wcb", 2 * D), ("win", 2 * DI), ("wxp", OC * 32), ("wout", OC * D)]
COLS16 = [("wxdt", DI), ("wdt", NST)]
ROWS_OF = GB * TYPES


def places(cols):
    at, out = 0, {}
    for name, n in cols:
        out[name] = (at, at + n)
        at += n
    return out, at


AT, WIDE = places(COLS)
EARLY = AT["wpl"][0]
AT16, WIDE16 = places(COLS16)


def build_program(nc, xT, adj, w128, w16, mask, rows, sel, spread, out):
    with ExitStack() as ctx:
        def sb(name, shape, dt=F32):
            return ctx.enter_context(nc.sbuf_tensor(name, shape, dt))

        def sem(name):
            return ctx.enter_context(nc.semaphore(name))

        bank = [ctx.enter_context(nc.psum_tensor(f"bank{i}", [P, 512], F32)) for i in range(8)]

        W = sb("W", [P, WIDE])
        W16 = sb("W16", [NST, WIDE16])
        XT = sb("XT", [P, B, S])
        arena = sb("arena", [P, 16384])
        XC = arena[:, 0:2048].rearrange("p (b t) -> p b t", b=B)
        PL = arena[:, 2048:4096].rearrange("p (b t) -> p b t", b=B)
        VL = arena[:, 4096:6144].rearrange("p (b d) -> p b d", b=B)
        BASE = arena[:, 6144:8192]
        MB = arena[:, 8192:10240].rearrange("p (b t) -> p b t", b=B)
        MK = arena[:, 10240:12288].bitcast(U8).rearrange("p (k n) -> p k n", k=TYPES)
        ADJ = arena[:, 12288:14336].bitcast(I32)
        XR = arena[:, :].bitcast(BF16).rearrange("p (t c) -> p t c", c=DI)

        spread_sb = sb("spread_sb", [PARTS * B, 2, P], BF16)
        rows_sb = sb("rows_sb", [P, 2, DI])

        qb = sb("qb", [P, B])
        qneg = sb("qneg", [P, B])
        qexp = sb("qexp", [P, B])
        cmd = sb("cmd", [P, T_ITER, B])
        pk = sb("pk", [P, T_ITER, B])
        pv = sb("pv", [P, T_ITER, B])
        gk = sb("gk", [P, T_ITER, B, TYPES])
        aq = sb("aq", [P, 3, TYPES])
        cb = sb("cb", [P, T_ITER * NG])

        work = sb("work", [P, 6656])
        PP, vrow, rrow, ES, E, Pr, PTs, MS = [work[:, i * GT:(i + 1) * GT] for i in range(8)]
        Vs = work[:, 4096:5120].rearrange("p (q b d) -> p q b d", q=2, b=GB)
        arep = work[:, 5120:6656].rearrange("p (c g n) -> p c g n", c=3, g=NG)
        XP = work[:, 0:6144].bitcast(BF16).rearrange("p (q b c) -> p q b c", q=PARTS, b=B)
        krep = work[:, 0:768].rearrange("p (n c) -> p n c", n=T_ITER * NG)
        qrep = work[:, 768:816]
        diag = work[:, 6144:6656].rearrange("p (k n) -> p k n", k=TAPS)
        p1 = sb("p1", [P, GT], BF16)
        p2 = sb("p2", [P, GT], BF16)
        Y = sb("Y", [P, GT], BF16)
        nmax = sb("nmax", [P, GB])
        sums = sb("sums", [P, GB])
        rsum = sb("rsum", [P, GB])

        X1 = sb("X1", [P, B, S])
        GATE = sb("GATE", [P, OC, B, S])
        XNT = sb("XNT", [P, OC, B, S])
        PAD = TAPS - 1
        xpad = sb("xpad", [P, OC, GB, PAD + S])
        st = sb("st", [P, GB, 6])
        mv = sb("mv", [P, GB, 2])
        sd = sb("sd", [P, GB])
        warm_in = sb("warm_in", [P, 1])
        rstd = sb("rstd", [P, GB])
        ssq = sb("ssq", [P, B])
        nrm = sb("nrm", [P, B])
        nf = gk[:].rearrange("p t b k -> p (t b k)").rearrange("p (b s) -> p b s", b=B)
        wx = sb("wx", [P, OC, 48])
        eps = sb("eps", [P, 1])
        ABC = sb("ABC", [P, 2, 3, S])
        work2 = sb("work2", [P, 6144])
        ak = work2[:, 0:768].rearrange("p (c t n) -> p c t n", c=3, t=T_ITER)
        sel_sb = work2[:, 1024:3072].bitcast(BF16).rearrange("p (q a b) -> p q a b", q=2, a=ROWS_OF)
        cv = work2[:, 0:512]
        XS = work2[:, 1024:2048].rearrange("p (c n) -> p c n", c=OC)
        RR = work2[:, 2048:3072].rearrange("p (b c) -> p b c", b=GB)
        XN = [work2[:, 3072:4096].rearrange("p (b c) -> p b c", b=GB), sb("XN1", [P, GB, DI])]
        PR = work2[0:48, 4096:6144]
        Dt = work2[:, 0:2048].rearrange("p (q h c) -> p q h c", q=4, h=2)
        H = work2[:, 2048:4096].rearrange("p (q h c) -> p q h c", q=4, h=2)
        U = work2[:, 4096:4608].rearrange("p (h c) -> p h c", h=2)
        YS = work2[:, 4608:5120].rearrange("p (h c) -> p h c", h=2)
        z = work2[:, 5120:5120 + OC * TB * B].rearrange("p (c t b) -> p c t b", c=OC, t=TB)
        cmat = sb("cmat", [P, 2, 2, TB * (TB + 1) * HB])
        nA = sb("nA", [P, 1])
        ob = sb("ob", [P, TB * B])
        OUT = XT[:].rearrange("p b t -> p (b t)").rearrange("p (t b) -> p t b", b=B)

        def w(name, a=0, b=None):
            lo, hi = AT[name]
            return W[:, lo + a:(lo + b if b is not None else hi)]

        scrx = nc.dram_tensor("rows_scratch", (PARTS * B, S, DI), BF16, kind="Internal").ap()
        scr = nc.dram_tensor("proj_scratch", (3, B, NST, S), F32, kind="Internal").ap()

        names = ("s_sk s_zc s_ob ld0 ldw s_krep s_q1r ld1 ld2 ld3 ld4 ld5 s_qb s_qn s_qe s_qd s_qbase s_cmd s_cmde s_pk s_pke s_gk s_ak s_ake s_aq "
                 "s_grep s_cb s_cbe s_ar s_zero s_pl s_ple s_vl s_vle s_mask s_xc0 "
                 "s_pc s_pp s_row s_v s_p1 s_r s_p2 s_y s_V s_Ve s_S s_es s_pred s_leak s_max s_exp s_rcp "
                 "s_sc s_pt s_ptc s_ms s_mse s_cx s_xc "
                 "s_cbo s_x1 s_in s_xr s_gate s_conv s_convp s_diag s_xs s_tr s_st s_mv s_sd s_rs s_n0 s_xg s_xn s_sq s_nr s_nf "
                 "s_q1 s_rr s_q2 s_q3 s_tb s_xnt s_pj s_pje s_wx s_wxe s_eps "
                 "s_scr s_xg4 s_abc s_th s_nA s_nAm s_a s_warm s_nft s_B s_xrow s_xrest s_X s_D s_U s_H s_yt s_yb s_Z s_z0 s_ys s_yT s_zz s_zg s_o s_oe s_out passed_dve passed_pe passed_pool").split()
        s = {n: sem(n) for n in names}

        block = ctx.enter_context(nc.Block())
        GC = [slice(g * GT, (g + 1) * GT) for g in range(NG)]

        def grp(t3, g):
            return t3[:, g * GB:(g + 1) * GB, :].rearrange("p b t -> p (b t)")

        def passed(eng, signal):
            eng.sem_inc(s[signal], 1)

        def proj_out(eng, g):
            eng.wait_ge(s["s_pje"], g + 1)
            for k in range(3):
                eng.dma_start(scr[k, g * GB:(g + 1) * GB].rearrange("b s t -> s b t"),
                              PR[k * NST:(k + 1) * NST, GC[g]].rearrange("s (b t) -> s b t", b=GB)).then_inc(s["s_scr"], 16)

        @block.sync
        def _(sp):
            sp.dma_start(W[:, 0:EARLY], w128[:, 0:EARLY]).then_inc(s["ld0"], 16)
            sp.dma_start(W[:, EARLY:], w128[:, EARLY:]).then_inc(s["ldw"], 16)
            sp.dma_start(XT[:].rearrange("p b t -> p (b t)"), xT).then_inc(s["ld1"], 16)
            sp.dma_start(ADJ, adj).then_inc(s["ld2"], 16)
            sp.dma_start(MB.rearrange("p b t -> p (b t)"), mask.broadcast_to((P, TOK))).then_inc(s["ld3"], 16)
            sp.dma_start(sel_sb.rearrange("p q a b -> p (q a b)").bitcast(U16), sel).then_inc(s["ld4"], 16)
            sp.dma_start(spread_sb[:].rearrange("p a b -> p (a b)").bitcast(U16), spread).then_inc(s["ld5"], 16)
            sp.dma_start(W16[:], w16).then_inc(s["ld5"], 16)
            sp.dma_start(rows_sb[:].rearrange("p a b -> p (a b)"), rows.broadcast_to((P, 2 * DI))).then_inc(s["ld5"], 16)
            def rows_out(g, q):
                sp.wait_ge(s[("s_q1", "s_q2", "s_q3")[q]], g + 1)
                r0 = (g * PARTS + q) * GB
                sp.dma_start(scrx[r0:r0 + GB, :, :].rearrange("r t c -> t r c"),
                             XP[:, q, g * GB:(g + 1) * GB, :]).then_inc(s["s_xg4"], 16)

            def rows_in(g0, g1, steps, done):
                r = slice(g0 * PARTS * GB, g1 * PARTS * GB)
                sp.dma_start(XR[r, steps, :], scrx[r, steps, :]).then_inc(s[done], 16)

            for g in range(NG - 1):
                if g == NG - 2:
                    sp.wait_ge(s["s_cbo"], NG)
                    sp.wait_ge(s["s_xg4"], 16 * PARTS * g)
                    rows_in(0, g, slice(0, S), "s_xrow")
                for q in range(PARTS):
                    rows_out(g, q)
                proj_out(sp, g)
            rows_out(NG - 1, 0)
            rows_out(NG - 1, 1)
            rows_out(NG - 1, 2)
            sp.wait_ge(s["s_xg4"], 16 * PARTS * NG)
            rows_in(NG - 2, NG, slice(0, FIRST), "s_xrow")
            rows_in(NG - 2, NG, slice(FIRST, S), "s_xrest")
            for b0, b1 in OUT_PARTS:
                sp.wait_ge(s["s_oe"], b1)
                sp.dma_start(out[:, b0 * TB * B:b1 * TB * B],
                             OUT[:, b0 * TB:b1 * TB, :].rearrange("p t b -> p (t b)")).then_inc(s["s_out"], 16)
            sp.wait_ge(s["s_out"], 16 * len(OUT_PARTS))

        @block.tensor
        def _(pe):
            def mm(o, a, b, start=True, stop=True):
                return nc.tensor.matmul(o, a, b, start=start, stop=stop)

            ident = w("ident")
            pe.wait_ge(s["ld0"], 16)
            mm(bank[0][:, 0:B], w("wqin"), w("qenc")).then_inc(s["s_qb"], 1)
            pe.wait_ge(s["s_qbase"], 1)
            for t in range(T_ITER):
                x = mm(bank[1][:, t * B:(t + 1) * B], w("wqt", t * D, (t + 1) * D), qb[:])
            x.then_inc(s["s_cmd"], 1)
            pe.wait_ge(s["ldw"], 16)
            pe.wait_ge(s["ld1"], 16)
            for g in range(NG):
                mm(bank[3 + g][:], w("wpl"), grp(XT, g)).then_inc(s["s_pl"], 1)
            pe.wait_ge(s["s_cmde"], 1)
            cf = cmd[:].rearrange("p t b -> p (t b)")
            mm(bank[0][:, 0:64], w("wpk"), cf)
            mm(bank[0][:, 64:128], w("wpv"), cf).then_inc(s["s_pk"], 1)
            for c in range(3):
                x = mm(bank[2][:, c * TYPES:(c + 1) * TYPES], w("wq", c * D, (c + 1) * D), w("cond", 0, TYPES))
            x.then_inc(s["s_aq"], 1)
            for g in range(NG):
                pe.wait_ge(s["s_ple"], g + 1)
                for b in range(GB):
                    x = mm(bank[3 + g][:, b * D:(b + 1) * D], XT[:, g * GB + b, :], w("wv", 0, D))
                x.then_inc(s["s_vl"], 1)
            pe.wait_ge(s["s_gk"], 1)
            gkf = gk[:].rearrange("p t b k -> p (t b k)")
            for c in range(3):
                if c == 2:
                    pe.wait_ge(s["s_pke"], 2)
                mm(bank[[1, 7, 0][c]][:, 0:256], w("wk", c * D, (c + 1) * D), gkf).then_inc(s["s_ak"], 1)
            pe.wait_ge(s["s_aq"], 2)
            pe.wait_ge(s["s_krep"], 2)
            mm(bank[2][0:48, 16:17], qrep, w("bq"))
            for n in range(T_ITER * NG):
                x = mm(bank[2][64:112, 17 + n:18 + n], krep[:, n, :], w("bk"))
            x.then_inc(s["s_cb"], 1)
            pe.wait_ge(s["ld5"], 48)
            pe.wait_ge(s["s_ake"], 1)
            for c in range(OC):
                x = mm(bank[1][:, c * NST:(c + 1) * NST], W16[:, c * P:(c + 1) * P], W16[:, AT16["wdt"][0]:AT16["wdt"][1]])
            x.then_inc(s["s_wx"], 1)
            pe.wait_ge(s["s_cbe"], 2)
            pe.wait_ge(s["s_wxe"], 2)
            pe.wait_ge(s["ld4"], 16)
            for g in range(NG):
                pe.wait_ge(s["s_vle"], g + 1)
            pe.wait_ge(s["s_ake"], 3)
            pe.wait_ge(s["s_xc0"], 1)

            def context(n, g):
                mm(bank[2][:], w("wpc"), grp(XC, g)).then_inc(s["s_pc"], 1)

            def score_rows(n, g):
                pe.wait_ge(s["s_pp"], n + 1)
                pe.wait_ge(s["s_ar"], n + 1)
                mm(bank[1][:], arep[:, 0, g, :], grp(XT, g), True, False)
                mm(bank[1][:], arep[:, 1, g, :], grp(XC, g), False, False)
                mm(bank[1][:], arep[:, 2, g, :], PP[:], False, True).then_inc(s["s_row"], 1)

            def slot(n, g, static, more=True, ahead=True):
                pg = (g - 1) % NG
                before = not (static and n == 0)

                def scores(k):
                    for b in range(GB):
                        o = bank[3 + k][:, b * S:(b + 1) * S]
                        row = b * TYPES + k
                        mm(o, Y[:, b * S:(b + 1) * S], sel_sb[:, 0, row, :], True, False)
                        x = mm(o, sel_sb[:, 1, row, :], Y[:, b * S:(b + 1) * S], False, True)
                    x.then_inc(s["s_S"], 1)

                if more:
                    for b in range(GB):
                        o = bank[2][:, b * D:(b + 1) * D]
                        mm(o, XC[:, g * GB + b, :], w("wv", D, 2 * D), True, False)
                        x = mm(o, PP[:, b * S:(b + 1) * S], w("wv", 2 * D, 3 * D), False, True)
                    x.then_inc(s["s_V"], 1)
                    pe.wait_ge(s["s_y"], n + 1)
                    if before:
                        pe.wait_ge(s["s_pred"], n * TYPES)
                    scores(0)
                    scores(1)
                if before:
                    pe.wait_ge(s["s_sc"], n)
                    if not (static and n == 1):
                        pe.wait_ge(s["s_xc"], n - 1)
                    for b in range(GB):
                        x = nc.tensor.transpose(bank[7][:, b * S:(b + 1) * S], Pr[:, b * S:(b + 1) * S], ident)
                    x.then_inc(s["s_pt"], 1)
                if more and ahead:
                    pe.wait_ge(s["s_Ve"], n + 1)
                    if not (static and n < NG):
                        pe.wait_ge(s["s_xc"], n - 2)
                    elif n == NG - 1:
                        pe.wait_ge(s["s_xc"], 1)
                    context(n + 1, (g + 1) % NG)
                if before:
                    pe.wait_ge(s["s_ptc"], n)
                    if not (static and n == 1):
                        pe.wait_ge(s["s_mse"], n - 1)
                    for b in range(GB):
                        x = mm(bank[0][:, b * S:(b + 1) * S], Vs[:, pg % 2, b, :], PTs[:, b * S:(b + 1) * S])
                    x.then_inc(s["s_ms"], 1)
                if more:
                    scores(2)
                    scores(3)
                    if ahead:
                        score_rows(n + 1, (g + 1) % NG)
                if before:
                    pe.wait_ge(s["s_mse"], n)
                    mm(bank[7][:], w("wmu", 0, D), grp(XC, pg), True, False)
                    mm(bank[7][:], w("wmu", D, 2 * D), MS[:], False, True).then_inc(s["s_cx"], 1)

            context(0, 0)
            score_rows(0, 0)
            for g in range(NG):
                slot(g, g, True)
            with pe.Fori(1, T_ITER - 1) as t:
                for g in range(NG):
                    slot(t * NG + g, g, False)
            for g in range(NG):
                slot((T_ITER - 1) * NG + g, g, True, ahead=g < NG - 1)

            WIN = [bank[1], bank[2], bank[3], bank[6]]

            def front_a(g):
                if g == 0:
                    pe.wait_ge(s["s_pred"], T_ITER * NG * TYPES)
                if g == NG - 1:
                    pe.wait_ge(s["s_xc"], T_ITER * NG)
                o = bank[5 if g == 0 else 7]
                if g > 1:
                    pe.wait_ge(s["s_x1"], g)
                mm(o[:], w("wcb", 0, D), grp(XT, g), True, False)
                mm(o[:], w("wcb", D, 2 * D), grp(XC, g), False, True).then_inc(s["s_cbo"], 1)
                pe.wait_ge(s["s_x1"], g + 1)
                for c in range(4):
                    if g:
                        pe.wait_ge([s["s_xr"], s["s_xs"], s["s_gate"], s["s_gate"]][c], 2 * g)
                    mm(WIN[c][:], w("win", c * P, (c + 1) * P), grp(X1, g)).then_inc(s["s_in"], 1)

            def taps(g):
                pe.wait_ge(s["s_diag"], TAPS)
                pe.wait_ge(s["s_xr"], 2 * g + 2)
                for k in range(TAPS):
                    x = mm(WIN[1][:], diag[:, k, :], xpad[:, 1, :, k:k + S], k == 0, k == TAPS - 1)
                x.then_inc(s["s_convp"], 1)

            def turn(g):
                pe.wait_ge(s["s_xs"], 2 * (g + 1))
                if g:
                    pe.wait_ge(s["s_xnt"], 2 * g)
                for b in range(GB):
                    for c in range(OC):
                        at = (b * OC + c) * P
                        x = nc.tensor.transpose(bank[4 + at // 512][:, at % 512:at % 512 + P],
                                                XS[:, c, b * S:(b + 1) * S], ident)
                x.then_inc(s["s_tr"], 1)

            def turn_back(g):
                pe.wait_ge(s["s_xn"], g + 1)
                for c in range(OC):
                    for b in range(GB):
                        x = nc.tensor.transpose(bank[4 + c][:, b * S:(b + 1) * S], XN[g % 2][:, b, c * P:(c + 1) * P], ident)
                    x.then_inc(s["s_tb"], 1)

            def project(g):
                pe.wait_ge(s["s_xnt"], 2 * (g + 1))
                if g:
                    pe.wait_ge(s["s_pje"], g)
                for c in range(OC):
                    x = mm(bank[0][0:48, :], wx[:, c, :], grp(XNT[:, c], g), c == 0, c == OC - 1)
                x.then_inc(s["s_pj"], 1)

            front_a(0)
            slot(T_ITER * NG, 0, True, more=False)
            taps(0)
            for g in range(NG):
                turn(g)
                if g:
                    project(g - 1)
                if g + 1 < NG:
                    front_a(g + 1)
                turn_back(g)
                if g + 1 < NG:
                    taps(g + 1)
            project(NG - 1)

            pe.wait_ge(s["s_pje"], NG)
            pe.wait_ge(s["s_nf"], 1)
            for h in range(2):
                x = mm(bank[7][:, h * S:(h + 1) * S], nf[:, h * HB:(h + 1) * HB, :].rearrange("p b s -> p (b s)"), ident)
            x.then_inc(s["s_nft"], 1)

            def spread_x(t, slot_):
                for h in range(2):
                    x = mm(bank[slot_][:, h * DI:(h + 1) * DI], spread_sb[:, h, :],
                           XR[0:PARTS * B, bass.ds(t, 1), :].rearrange("p a c -> p (a c)"))
                x.then_inc(s["s_X"], 1)

            def blk(nb, j, tail, warm, ahead):
                t0 = nb * TB
                if warm:
                    spread_x(t0, 0)
                    spread_x(t0 + 1, 1)
                pe.wait_ge(s["s_Z"], 2 * (nb + 1))
                for k in range(TB):
                    t = t0 + k
                    if k + 2 < TB or ahead:
                        pe.wait_ge(s["s_D"], 2 * (t + 1))
                        spread_x(t + 2, k % 2)
                    for h in range(2):
                        pe.wait_ge(s["s_H"], 2 * t + h + 1)
                        x = mm(bank[2 + 2 * j + h][0:TB * HB, 0:DI], cmat[:, h, j, k * TB * HB:(k + 1) * TB * HB],
                               H[:, k % 4, h, :], k == 0, k == TB - 1)
                        x.then_inc(s["s_yt"], 1)
                    if tail and k == 2:
                        tail_a(nb - 1)
                    if tail and k == 6:
                        tail_b(nb - 1)

            def tail_a(nb):
                pe.wait_ge(s["s_ys"], 2 * (nb + 1))
                if not (isinstance(nb, int) and nb == 0):
                    pe.wait_ge(s["s_zc"], nb)
                passed(pe, "passed_pe")
                for c in range(OC):
                    for h in range(2):
                        o = bank[6][:, c * TB * B:(c + 1) * TB * B].rearrange("p (t b) -> p t b", b=B)[:, :, h * HB:(h + 1) * HB]
                        x = nc.tensor.transpose(o, YS[0:TB * HB, h, c * P:(c + 1) * P], ident[0:TB * HB, 0:TB * HB])
                x.then_inc(s["s_yT"], 1)

            def tail_b(nb):
                pe.wait_ge(s["s_zg"], nb + 1)
                if isinstance(nb, int) and nb == 0:
                    pe.wait_ge(s["s_B"], 1)
                if not (isinstance(nb, int) and nb == 0):
                    pe.wait_ge(s["s_ob"], nb)
                for c in range(OC):
                    x = mm(bank[7][:, 0:TB * B], w("wout", c * D, (c + 1) * D), z[:, c].rearrange("p t b -> p (t b)"),
                           c == 0, c == OC - 1)
                x.then_inc(s["s_o"], 1)

            pe.wait_ge(s["s_xrow"], 16 * 2)
            blk(0, 0, False, True, True)
            blk(1, 1, True, False, True)
            pe.wait_ge(s["s_xrest"], 16)
            with pe.Fori(1, NBLK // 2 - 1) as it:
                blk(it * 2, 0, True, False, True)
                blk(it * 2 + 1, 1, True, False, True)
            blk(NBLK - 2, 0, True, False, True)
            blk(NBLK - 1, 1, True, False, False)
            tail_a(NBLK - 1)
            tail_b(NBLK - 1)

        @block.vector
        def _(v):
            def tt(o, a, b, op):
                return nc.vector.tensor_tensor(o, a, b, op)

            def stt(o, a, sc, b, op0, op1):
                return nc.vector.scalar_tensor_tensor(out=o, in0=a, scalar=sc, in1=b, op0=op0, op1=op1)

            nc.vector.memset(cb[:], 0.0).then_inc(s["s_zero"], 1)
            nc.vector.memset(arep[:], 0.0).then_inc(s["s_zero"], 1)
            nc.vector.memset(eps[:], 1e-5).then_inc(s["s_eps"], 1)
            nc.vector.memset(xpad[:], 0.0).then_inc(s["s_zero"], 1)
            nc.vector.memset(cmat[:], 0.0).then_inc(s["s_z0"], 1)
            v.wait_ge(s["ld0"], 16)
            v.wait_ge(s["s_qb"], 1)
            nc.vector.tensor_scalar(qb[:], bank[0][:, 0:B], w("bqin"), 0.0, ALU.add, ALU.max).then_inc(s["s_qd"], 1)
            nc.vector.tensor_scalar(qneg[:], bank[0][:, 0:B], w("bqin"), 0.0, ALU.add, ALU.min).then_inc(s["s_qn"], 1)
            v.wait_ge(s["s_qe"], 1)
            v.wait_ge(s["s_qd"], 1)
            stt(qb[:], qexp[:], -1.0, qb[:], ALU.add, ALU.add).then_inc(s["s_qbase"], 1)
            v.wait_ge(s["s_cmd"], 1)
            for t in range(T_ITER):
                x = nc.vector.tensor_scalar(cmd[:, t, :], bank[1][:, t * B:(t + 1) * B], w("bqt", t, t + 1), None, ALU.add)
            x.then_inc(s["s_cmde"], 1)
            v.wait_ge(s["ldw"], 16)
            nc.vector.tensor_copy(qrep.rearrange("p (a k) -> p a k", k=TYPES),
                                  w("cond", 0, TYPES).rearrange("p (o k) -> p o k", o=1).broadcast_to((P, 12, TYPES))).then_inc(s["s_krep"], 1)
            for g in range(NG):
                v.wait_ge(s["s_pl"], g + 1)
                nc.vector.tensor_scalar(grp(PL, g), bank[3 + g][:], w("bpl"), None, ALU.add).then_inc(s["s_ple"], 1)
            v.wait_ge(s["s_pk"], 1)
            nc.vector.tensor_scalar(pk[:].rearrange("p t b -> p (t b)"), bank[0][:, 0:64], w("bpk"), None, ALU.add).then_inc(s["s_pke"], 1)
            nc.vector.tensor_scalar(pv[:].rearrange("p t b -> p (t b)"), bank[0][:, 64:128], w("bpv"), None, ALU.add).then_inc(s["s_pke"], 1)
            v.wait_ge(s["s_pke"], 2)
            w2 = w("cond", B, B + TYPES)
            tt(gk[:].rearrange("p t b k -> p (t b) k"),
               pk[:].rearrange("p t (b o) -> p (t b) o", o=1).broadcast_to((P, T_ITER * B, TYPES)),
               w2.rearrange("p (o k) -> p o k", o=1).broadcast_to((P, T_ITER * B, TYPES)), ALU.mult).then_inc(s["s_gk"], 1)
            v.wait_ge(s["s_gk"], 1)
            for n in range(0, T_ITER * NG, NG):
                t = n // NG
                x = nc.vector.tensor_copy(krep[:, n:n + NG, :].rearrange("p g (a r) -> p g a r", a=PARTS),
                                          gk[:, t].rearrange("p (g b) k -> p g (b k)", g=NG).rearrange("p g (o r) -> p g o r", o=1)
                                          .broadcast_to((P, NG, PARTS, ROWS_OF)))
            x.then_inc(s["s_krep"], 1)
            v.wait_ge(s["s_aq"], 1)
            nc.vector.tensor_copy(aq[:].rearrange("p c k -> p (c k)"), bank[2][:, 0:12]).then_inc(s["s_aq"], 1)
            for g in range(NG):
                v.wait_ge(s["s_vl"], g + 1)
                nc.vector.tensor_copy(VL[:, g * GB:(g + 1) * GB, :].rearrange("p b d -> p (b d)"), bank[3 + g][:]).then_inc(s["s_vle"], 1)
            for c in range(3):
                v.wait_ge(s["s_ak"], c + 1)
                nc.vector.tensor_copy(ak[:, c].rearrange("p t n -> p (t n)"), bank[[1, 7, 0][c]][:, 0:256]).then_inc(s["s_ake"], 1)
            v.wait_ge(s["ld3"], 16)
            nc.vector.tensor_scalar(XC.rearrange("p b t -> p (b t)"), MB.rearrange("p b t -> p (b t)"), w("init"), None,
                                    ALU.mult).then_inc(s["s_xc0"], 1)
            v.wait_ge(s["s_cb"], 1)
            v.wait_ge(s["s_zero"], 1)
            nc.vector.tensor_copy(cb[0:48, :], bank[2][0:48, 16:17].broadcast_to((48, T_ITER * NG))).then_inc(s["s_cbe"], 1)
            nc.vector.tensor_copy(cb[64:112, :], bank[2][64:112, 17:17 + T_ITER * NG]).then_inc(s["s_cbe"], 1)
            v.wait_ge(s["s_wx"], 1)
            nc.vector.tensor_copy(wx[:, :, 0:32], w("wxp").rearrange("p (c n) -> p c n", c=OC)).then_inc(s["s_wxe"], 1)
            nc.vector.tensor_copy(wx[:, :, 32:48], bank[1][:, 0:2 * NST].rearrange("p (c n) -> p c n", c=OC)).then_inc(s["s_wxe"], 1)
            v.wait_ge(s["s_vle"], NG)
            v.wait_ge(s["s_ple"], NG)

            def masks(g):
                for k in range(TYPES):
                    nc.vector.tensor_scalar(MK[:, k, GC[g]], ADJ[:, GC[g]], float(k + 1), None, ALU.is_equal).then_inc(s["s_mask"], 1)
                nc.vector.tensor_scalar(BASE[:, GC[g]], ADJ[:, GC[g]], 0.0, MASKED / ALPHA, ALU.is_le, ALU.mult).then_inc(s["s_mask"], 1)

            def joint(n, g):
                v.wait_ge(s["s_pc"], n + 1)
                stt(PP[:], bank[2][:], w("bpc"), grp(PL, g), ALU.add, ALU.mult).then_inc(s["s_pp"], 1)

            def new_context(n, g, final):
                v.wait_ge(s["s_cx"], n + 1)
                if final:
                    nc.vector.tensor_scalar(grp(XC, g), bank[7][:], w("bmu"), None, ALU.add).then_inc(s["s_xc"], 1)
                else:
                    stt(grp(XC, g), bank[7][:], w("bmu"), grp(MB, g), ALU.add, ALU.mult).then_inc(s["s_xc"], 1)

            def rows_rest(n):
                v.wait_ge(s["s_v"], n + 1)
                v.wait_ge(s["s_r"], n)
                nc.vector.tensor_copy(p1[:], vrow[:]).then_inc(s["s_p1"], 1)
                v.wait_ge(s["s_p1"], n + 1)
                v.wait_ge(s["s_y"], n)
                stt(rrow[:], p1[:], w("nm12"), vrow[:], ALU.mult, ALU.add).then_inc(s["s_r"], 1)

            def rows_second(n):
                v.wait_ge(s["s_r"], n + 1)
                nc.vector.tensor_copy(p2[:], rrow[:]).then_inc(s["s_p2"], 1)

            def rows_split(n):
                v.wait_ge(s["s_p2"], n + 1)
                v.wait_ge(s["s_S"], n * TYPES)
                stt(Y[:], p2[:], w("nm3"), rrow[:], ALU.mult, ALU.add).then_inc(s["s_y"], 1)

            def slot(n, t, g, static, more=True, ahead=True):
                pg = (g - 1) % NG
                before = not (static and n == 0)

                def choose(k):
                    v.wait_ge(s["s_S"], n * TYPES + k + 1)
                    v.wait_ge(s["s_pred"], n * TYPES + k)
                    passed(v, "passed_dve")
                    nc.vector.copy_predicated(ES[:], MK[:, k, GC[g]], bank[3 + k][:]).then_inc(s["s_pred"], 1)

                if more:
                    v.wait_ge(s["s_V"], n + 1)
                    tt(Vs[:, g % 2].rearrange("p b d -> p (b d)"), bank[2][:],
                       VL[:, g * GB:(g + 1) * GB, :].rearrange("p b d -> p (b d)"), ALU.add).then_inc(s["s_Ve"], 1)
                    v.wait_ge(s["s_es"], n + 1)
                    choose(0)
                    choose(1)
                    if ahead:
                        joint(n + 1, (g + 1) % NG)
                if before:
                    v.wait_ge(s["s_ms"], n)
                    pt = (t if g else t - 1)
                    stt(MS[:].rearrange("p (b t) -> p b t", b=GB), bank[0][:].rearrange("p (b t) -> p b t", b=GB), w("bv"),
                        pv[:, bass.ds(pt, 1), pg * GB:(pg + 1) * GB].rearrange("p o b -> p b o").broadcast_to((P, GB, S)),
                        ALU.add, ALU.mult).then_inc(s["s_mse"], 1)
                if more:
                    for k in range(2, TYPES):
                        choose(k)
                    v.wait_ge(s["s_pred"], n * TYPES + TYPES)
                    stt(E[:], ES[:], ALPHA, ES[:], ALU.mult, ALU.max).then_inc(s["s_leak"], 1)
                    v.wait_ge(s["s_leak"], n + 1)
                    nc.vector.tensor_reduce(nmax[:], E[:].rearrange("p (b t) -> p b t", b=GB), AX.X, ALU.max,
                                            negate=True).then_inc(s["s_max"], 1)
                    if ahead:
                        rows_rest(n + 1)
                    if ahead:
                        rows_second(n + 1)
                    v.wait_ge(s["s_exp"], (n + 1) * GB)
                    v.wait_ge(s["s_sc"], n)
                    nc.vector.reciprocal(rsum[:], sums[:]).then_inc(s["s_rcp"], 1)
                    if ahead:
                        rows_split(n + 1)
                if before:
                    new_context(n - 1, pg, static and n - 1 >= (T_ITER - 1) * NG)

            joint(0, 0)
            v.wait_ge(s["ld2"], 16)
            masks(0)
            rows_rest(0)
            rows_second(0)
            rows_split(0)
            for g in range(NG):
                v.wait_ge(s["s_mask"], (TYPES + 1) * (g + 1))
                slot(g, 0, g, True)
                if g + 1 < NG:
                    masks(g + 1)
            with v.Fori(1, T_ITER - 1) as t:
                for g in range(NG):
                    slot(t * NG + g, t, g, False)
            t = T_ITER - 1
            for g in range(NG):
                slot(t * NG + g, t, g, True, ahead=g < NG - 1)

            def residual(g):
                v.wait_ge(s["s_cbo"], g + 1)
                stt(grp(X1, g), bank[5 if g == 0 else 7][:], w("bcb"), grp(XT, g), ALU.add, ALU.add).then_inc(s["s_x1"], 1)

            def widen(g):
                for c in range(OC):
                    v.wait_ge(s["s_in"], 4 * g + c + 1)
                    if g:
                        v.wait_ge(s["s_conv"] if c == 0 else s["s_convp"], TAPS * g if c == 0 else g)
                    tt(xpad[:, c, :, PAD:], bank[1 + c][:].rearrange("p (b t) -> p b t", b=GB),
                       w("cond", c * B + g * GB, c * B + (g + 1) * GB).rearrange("p (b o) -> p b o", o=1).broadcast_to((P, GB, S)),
                       ALU.add).then_inc(s["s_xr"], 1)

            tr = [bank[4 + b // 2][:, (b % 2) * DI:(b % 2 + 1) * DI] for b in range(GB)]

            def convolve(g):
                if g:
                    v.wait_ge(s["s_xs"], 2 * (g - 1) + 1)
                v.wait_ge(s["s_xr"], 2 * g + 1)
                o = cv.rearrange("p (b t) -> p b t", b=GB)
                for k in range(TAPS):
                    wk = w("conv", k, k + 1)
                    src = xpad[:, 0, :, k:k + S]
                    if k == 0:
                        nc.vector.tensor_scalar(o, src, wk, w("bconv", 0, 1), ALU.mult, ALU.add).then_inc(s["s_conv"], 1)
                    else:
                        v.wait_ge(s["s_conv"], TAPS * g + k)
                        stt(o, src, wk, o, ALU.mult, ALU.add).then_inc(s["s_conv"], 1)

            def moments(g):
                v.wait_ge(s["s_tr"], g + 1)
                for b in range(GB):
                    nc.vector.bn_stats(st[:, b, :], tr[b]).then_inc(s["s_st"], 1)
                for b in range(GB):
                    v.wait_ge(s["s_st"], GB * g + b + 1)
                    nc.vector.bn_aggr(mv[:, b, :], st[:, b, :]).then_inc(s["s_mv"], 1)

            def normalize(g):
                if g > 1:
                    v.wait_ge(s["s_sq"], GB * (g - 1))
                    v.wait_ge(s["s_rr"], g - 1)
                v.wait_ge(s["s_mv"], GB * (g + 1))
                for b in range(GB):
                    stt(XN[g % 2][:, b, :], tr[b], mv[:, b, 0:1], rows_sb[:, 0, :], ALU.subtract, ALU.mult).then_inc(s["s_n0"], 1)
                v.wait_ge(s["s_sd"], g + 1)
                nc.vector.reciprocal(rstd[:], sd[:]).then_inc(s["s_rs"], 1)
                v.wait_ge(s["s_rs"], g + 1)
                for b in range(GB):
                    v.wait_ge(s["s_n0"], GB * g + b + 1)
                    x = stt(XN[g % 2][:, b, :], XN[g % 2][:, b, :], rstd[:, b:b + 1], rows_sb[:, 1, :], ALU.mult, ALU.add)
                x.then_inc(s["s_xn"], 1)

            def third_part(g):
                v.wait_ge(s["s_q2"], g + 1)
                v.wait_ge(s["s_rr"], g + 1)
                bs = slice(g * GB, (g + 1) * GB)
                tt(XP[:, 2, bs, :], RR[:], XP[:, 1, bs, :], ALU.subtract).then_inc(s["s_q3"], 1)

            v.wait_ge(s["s_eps"], 1)
            v.wait_ge(s["ld5"], 48)
            v.wait_ge(s["s_zero"], 3)
            residual(0)
            v.wait_ge(s["s_row"], T_ITER * NG)
            for k in range(TAPS):
                nc.vector.tensor_scalar(diag[:, k, :], w("ident"), w("conv", TAPS + k, TAPS + k + 1), None, ALU.mult).then_inc(s["s_diag"], 1)
            widen(0)
            slot(T_ITER * NG, T_ITER, 0, True, more=False)
            convolve(0)
            for g in range(NG):
                moments(g)
                if g + 1 < NG:
                    residual(g + 1)
                normalize(g)
                if g + 1 < NG:
                    widen(g + 1)
                    convolve(g + 1)
                if g:
                    third_part(g - 1)
            g = NG - 1
            bs = slice(g * GB, (g + 1) * GB)
            v.wait_ge(s["s_xn"], NG)
            nc.vector.tensor_copy(XP[:, 0, bs, :], XN[g % 2][:]).then_inc(s["s_q1"], 1)
            v.wait_ge(s["s_q1"], NG)
            v.wait_ge(s["s_q3"], NG - 1)
            tt(RR[:], XN[g % 2][:], XP[:, 0, bs, :], ALU.subtract).then_inc(s["s_rr"], 1)
            v.wait_ge(s["s_rr"], NG)
            nc.vector.tensor_copy(XP[:, 1, bs, :], RR[:]).then_inc(s["s_q2"], 1)
            third_part(g)
            v.wait_ge(s["s_nr"], 1)
            nc.vector.tensor_scalar(nf, nrm[:].rearrange("p (b o) -> p b o", o=1).broadcast_to((P, B, NST)), 1.0, None,
                                    ALU.min).then_inc(s["s_nf"], 1)

            v.wait_ge(s["s_nA"], 1)
            nc.vector.tensor_scalar(nA[:], nA[:], -0.01, None, ALU.mult).then_inc(s["s_nAm"], 1)
            v.wait_ge(s["s_abc"], 16 * 3)
            v.wait_ge(s["s_th"], 1)
            v.wait_ge(s["s_nAm"], 1)
            nc.vector.tensor_scalar(ABC[:, :, 2, :], ABC[:, :, 2, :], nA[:], 1.0, ALU.mult, ALU.add).then_inc(s["s_a"], 1)
            v.wait_ge(s["s_nft"], 1)
            tt(ABC[:, :, 0, :], ABC[:, :, 0, :], bank[7][:, 0:2 * S].rearrange("p (h t) -> p h t", h=2), ALU.mult).then_inc(s["s_B"], 1)
            v.wait_ge(s["s_q3"], NG)
            nc.vector.memset(H[:, 3], 0.0).then_inc(s["s_a"], 1)
            v.wait_ge(s["s_a"], 2)

            def blk(nb, warm):
                t0 = nb * TB
                for k in range(TB):
                    t = t0 + k
                    for h in range(2):
                        v.wait_ge(s["s_D"], 2 * t + h + 1)
                        if not (warm and k == 0):
                            v.wait_ge(s["s_H"], 2 * t + h - 1)
                        stt(U[:, h, :], H[:, (k + 3) % 4, h, :], ABC[:, h, 2, bass.ds(t, 1)], Dt[:, k % 4, h, :],
                            ALU.mult, ALU.add).then_inc(s["s_U"], 1)
                    for h in range(2):
                        v.wait_ge(s["s_U"], 2 * t + h + 1)
                        if not (warm and k < 4):
                            v.wait_ge(s["s_yt"], 2 * (t - 3) + h - 1)
                        nc.vector.tensor_scalar(H[:, k % 4, h, :], U[:, h, :], 10.0, -10.0, ALU.min, ALU.max).then_inc(s["s_H"], 1)
            for nb in range(4):
                blk(nb, nb == 0)
            with v.Fori(1, NBLK // 4) as it:
                for j in range(4):
                    blk(it * 4 + j, False)

        @block.scalar
        def _(act):
            def a_(o, i, f, bias=0.0, scale=1.0, **k):
                return nc.scalar.activation(o, i, f, bias=bias, scale=scale, **k)

            act.wait_ge(s["s_qn"], 1)
            a_(qexp[:], qneg[:], ACT.Exp).then_inc(s["s_qe"], 1)
            act.wait_ge(s["s_cbe"], 2)

            def rows(n):
                act.wait_ge(s["s_row"], n + 1)
                act.wait_ge(s["s_r"], n)
                a_(vrow[:], bank[1][:], ACT.Identity, bias=cb[:, bass.ds(n, 1)]).then_inc(s["s_v"], 1)

            def slot(n, g, static, more=True, ahead=True):
                if more:
                    if static and n < NG:
                        act.wait_ge(s["s_mask"], (TYPES + 1) * (n + 1))
                    act.wait_ge(s["s_leak"], n)
                    a_(ES[:], BASE[:, GC[g]], ACT.Copy).then_inc(s["s_es"], 1)
                if not (static and n == 0):
                    act.wait_ge(s["s_pt"], n)
                    if not (static and n == 1):
                        act.wait_ge(s["s_ms"], n - 1)
                    a_(PTs[:], bank[7][:], ACT.Copy).then_inc(s["s_ptc"], 1)
                if more:
                    if ahead:
                        rows(n + 1)
                    act.wait_ge(s["s_max"], n + 1)
                    act.wait_ge(s["s_rcp"], n)
                    for b in range(GB):
                        cs = slice(b * S, (b + 1) * S)
                        a_(Pr[:, cs], E[:, cs], ACT.Exp, bias=nmax[:, b:b + 1], accum_out=sums[:, b:b + 1]).then_inc(s["s_exp"], 1)

            rows(0)
            for g in range(NG):
                slot(g, g, True)
            with act.Fori(1, T_ITER - 1) as t:
                for g in range(NG):
                    slot(t * NG + g, g, False)
            for g in range(NG):
                slot((T_ITER - 1) * NG + g, g, True, ahead=g < NG - 1)
            slot(T_ITER * NG, 0, True, more=False)

            def gates(g):
                for c in range(OC):
                    act.wait_ge(s["s_in"], 4 * g + 2 + c + 1)
                    a_(grp(GATE[:, c], g), bank[(3, 6)[c]][:], ACT.Silu).then_inc(s["s_gate"], 1)

            def activate(g):
                for c in range(OC):
                    if g:
                        act.wait_ge(s["s_tr"], g)
                    if c == 0:
                        act.wait_ge(s["s_conv"], TAPS * (g + 1))
                        a_(XS[:, c, :], cv, ACT.Silu).then_inc(s["s_xs"], 1)
                    else:
                        act.wait_ge(s["s_convp"], g + 1)
                        a_(XS[:, c, :], bank[2][:], ACT.Silu, bias=w("bconv", 1, 2)).then_inc(s["s_xs"], 1)
                a_(warm_in[:], eps[:], ACT.Sqrt).then_inc(s["s_warm"], 1)

            def deviation(g):
                act.wait_ge(s["s_mv"], GB * (g + 1))
                act.wait_ge(s["s_rs"], g)
                a_(sd[:], mv[:, :, 1], ACT.Sqrt, bias=eps[:]).then_inc(s["s_sd"], 1)

            def squares(g):
                act.wait_ge(s["s_xn"], g + 1)
                for b in range(GB):
                    at = g * GB + b
                    junk = XP[:, 1, at, :] if g < NG - 1 else cv[:, (b % 2) * DI:(b % 2 + 1) * DI]
                    if g == NG - 1 and b > 1:
                        act.wait_ge(s["s_sq"], GB * g + b - 1)
                    a_(junk, XN[g % 2][:, b, :], ACT.Square, accum_out=ssq[:, at:at + 1]).then_inc(s["s_sq"], 1)

            def turned(g):
                for c in range(OC):
                    act.wait_ge(s["s_tb"], 2 * g + c + 1)
                    a_(grp(XNT[:, c], g), bank[4 + c][:], ACT.Copy).then_inc(s["s_xnt"], 1)

            def first_part(g):
                act.wait_ge(s["s_xn"], g + 1)
                a_(XP[:, 0, g * GB:(g + 1) * GB, :], XN[g % 2][:], ACT.Copy).then_inc(s["s_q1"], 1)

            def second_part(g):
                act.wait_ge(s["s_rr"], g + 1)
                act.wait_ge(s["s_sq"], GB * (g + 1))
                a_(XP[:, 1, g * GB:(g + 1) * GB, :], RR[:], ACT.Copy).then_inc(s["s_q2"], 1)

            def projected(g):
                act.wait_ge(s["s_pj"], g + 1)
                a_(PR[:, GC[g]], bank[0][0:48, :], ACT.Copy).then_inc(s["s_pje"], 1)

            def skip(g):
                act.wait_ge(s["s_xnt"], OC * (g + 1))
                for c in range(OC):
                    a_(grp(XNT[:, c], g), grp(XNT[:, c], g), ACT.Copy, scale=w("dskip", c, c + 1)).then_inc(s["s_sk"], 1)

            act.wait_ge(s["s_eps"], 1)
            gates(0)
            activate(0)
            for g in range(NG):
                deviation(g)
                if g:
                    second_part(g - 1)
                    projected(g - 1)
                if g + 1 < NG:
                    first_part(g)
                    turned(g)
                    gates(g + 1)
                    activate(g + 1)
                    squares(g)
                if g:
                    skip(g - 1)
            turned(NG - 1)
            squares(NG - 1)
            projected(NG - 1)
            proj_out(act, NG - 1)
            act.wait_ge(s["s_sq"], GB * NG)
            a_(nrm[:], ssq[:], ACT.Sqrt).then_inc(s["s_nr"], 1)

            a_(nA[:], w("alog"), ACT.Tanh).then_inc(s["s_nA"], 1)
            act.wait_ge(s["s_scr"], 16 * 3 * NG)
            for k in (2, 0, 1):
                act.dma_start(ABC[:, :, k, :], scr[k].rearrange("(h b) s t -> (b s) h t", h=2)).then_inc(s["s_abc"], 16)
            skip(NG - 1)
            act.wait_ge(s["s_abc"], 16 * 3)
            a_(ABC[:, :, 2, :], ABC[:, :, 2, :], ACT.Tanh, bias=w("bdt")).then_inc(s["s_th"], 1)
            act.wait_ge(s["s_B"], 1)

            def blk(nb, j, tail, warm):
                t0 = nb * TB
                for k in range(TB):
                    t = t0 + k
                    act.wait_ge(s["s_X"], t + 1)
                    if not (warm and k < 4):
                        act.wait_ge(s["s_U"], 2 * (t - 3))
                    for h in range(2):
                        a_(Dt[:, k % 4, h, :], bank[k % 2][:, h * DI:(h + 1) * DI], ACT.Copy,
                           scale=ABC[:, h, 0, bass.ds(t, 1)]).then_inc(s["s_D"], 1)
                    if tail and k == 0 and not (isinstance(nb, int) and nb == 1):
                        copy_out(nb - 2)
                    if tail and k == 1:
                        copy_y(nb - 1, 1 - j)
                    if tail and k == 4:
                        copy_z(nb - 1)

            def copy_y(nb, j):
                for h in range(2):
                    act.wait_ge(s["s_yt"], 2 * (nb + 1) * TB)
                    if not (isinstance(nb, int) and nb == 0):
                        act.wait_ge(s["s_yT"], nb)
                    yb = bank[2 + 2 * j + h][0:TB * HB, 0:DI]
                    a_(YS[0:TB * HB, h, :], yb, ACT.Copy).then_inc(s["s_ys"], 1)

            def copy_z(nb):
                act.wait_ge(s["s_yT"], nb + 1)
                if not (isinstance(nb, int) and nb == 0):
                    act.wait_ge(s["s_o"], nb)
                a_(z.rearrange("p c t b -> p (c t b)"), bank[6][:, 0:OC * TB * B], ACT.Copy).then_inc(s["s_zc"], 1)

            def copy_out(nb):
                act.wait_ge(s["s_o"], nb + 1)
                if not (isinstance(nb, int) and nb == 0):
                    act.wait_ge(s["s_oe"], nb)
                a_(ob[:], bank[7][:, 0:TB * B], ACT.Copy).then_inc(s["s_ob"], 1)

            blk(0, 0, False, True)
            blk(1, 1, True, False)
            blk(2, 0, True, False)
            blk(3, 1, True, False)
            with act.Fori(2, NBLK // 2) as it:
                blk(it * 2, 0, True, False)
                blk(it * 2 + 1, 1, True, False)
            copy_out(NBLK - 2)
            copy_y(NBLK - 1, 1)
            copy_z(NBLK - 1)
            copy_out(NBLK - 1)

        @block.gpsimd
        def _(pool):
            cp = nc.gpsimd.tensor_copy
            pool.wait_ge(s["s_zero"], 2)
            pool.wait_ge(s["s_aq"], 2)
            for c in range(3):
                for g in range(NG):
                    cp(arep[:, c, g, 0:48].rearrange("p (a k) -> p a k", k=TYPES),
                       aq[:, c, :].rearrange("p (o k) -> p o k", o=1).broadcast_to((P, 12, TYPES)))
            pool.wait_ge(s["s_ake"], 3)

            def key_cols(t, g):
                src = ak[:, :, bass.ds(t, 1), g * ROWS_OF:(g + 1) * ROWS_OF]
                o = arep[:, :, g, 64:112].rearrange("p c (a n) -> p c a n", n=ROWS_OF)
                return cp(o, src.broadcast_to((P, 3, PARTS, ROWS_OF)))

            for g in range(NG):
                key_cols(0, g).then_inc(s["s_ar"], 1)


            def slot(n, t, g, final):
                if not final:
                    pool.wait_ge(s["s_row"], n + 1)
                    passed(pool, "passed_pool")
                    key_cols(t + 1, g).then_inc(s["s_ar"], 1)
                pool.wait_ge(s["s_rcp"], n + 1)
                p3 = Pr[:].rearrange("p (b t) -> p b t", b=GB)
                nc.gpsimd.tensor_tensor(p3, p3, rsum[:].rearrange("p (b o) -> p b o", o=1).broadcast_to((P, GB, S)),
                                        ALU.mult).then_inc(s["s_sc"], 1)

            for g in range(NG):
                slot(g, 0, g, False)
            with pool.Fori(1, T_ITER - 1) as t:
                for g in range(NG):
                    slot(t * NG + g, t, g, False)
            for g in range(NG):
                slot((T_ITER - 1) * NG + g, T_ITER - 1, g, True)

            def rest(g):
                pool.wait_ge(s["s_q1"], g + 1)
                pool.wait_ge(s["s_q3"], g)
                nc.gpsimd.tensor_tensor(RR[:], XN[g % 2][:], XP[:, 0, g * GB:(g + 1) * GB, :], ALU.subtract).then_inc(s["s_rr"], 1)

            for g in range(NG - 1):
                rest(g)

            pool.wait_ge(s["s_z0"], 1)
            pool.wait_ge(s["s_abc"], 16 * 3)

            def fill(nb, j):
                for h in range(2):
                    o = cmat[:, h, j, :].rearrange("p (k n) -> p k n", k=TB)[:, :, 0:HB]
                    c3 = ABC[:, h, 1, bass.ds(nb * TB, TB)].rearrange("p (t o) -> p t o", o=1).broadcast_to((P, TB, HB))
                    m3 = w("half8").rearrange("p (o b) -> p o b", o=1).broadcast_to((P, TB, HB))
                    nc.gpsimd.tensor_tensor(o, c3, m3, ALU.mult).then_inc(s["s_Z"], 1)

            fill(0, 0)
            fill(1, 1)

            def view(t4, nb):
                return t4[:, :, bass.ds(nb * TB, TB)].rearrange("p b t -> p t b")

            def gate(nb):
                pool.wait_ge(s["s_zc"], nb + 1)
                for c in range(OC):
                    nc.gpsimd.tensor_tensor(z[:, c], z[:, c], view(XNT[:, c], nb), ALU.add).then_inc(s["s_zz"], 1)
                for c in range(OC):
                    pool.wait_ge(s["s_zz"], OC * nb + c + 1)
                    x = nc.gpsimd.tensor_tensor(z[:, c], z[:, c], view(GATE[:, c], nb), ALU.mult)
                x.then_inc(s["s_zg"], 1)

            def result(nb):
                pool.wait_ge(s["s_ob"], nb + 1)
                nc.gpsimd.tensor_tensor(OUT[:, bass.ds(nb * TB, TB), :], view(X1, nb),
                                        ob[:].rearrange("p (t b) -> p t b", b=B), ALU.add).then_inc(s["s_oe"], 1)

            pool.wait_ge(s["s_sk"], OC * NG)
            for nb in range(2):
                pool.wait_ge(s["s_yt"], 2 * (nb + 1) * TB)
                fill(nb + 2, nb)
                if nb:
                    result(nb - 1)
                gate(nb)
            with pool.Fori(1, NBLK // 2 - 1) as it:
                for j in range(2):
                    nb = it * 2 + j
                    pool.wait_ge(s["s_yt"], 2 * (nb + 1) * TB)
                    fill(nb + 2, j)
                    result(nb - 1)
                    gate(nb)
            for nb in range(NBLK - 2, NBLK):
                result(nb - 1)
                gate(nb)
            result(NBLK - 1)


def _sel_constants():
    import numpy as np
    one = 0x3F80
    sel = np.zeros((P, 2, ROWS_OF, P), np.uint16)
    for p in range(P):
        if p % 64 < PARTS * ROWS_OF:
            sel[p, p // 64, p % 64 % ROWS_OF, :] = one
    spread = np.zeros((PARTS * B, 2, P), np.uint16)
    for p in range(PARTS * B):
        b = p // (PARTS * GB) * GB + p % GB
        spread[p, b // HB, (b % HB) * NST:(b % HB + 1) * NST] = one
    return sel.reshape(P, -1), spread.reshape(PARTS * B, -1)


def kernel(**inputs):
    import numpy as np
    import concourse.bacc as bacc
    from concourse.bass_utils import run_bass_kernel_spmd

    i = {k: np.asarray(v) for k, v in inputs.items()}
    L0 = {k[8:]: v for k, v in i.items() if k.startswith("L0_cond_")}
    L1 = {k[8:]: v for k, v in i.items() if k.startswith("L1_cond_")}

    def chunks(a):
        return a.reshape(-1, P, a.shape[-1]).transpose(1, 0, 2).reshape(P, -1)

    part = np.arange(P) % 64 // ROWS_OF
    col = lambda a: a.reshape(-1, 1)
    f = {
        "ident": np.eye(P, dtype=np.float32), "wqin": L0["w_qin"].T,
        "wqt": i["fside_BxSxS_0"][:T_ITER].transpose(2, 0, 1).reshape(P, -1),
        "wpl": L0["w_pl"].T, "wpc": L0["w_pc"].T, "wq": L0["w_q"], "wk": L0["w_k"],
        "wv": chunks(L0["w_v"].T), "wpk": L0["w_pk"].T, "wpv": L0["w_pv"].T,
        "wmu": chunks(L0["w_mu"].T), "wcb": chunks(L0["w_cb"].T), "win": L1["W_in"].T,
        "wxp": chunks(L1["W_xproj"].T[:, 0:32]), "wout": chunks(L1["W_out"].T),
        "cond": chunks(i["cond_2048"].T), "qenc": i["fside_BxS_0"].T,
        "bqin": col(L0["b_qin"]), "bqt": i["mask_BxS_ff0"][:T_ITER].T, "bpl": col(L0["b_pl"]),
        "bpc": col(L0["b_pc"]), "bq": col(L0["b_q"]), "bk": col(L0["b_k"]), "bv": col(L0["b_v"]),
        "bpk": col(L0["b_pk"]), "bpv": col(L0["b_pv"]), "bmu": col(L0["b_mu"]), "bcb": col(L0["b_cb"]),
        "init": L0["init_mem"].T, "conv": chunks(L1["W_conv"][:, 0, :]), "bconv": chunks(col(L1["b_conv"])),
        "dskip": chunks(col(L1["D"])),
        "bdt": col(np.tile(L1["b_dt"], HB)), "alog": col(np.tile(L1["A_log"], HB)),
        "nm12": col(np.where(part >= 1, -1.0, 0.0).astype(np.float32)),
        "nm3": col(np.where(part >= 2, -1.0, 0.0).astype(np.float32)),
        "half8": np.repeat(np.eye(HB, dtype=np.float32), NST, axis=0),
    }
    w128 = np.concatenate([f[n] for n, _ in COLS], axis=1)
    w16 = np.concatenate([L1["W_xproj"][32:48], L1["W_dt"].T], axis=1)
    sel, spread = _sel_constants()
    arrays = {
        "xT": i["x"].transpose(2, 0, 1).reshape(P, TOK), "adj": i["itok_BxSxS_0_4"].transpose(1, 0, 2).reshape(P, TOK),
        "w128": w128, "w16": w16, "mask": i["mask_BxS_ff1"].reshape(1, TOK),
        "rows": np.concatenate([L1["ln_g"], L1["ln_b"]]).reshape(1, 2 * DI), "sel": sel, "spread": spread,
    }
    arrays = {k: np.ascontiguousarray(v) for k, v in arrays.items()}
    nc = bacc.Bacc("TRN2", target_bir_lowering=False, num_devices=1)
    args = [nc.dram_tensor(k, a.shape, mybir.dt.from_np(a.dtype), kind="ExternalInput").ap() for k, a in arrays.items()]
    out = nc.dram_tensor("outT", (P, TOK), F32, kind="ExternalOutput").ap()
    build_program(nc, *args, out)
    r = run_bass_kernel_spmd(nc, [arrays], core_ids=[0])
    y = np.asarray(r.results[0]["outT"])
    return np.ascontiguousarray(y.reshape(D, S, B).transpose(2, 1, 0))
```

```python
from contextlib import ExitStack

import concourse.bass as bass
from concourse import mybir

F32 = mybir.dt.float32
BF16 = mybir.dt.bfloat16
I32 = mybir.dt.int32
U8 = mybir.dt.uint8
U16 = mybir.dt.uint16
ALU = mybir.AluOpType
ACT = mybir.ActivationFunctionType
AX = mybir.AxisListType

P = 128
B, S, D = 16, 128, 128
TOK = B * S
T_ITER, TYPES = 4, 4
NG, GB = 4, 4
GT = GB * S
OC = 2
DI = OC * P
NST = 16
HB = B // 2
TB = 8
NBLK = S // TB
FIRST = 4 * TB
OUT_PARTS = [(0, 8), (8, 12), (12, 15), (15, 16)]
TAPS = 4
PARTS = 3
MASKED = -9000000000000000.0
ALPHA = 0.2

COLS = [("wqin", D), ("wqt", T_ITER * D), ("qenc", B), ("cond", OC * B),
        ("bqin", 1), ("bqt", T_ITER), ("bpl", 1), ("bpc", 1), ("bq", 1), ("bk", 1), ("bv", 1),
        ("bpk", 1), ("bpv", 1), ("bmu", 1), ("bcb", 1), ("init", 1), ("conv", OC * TAPS),
        ("bconv", OC), ("dskip", OC), ("bdt", 1), ("alog", 1), ("nm12", 1), ("nm3", 1), ("half8", HB),
        ("wpl", D), ("wpk", D), ("wpv", D), ("wq", 3 * D), ("wv", 3 * D), ("wk", 3 * D), ("wpc", D),
        ("ident", P), ("wmu", 2 * D), ("wmun", 2 * D), ("wcb", 2 * D), ("win", 2 * DI), ("wxp", OC * 32), ("wout", OC * D)]
COLS16 = [("wxdt", DI), ("wdt", NST)]
ROWS_OF = GB * TYPES


def places(cols):
    at, out = 0, {}
    for name, n in cols:
        out[name] = (at, at + n)
        at += n
    return out, at


AT, WIDE = places(COLS)
W_PARTS = [(0, AT["wpl"][0]), (AT["wpl"][0], AT["wq"][0]), (AT["wq"][0], AT["ident"][0]), (AT["ident"][0], WIDE)]
AT16, WIDE16 = places(COLS16)


def build_program(nc, xT, adj, w128, w16, mask, rows, sel, spread, out):
    with ExitStack() as ctx:
        def sb(name, shape, dt=F32):
            return ctx.enter_context(nc.sbuf_tensor(name, shape, dt))

        def sem(name):
            return ctx.enter_context(nc.semaphore(name))

        bank = [ctx.enter_context(nc.psum_tensor(f"bank{i}", [P, 512], F32)) for i in range(8)]

        W = sb("W", [P, WIDE])
        W16 = sb("W16", [NST, WIDE16])
        XT = sb("XT", [P, B, S])
        arena = sb("arena", [P, 16384])
        XC = arena[:, 0:2048].rearrange("p (b t) -> p b t", b=B)
        PL = arena[:, 2048:4096].rearrange("p (b t) -> p b t", b=B)
        VL = arena[:, 4096:6144].rearrange("p (b d) -> p b d", b=B)
        BASE = arena[:, 6144:8192]
        MB = arena[:, 8192:10240].rearrange("p (b t) -> p b t", b=B)
        MK = arena[:, 10240:12288].bitcast(U8).rearrange("p (k n) -> p k n", k=TYPES)
        ADJ = arena[:, 12288:14336].bitcast(I32)
        XR = arena[:, :].bitcast(BF16).rearrange("p (t c) -> p t c", c=DI)

        spread_sb = sb("spread_sb", [PARTS * B, 2, P], BF16)
        rows_sb = sb("rows_sb", [P, 2, DI])

        qb = sb("qb", [P, B])
        qneg = sb("qneg", [P, B])
        qexp = sb("qexp", [P, B])
        cmd = sb("cmd", [P, T_ITER, B])
        pk = sb("pk", [P, T_ITER, B])
        pv = sb("pv", [P, T_ITER, B])
        gk = sb("gk", [P, T_ITER, B, TYPES])
        aq = sb("aq", [P, 3, TYPES])
        cb = sb("cb", [P, T_ITER * NG])

        work = sb("work", [P, 6656])
        PP, vrow, rrow, ES, E, Pr, PTs, MS = [work[:, i * GT:(i + 1) * GT] for i in range(8)]
        Vs = work[:, 4096:5120].rearrange("p (q b d) -> p q b d", q=2, b=GB)
        arep = work[:, 5120:6656].rearrange("p (c g n) -> p c g n", c=3, g=NG)
        XP = work[:, 0:6144].bitcast(BF16).rearrange("p (q b c) -> p q b c", q=PARTS, b=B)
        krep = work[:, 0:768].rearrange("p (n c) -> p n c", n=T_ITER * NG)
        qrep = work[:, 768:816]
        diag = work[:, 6144:6656].rearrange("p (k n) -> p k n", k=TAPS)
        p1 = sb("p1", [P, GT], BF16)
        p2 = sb("p2", [P, GT], BF16)
        Y = sb("Y", [P, GT], BF16)
        nmax = sb("nmax", [P, GB])
        sums = sb("sums", [P, GB])
        rsum = sb("rsum", [P, GB])

        X1 = sb("X1", [P, B, S])
        GATE = sb("GATE", [P, OC, B, S])
        XNT = sb("XNT", [P, OC, B, S])
        PAD = TAPS - 1
        xpad = sb("xpad", [P, OC, GB, PAD + S])
        st = sb("st", [P, GB, 6])
        mv = sb("mv", [P, GB, 2])
        sd = sb("sd", [P, GB])
        warm_in = sb("warm_in", [P, 1])
        rstd = sb("rstd", [P, GB])
        ssq = sb("ssq", [P, B])
        nrm = sb("nrm", [P, B])
        nf = gk[:].rearrange("p t b k -> p (t b k)").rearrange("p (b s) -> p b s", b=B)
        wx = sb("wx", [P, OC, 48])
        eps = sb("eps", [P, 1])
        ABC = sb("ABC", [P, 2, 3, S])
        work2 = sb("work2", [P, 6144])
        ak = work2[:, 0:768].rearrange("p (c t n) -> p c t n", c=3, t=T_ITER)
        sel_sb = work2[:, 1024:3072].bitcast(BF16).rearrange("p (q a b) -> p q a b", q=2, a=ROWS_OF)
        cv = work2[:, 0:512]
        XS = work2[:, 1024:2048].rearrange("p (c n) -> p c n", c=OC)
        RR = work2[:, 2048:3072].rearrange("p (b c) -> p b c", b=GB)
        XN = [work2[:, 3072:4096].rearrange("p (b c) -> p b c", b=GB), sb("XN1", [P, GB, DI])]
        PR = work2[0:48, 4096:6144]
        Dt = work2[:, 0:2048].rearrange("p (q h c) -> p q h c", q=4, h=2)
        H = work2[:, 2048:4096].rearrange("p (q h c) -> p q h c", q=4, h=2)
        U = work2[:, 4096:4608].rearrange("p (h c) -> p h c", h=2)
        YS = work2[:, 4608:5120].rearrange("p (h c) -> p h c", h=2)
        z = work2[:, 5120:5120 + OC * TB * B].rearrange("p (c t b) -> p c t b", c=OC, t=TB)
        cmat = sb("cmat", [P, 2, 2, TB * (TB + 1) * HB])
        nA = sb("nA", [P, 1])
        ablk = sb("ablk", [P, 2, 2, TB])
        ob = work[:, 0:TB * B]
        OUT = XT[:].rearrange("p b t -> p (b t)").rearrange("p (t b) -> p t b", b=B)

        def w(name, a=0, b=None):
            lo, hi = AT[name]
            return W[:, lo + a:(lo + b if b is not None else hi)]

        scrx = nc.dram_tensor("rows_scratch", (PARTS * B, S, DI), BF16, kind="Internal").ap()
        scr = nc.dram_tensor("proj_scratch", (3, B, NST, S), F32, kind="Internal").ap()

        names = []
        names += """
            x_first_loaded x_loaded mask_first_loaded mask_loaded adj_loaded sel_loaded w0_loaded w1_loaded
            w2_loaded w3_loaded w16_loaded spread_and_ln_loaded zeroed pad_zeroed cmat_zeroed eps_ready
            question_product question_negative question_exp question_positive q_base_ready cmd_product cmd_ready
            pk_pv_product pk_pv_ready key_edge_ready key_fold_product key_fold_ready query_fold
            bias_weights_ready row_bias_product row_bias_ready row_weights_ready pl_product pl_ready
            v_share_product v_share_first_kept v_share_kept dt_fold_product xproj_weights_ready masks_ready
            first_context_ready
            """.split()
        names += """
            pc_product joint_ready rows_product rows_ready part1_ready rest1_ready part2_ready row_parts_ready
            v_product v_ready scores_product base_copied scores_chosen leaky_ready max_ready exp_ready
            inverse_ready probs_ready probs_turned probs_turned_copied message_product message_ready
            context_product context_ready
            """.split()
        names += """
            win_product widened_ready gate_ready diag_ready conv0_step conv1_product silu_ready sqrt_table_in
            silu_turned stats_ready moments_ready centred_ready deviation_ready inverse_deviation_ready xn_ready
            xn_part1_ready xn_rest_ready xn_part2_ready xn_part3_ready xn_parts_stored xn_turned xnt_ready
            squares_summed norm_ready norm_factor_ready norm_rows_product proj_product proj_ready proj_stored
            proj_last_stored abc_loaded skip_done rows_loaded rows_rest_loaded tanh_dt_ready tanh_alog_ready
            minus_a_ready b_rows_ready a_or_h_ready
            """.split()
        names += """
            c_filled a_of_block x_spread d_ready u_ready h_ready y_step y_copied y_turned z_copied z_summed
            z_gated out_product out_copied out_ready out_stored
            """.split()
        names += """
            passed_dve passed_pe passed_pool
            """.split()
        s = {n: sem(n) for n in names}

        block = ctx.enter_context(nc.Block())
        GC = [slice(g * GT, (g + 1) * GT) for g in range(NG)]

        def grp(t3, g):
            return t3[:, g * GB:(g + 1) * GB, :].rearrange("p b t -> p (b t)")

        def passed(eng, signal):
            eng.sem_inc(s[signal], 1)

        def proj_out(eng, g):
            eng.wait_ge(s["proj_ready"], g + 1)
            for k in range(3):
                eng.dma_start(scr[k, g * GB:(g + 1) * GB].rearrange("b s t -> s b t"),
                              PR[k * NST:(k + 1) * NST, GC[g]].rearrange("s (b t) -> s b t", b=GB)
                              ).then_inc(s["proj_stored" if g < NG - 1 else "proj_last_stored"], 16)

        def rows_abc(eng, b0, b1):
            h, r0 = b0 // HB, b0 % HB * NST
            eng.dma_start(ABC[r0:r0 + (b1 - b0) * NST, h, :, :],
                          scr[:, b0:b1].rearrange("k b s t -> (b s) k t")).then_inc(s["abc_loaded"], 16)

        def view(t4, nb):
            return t4[:, :, bass.ds(nb * TB, TB)].rearrange("p b t -> p t b")

        def gate(eng, e, nb):
            eng.wait_ge(s["z_copied"], nb + 1)
            for c in range(OC):
                e.tensor_tensor(z[:, c], z[:, c], view(XNT[:, c], nb), ALU.add).then_inc(s["z_summed"], 1)
            for c in range(OC):
                eng.wait_ge(s["z_summed"], OC * nb + c + 1)
                x = e.tensor_tensor(z[:, c], z[:, c], view(GATE[:, c], nb), ALU.mult)
            x.then_inc(s["z_gated"], 1)

        def result(eng, e, nb):
            eng.wait_ge(s["out_copied"], nb + 1)
            e.tensor_tensor(OUT[:, bass.ds(nb * TB, TB), :], view(X1, nb),
                            ob.rearrange("p (t b) -> p t b", b=B), ALU.add).then_inc(s["out_ready"], 1)

        @block.sync
        def _(sp):
            def load_w(i):
                a, b = W_PARTS[i]
                sp.dma_start(W[:, a:b], w128[:, a:b]).then_inc(s[f"w{i}_loaded"], 16)

            load_w(0)
            load_w(1)
            XTf, MBf = XT[:].rearrange("p b t -> p (b t)"), MB.rearrange("p b t -> p (b t)")
            sp.dma_start(XTf[:, 0:GT], xT[:, 0:GT]).then_inc(s["x_first_loaded"], 16)
            load_w(2)
            sp.dma_start(MBf[:, 0:GT], mask[:, 0:GT].broadcast_to((P, GT))).then_inc(s["mask_first_loaded"], 16)
            sp.dma_start(XTf[:, GT:], xT[:, GT:]).then_inc(s["x_loaded"], 16)
            sp.dma_start(sel_sb.rearrange("p q a b -> p (q a b)").bitcast(U16), sel).then_inc(s["sel_loaded"], 16)
            sp.dma_start(ADJ, adj).then_inc(s["adj_loaded"], 16)
            sp.dma_start(MBf[:, GT:], mask[:, GT:].broadcast_to((P, TOK - GT))).then_inc(s["mask_loaded"], 16)
            sp.dma_start(W16[:], w16).then_inc(s["w16_loaded"], 16)
            load_w(3)
            sp.dma_start(spread_sb[:].rearrange("p a b -> p (a b)").bitcast(U16), spread).then_inc(s["spread_and_ln_loaded"], 16)
            sp.dma_start(rows_sb[:].rearrange("p a b -> p (a b)"), rows.broadcast_to((P, 2 * DI))).then_inc(s["spread_and_ln_loaded"], 16)
            def rows_out(g, q):
                sp.wait_ge(s[("xn_part1_ready", "xn_part2_ready", "xn_part3_ready")[q]], g + 1)
                r0 = (g * PARTS + q) * GB
                sp.dma_start(scrx[r0:r0 + GB, :, :].rearrange("r t c -> t r c"),
                             XP[:, q, g * GB:(g + 1) * GB, :]).then_inc(s["xn_parts_stored"], 16)

            def rows_in(g0, g1, steps, done):
                r = slice(g0 * PARTS * GB, g1 * PARTS * GB)
                sp.dma_start(XR[r, steps, :], scrx[r, steps, :]).then_inc(s[done], 16)

            for g in range(NG - 1):
                if g == NG - 2:
                    sp.wait_ge(s["context_product"], T_ITER * NG)
                    sp.wait_ge(s["xn_parts_stored"], 16 * PARTS * g)
                    rows_in(0, g, slice(0, S), "rows_loaded")
                for q in range(PARTS):
                    rows_out(g, q)
                proj_out(sp, g)
            rows_out(NG - 1, 0)
            sp.wait_ge(s["proj_stored"], 16 * 3 * (NG - 1))
            rows_abc(sp, 0, HB)
            rows_abc(sp, HB, HB + GB)
            rows_out(NG - 1, 1)
            rows_out(NG - 1, 2)
            sp.wait_ge(s["xn_parts_stored"], 16 * PARTS * NG)
            rows_in(NG - 2, NG, slice(0, FIRST), "rows_loaded")
            sp.wait_ge(s["abc_loaded"], 16 * 3)
            rows_in(NG - 2, NG, slice(FIRST, S), "rows_rest_loaded")
            for b0, b1 in OUT_PARTS:
                sp.wait_ge(s["out_ready"], b1)
                sp.dma_start(out[:, b0 * TB * B:b1 * TB * B],
                             OUT[:, b0 * TB:b1 * TB, :].rearrange("p t b -> p (t b)")).then_inc(s["out_stored"], 16)
            sp.wait_ge(s["out_stored"], 16 * len(OUT_PARTS))

        @block.tensor
        def _(pe):
            def mm(o, a, b, start=True, stop=True):
                return nc.tensor.matmul(o, a, b, start=start, stop=stop)

            ident = w("ident")
            pe.wait_ge(s["w0_loaded"], 16)
            mm(bank[0][:, 0:B], w("wqin"), w("qenc")).then_inc(s["question_product"], 1)
            pe.wait_ge(s["q_base_ready"], 1)
            for t in range(T_ITER):
                x = mm(bank[1][:, t * B:(t + 1) * B], w("wqt", t * D, (t + 1) * D), qb[:])
            x.then_inc(s["cmd_product"], 1)
            pe.wait_ge(s["w1_loaded"], 16)
            pe.wait_ge(s["cmd_ready"], 1)
            cf = cmd[:].rearrange("p t b -> p (t b)")
            mm(bank[0][:, 0:64], w("wpk"), cf)
            mm(bank[0][:, 64:128], w("wpv"), cf).then_inc(s["pk_pv_product"], 1)
            pe.wait_ge(s["x_first_loaded"], 16)
            mm(bank[3][:], w("wpl"), grp(XT, 0)).then_inc(s["pl_product"], 1)
            pe.wait_ge(s["w2_loaded"], 16)
            for c in range(3):
                x = mm(bank[2][:, c * TYPES:(c + 1) * TYPES], w("wq", c * D, (c + 1) * D), w("cond", 0, TYPES))
            x.then_inc(s["query_fold"], 1)
            pe.wait_ge(s["key_edge_ready"], 1)
            gkf = gk[:].rearrange("p t b k -> p (t b k)")
            for c in range(3):
                if c == 2:
                    pe.wait_ge(s["pk_pv_ready"], 2)
                mm(bank[[1, 7, 0][c]][:, 0:256], w("wk", c * D, (c + 1) * D), gkf).then_inc(s["key_fold_product"], 1)
            pe.wait_ge(s["query_fold"], 2)
            pe.wait_ge(s["bias_weights_ready"], 2)
            mm(bank[2][0:48, 16:17], qrep, w("bq"))
            for n in range(T_ITER * NG):
                x = mm(bank[2][64:112, 17 + n:18 + n], krep[:, n, :], w("bk"))
            x.then_inc(s["row_bias_product"], 1)

            def share_of_v(g):
                pe.wait_ge(s["pl_ready"], g + 1)
                for b in range(GB):
                    x = mm(bank[3 + g][:, b * D:(b + 1) * D], XT[:, g * GB + b, :], w("wv", 0, D))
                x.then_inc(s["v_share_product"], 1)

            share_of_v(0)
            pe.wait_ge(s["row_bias_ready"], 2)
            pe.wait_ge(s["key_fold_ready"], 3)
            pe.wait_ge(s["first_context_ready"], 1)

            def context(n, g):
                mm(bank[2][:], w("wpc"), grp(XC, g)).then_inc(s["pc_product"], 1)

            def score_rows(n, g):
                pe.wait_ge(s["row_weights_ready"], n + 1)
                mm(bank[1][:], arep[:, 0, g, :], grp(XT, g), True, False)
                mm(bank[1][:], arep[:, 1, g, :], grp(XC, g), False, False)
                pe.wait_ge(s["joint_ready"], n + 1)
                mm(bank[1][:], arep[:, 2, g, :], PP[:], False, True).then_inc(s["rows_product"], 1)

            def turn_probs(n, static):
                pe.wait_ge(s["probs_ready"], n + 1)
                if not (static and n == 0):
                    pe.wait_ge(s["context_ready"], n)
                else:
                    pe.wait_ge(s["xproj_weights_ready"], 3)
                for b in range(GB):
                    x = nc.tensor.transpose(bank[7][:, b * S:(b + 1) * S], Pr[:, b * S:(b + 1) * S], ident)
                x.then_inc(s["probs_turned"], 1)

            def message(n, g, static):
                pe.wait_ge(s["probs_turned_copied"], n + 1)
                if not (static and n == 0):
                    pe.wait_ge(s["message_ready"], n)
                for b in range(GB):
                    x = mm(bank[0][:, b * S:(b + 1) * S], Vs[:, g % 2, b, :], PTs[:, b * S:(b + 1) * S])
                x.then_inc(s["message_product"], 1)

            def next_context(n, g, final=False):
                pe.wait_ge(s["message_ready"], n + 1)
                if final:
                    mm(bank[7][:], w("wcb", 0, D), grp(XT, g), True, False)
                    mm(bank[7][:], w("wmun", 0, D), grp(XC, g), False, False)
                    mm(bank[7][:], w("wmun", D, 2 * D), MS[:], False, True).then_inc(s["context_product"], 1)
                    return
                mm(bank[7][:], w("wmu", 0, D), grp(XC, g), True, False)
                mm(bank[7][:], w("wmu", D, 2 * D), MS[:], False, True).then_inc(s["context_product"], 1)

            WIN = [bank[1], bank[2], bank[3], bank[6]]

            def widened(g, chunks):
                pe.wait_ge(s["context_ready"], (T_ITER - 1) * NG + g + 1)
                for c in chunks:
                    if g:
                        pe.wait_ge([s["widened_ready"], s["silu_ready"], s["gate_ready"], s["gate_ready"]][c], 2 * g)
                    mm(WIN[c][:], w("win", c * P, (c + 1) * P), grp(X1, g)).then_inc(s["win_product"], 1)

            def slot(n, g, static, ahead=True):
                pg = (g - 1) % NG
                before = not (static and n == 0)

                def scores(k):
                    for b in range(GB):
                        o = bank[3 + k][:, b * S:(b + 1) * S]
                        row = b * TYPES + k
                        mm(o, Y[:, b * S:(b + 1) * S], sel_sb[:, 0, row, :], True, False)
                        x = mm(o, sel_sb[:, 1, row, :], Y[:, b * S:(b + 1) * S], False, True)
                    x.then_inc(s["scores_product"], 1)

                for b in range(GB):
                    o = bank[2][:, b * D:(b + 1) * D]
                    mm(o, XC[:, g * GB + b, :], w("wv", D, 2 * D), True, False)
                    x = mm(o, PP[:, b * S:(b + 1) * S], w("wv", 2 * D, 3 * D), False, True)
                x.then_inc(s["v_product"], 1)
                pe.wait_ge(s["row_parts_ready"], n + 1)
                if before:
                    pe.wait_ge(s["scores_chosen"], n * TYPES)
                else:
                    pe.wait_ge(s["v_share_first_kept"], 1)
                    pe.wait_ge(s["v_share_kept"], NG - 1)
                scores(0)
                scores(1)
                if before:
                    turn_probs(n - 1, static)
                if ahead:
                    pe.wait_ge(s["v_ready"], n + 1)
                    if not (static and n < NG):
                        pe.wait_ge(s["context_ready"], n - 2)
                    elif n == NG - 1:
                        pe.wait_ge(s["context_ready"], 1)
                    else:
                        pe.wait_ge(s["first_context_ready"], n + 2)
                    context(n + 1, (g + 1) % NG)
                else:
                    pe.wait_ge(s["v_ready"], n + 1)
                    widened(0, [0, 1])
                if before:
                    message(n - 1, pg, static)
                scores(2)
                scores(3)
                if ahead:
                    score_rows(n + 1, (g + 1) % NG)
                if before:
                    next_context(n - 1, pg, static and n - 1 >= (T_ITER - 1) * NG)

            context(0, 0)
            score_rows(0, 0)
            pe.wait_ge(s["x_loaded"], 16)
            for g in range(1, NG):
                mm(bank[3 + g][:], w("wpl"), grp(XT, g)).then_inc(s["pl_product"], 1)
            for g in range(1, NG):
                share_of_v(g)
            pe.wait_ge(s["w16_loaded"], 16)
            for c in range(OC):
                mm(bank[7][:, c * NST:(c + 1) * NST], W16[:, c * P:(c + 1) * P], W16[:, AT16["wdt"][0]:AT16["wdt"][1]])
            pe.wait_ge(s["w3_loaded"], 16)
            for c in range(2):
                mm(bank[7][:, (1 + c) * P:(2 + c) * P], w("wmun", c * D, (c + 1) * D), w("wcb", D, 2 * D))
            mm(bank[7][:, 3 * P:3 * P + 1], w("wcb", D, 2 * D), w("bmu")).then_inc(s["dt_fold_product"], 1)
            pe.wait_ge(s["sel_loaded"], 16)
            pe.wait_ge(s["w3_loaded"], 16)
            pe.wait_ge(s["spread_and_ln_loaded"], 32)
            for g in range(NG):
                slot(g, g, True)
            with pe.Fori(1, T_ITER - 1) as t:
                for g in range(NG):
                    slot(t * NG + g, g, False)
            for g in range(NG):
                slot((T_ITER - 1) * NG + g, g, True, ahead=g < NG - 1)

            def taps(g):
                pe.wait_ge(s["diag_ready"], TAPS)
                pe.wait_ge(s["widened_ready"], 2 * g + 2)
                for k in range(TAPS):
                    x = mm(WIN[1][:], diag[:, k, :], xpad[:, 1, :, k:k + S], k == 0, k == TAPS - 1)
                x.then_inc(s["conv1_product"], 1)

            def turn(g):
                pe.wait_ge(s["silu_ready"], 2 * (g + 1))
                if g:
                    pe.wait_ge(s["xnt_ready"], 2 * g)
                for b in range(GB):
                    for c in range(OC):
                        at = (b * OC + c) * P
                        x = nc.tensor.transpose(bank[4 + at // 512][:, at % 512:at % 512 + P],
                                                XS[:, c, b * S:(b + 1) * S], ident)
                x.then_inc(s["silu_turned"], 1)

            def turn_back(g):
                pe.wait_ge(s["xn_ready"], g + 1)
                for c in range(OC):
                    for b in range(GB):
                        x = nc.tensor.transpose(bank[4 + c][:, b * S:(b + 1) * S], XN[g % 2][:, b, c * P:(c + 1) * P], ident)
                    x.then_inc(s["xn_turned"], 1)

            def project(g):
                pe.wait_ge(s["xnt_ready"], 2 * (g + 1))
                if g:
                    pe.wait_ge(s["proj_ready"], g)
                else:
                    pe.wait_ge(s["xproj_weights_ready"], 4)
                for c in range(OC):
                    x = mm(bank[0][0:48, :], wx[:, c, :], grp(XNT[:, c], g), c == 0, c == OC - 1)
                x.then_inc(s["proj_product"], 1)

            last = T_ITER * NG - 1
            pe.wait_ge(s["scores_chosen"], T_ITER * NG * TYPES)
            widened(0, [2, 3])
            taps(0)
            turn_probs(last, True)
            widened(1, [0])
            message(last, NG - 1, True)
            for g in range(NG):
                turn(g)
                if g + 1 < NG:
                    widened(g + 1, [1, 2, 3])
                if g == 0:
                    next_context(last, NG - 1, True)
                if g == NG - 1:
                    pe.wait_ge(s["moments_ready"], GB * NG)
                if g:
                    project(g - 1)
                if g + 1 < NG:
                    taps(g + 1)
                turn_back(g)
                if g + 2 < NG:
                    widened(g + 2, [0])
            project(NG - 1)

            pe.wait_ge(s["proj_ready"], NG)
            pe.wait_ge(s["norm_factor_ready"], 1)
            for h in range(2):
                x = mm(bank[7][:, h * S:(h + 1) * S], nf[:, h * HB:(h + 1) * HB, :].rearrange("p b s -> p (b s)"), ident)
            x.then_inc(s["norm_rows_product"], 1)

            def spread_x(t, slot_):
                for h in range(2):
                    x = mm(bank[slot_][:, h * DI:(h + 1) * DI], spread_sb[:, h, :],
                           XR[0:PARTS * B, bass.ds(t, 1), :].rearrange("p a c -> p (a c)"))
                x.then_inc(s["x_spread"], 1)

            def blk(nb, j, tail, warm, ahead):
                t0 = nb * TB
                if warm:
                    spread_x(t0, 0)
                    spread_x(t0 + 1, 1)
                pe.wait_ge(s["c_filled"], 2 * (nb + 1))
                for k in range(TB):
                    t = t0 + k
                    if k + 2 < TB or ahead:
                        pe.wait_ge(s["d_ready"], 2 * (t + 1))
                        spread_x(t + 2, k % 2)
                    for h in range(2):
                        pe.wait_ge(s["h_ready"], 2 * t + h + 1)
                        x = mm(bank[2 + 2 * j + h][0:TB * HB, 0:DI], cmat[:, h, j, k * TB * HB:(k + 1) * TB * HB],
                               H[:, k % 4, h, :], k == 0, k == TB - 1)
                        x.then_inc(s["y_step"], 1)
                    if tail and k == 2:
                        tail_a(nb - 1)
                    if tail and k == 6:
                        tail_b(nb - 1)

            def tail_a(nb):
                pe.wait_ge(s["y_copied"], 2 * (nb + 1))
                if not (isinstance(nb, int) and nb == 0):
                    pe.wait_ge(s["z_copied"], nb)
                passed(pe, "passed_pe")
                for c in range(OC):
                    for h in range(2):
                        o = bank[6][:, c * TB * B:(c + 1) * TB * B].rearrange("p (t b) -> p t b", b=B)[:, :, h * HB:(h + 1) * HB]
                        x = nc.tensor.transpose(o, YS[0:TB * HB, h, c * P:(c + 1) * P], ident[0:TB * HB, 0:TB * HB])
                x.then_inc(s["y_turned"], 1)

            def tail_b(nb):
                pe.wait_ge(s["z_gated"], nb + 1)
                if isinstance(nb, int) and nb == 0:
                    pe.wait_ge(s["b_rows_ready"], 1)
                if not (isinstance(nb, int) and nb == 0):
                    pe.wait_ge(s["out_copied"], nb)
                for c in range(OC):
                    x = mm(bank[7][:, 0:TB * B], w("wout", c * D, (c + 1) * D), z[:, c].rearrange("p t b -> p (t b)"),
                           c == 0, c == OC - 1)
                x.then_inc(s["out_product"], 1)

            pe.wait_ge(s["rows_loaded"], 16 * 2)
            blk(0, 0, False, True, True)
            blk(1, 1, True, False, True)
            pe.wait_ge(s["rows_rest_loaded"], 16)
            with pe.Fori(1, NBLK // 2 - 1) as it:
                blk(it * 2, 0, True, False, True)
                blk(it * 2 + 1, 1, True, False, True)
            blk(NBLK - 2, 0, True, False, True)
            blk(NBLK - 1, 1, True, False, False)
            tail_a(NBLK - 1)
            tail_b(NBLK - 1)

        @block.vector
        def _(v):
            def tt(o, a, b, op):
                return nc.vector.tensor_tensor(o, a, b, op)

            def stt(o, a, sc, b, op0, op1):
                return nc.vector.scalar_tensor_tensor(out=o, in0=a, scalar=sc, in1=b, op0=op0, op1=op1)

            nc.vector.memset(cb[:], 0.0).then_inc(s["zeroed"], 1)
            nc.vector.memset(eps[:], 1e-5).then_inc(s["eps_ready"], 1)
            v.wait_ge(s["w0_loaded"], 16)
            v.wait_ge(s["question_product"], 1)
            nc.vector.tensor_scalar(qb[:], bank[0][:, 0:B], w("bqin"), 0.0, ALU.add, ALU.max).then_inc(s["question_positive"], 1)
            nc.vector.tensor_scalar(qneg[:], bank[0][:, 0:B], w("bqin"), 0.0, ALU.add, ALU.min).then_inc(s["question_negative"], 1)
            v.wait_ge(s["question_exp"], 1)
            v.wait_ge(s["question_positive"], 1)
            stt(qb[:], qexp[:], -1.0, qb[:], ALU.add, ALU.add).then_inc(s["q_base_ready"], 1)
            v.wait_ge(s["cmd_product"], 1)
            for t in range(T_ITER):
                x = nc.vector.tensor_scalar(cmd[:, t, :], bank[1][:, t * B:(t + 1) * B], w("bqt", t, t + 1), None, ALU.add)
            x.then_inc(s["cmd_ready"], 1)
            nc.vector.tensor_copy(qrep.rearrange("p (a k) -> p a k", k=TYPES),
                                  w("cond", 0, TYPES).rearrange("p (o k) -> p o k", o=1).broadcast_to((P, 12, TYPES))).then_inc(s["bias_weights_ready"], 1)
            v.wait_ge(s["pk_pv_product"], 1)
            nc.vector.tensor_scalar(pk[:].rearrange("p t b -> p (t b)"), bank[0][:, 0:64], w("bpk"), None, ALU.add).then_inc(s["pk_pv_ready"], 1)
            nc.vector.tensor_scalar(pv[:].rearrange("p t b -> p (t b)"), bank[0][:, 64:128], w("bpv"), None, ALU.add).then_inc(s["pk_pv_ready"], 1)
            v.wait_ge(s["pk_pv_ready"], 2)
            w2 = w("cond", B, B + TYPES)
            tt(gk[:].rearrange("p t b k -> p (t b) k"),
               pk[:].rearrange("p t (b o) -> p (t b) o", o=1).broadcast_to((P, T_ITER * B, TYPES)),
               w2.rearrange("p (o k) -> p o k", o=1).broadcast_to((P, T_ITER * B, TYPES)), ALU.mult).then_inc(s["key_edge_ready"], 1)
            v.wait_ge(s["key_edge_ready"], 1)
            for n in range(0, T_ITER * NG, NG):
                t = n // NG
                x = nc.vector.tensor_copy(krep[:, n:n + NG, :].rearrange("p g (a r) -> p g a r", a=PARTS),
                                          gk[:, t].rearrange("p (g b) k -> p g (b k)", g=NG).rearrange("p g (o r) -> p g o r", o=1)
                                          .broadcast_to((P, NG, PARTS, ROWS_OF)))
            x.then_inc(s["bias_weights_ready"], 1)
            v.wait_ge(s["query_fold"], 1)
            nc.vector.tensor_copy(aq[:].rearrange("p c k -> p (c k)"), bank[2][:, 0:12]).then_inc(s["query_fold"], 1)
            v.wait_ge(s["row_bias_product"], 1)
            v.wait_ge(s["zeroed"], 1)
            nc.vector.tensor_copy(cb[0:48, :], bank[2][0:48, 16:17].broadcast_to((48, T_ITER * NG))).then_inc(s["row_bias_ready"], 1)
            nc.vector.tensor_copy(cb[64:112, :], bank[2][64:112, 17:17 + T_ITER * NG]).then_inc(s["row_bias_ready"], 1)

            def masks(g):
                for k in range(TYPES):
                    nc.vector.tensor_scalar(MK[:, k, GC[g]], ADJ[:, GC[g]], float(k + 1), None, ALU.is_equal).then_inc(s["masks_ready"], 1)
                nc.vector.tensor_scalar(BASE[:, GC[g]], ADJ[:, GC[g]], 0.0, MASKED / ALPHA, ALU.is_le, ALU.mult).then_inc(s["masks_ready"], 1)

            def joint(n, g):
                v.wait_ge(s["pc_product"], n + 1)
                stt(PP[:], bank[2][:], w("bpc"), grp(PL, g), ALU.add, ALU.mult).then_inc(s["joint_ready"], 1)

            def new_context(n, g, final):
                v.wait_ge(s["context_product"], n + 1)
                if final:
                    v.wait_ge(s["xproj_weights_ready"], 3)
                    stt(grp(X1, g), bank[7][:], w("bcb"), grp(XT, g), ALU.add, ALU.add).then_inc(s["context_ready"], 1)
                else:
                    stt(grp(XC, g), bank[7][:], w("bmu"), grp(MB, g), ALU.add, ALU.mult).then_inc(s["context_ready"], 1)

            def rows_rest(n):
                v.wait_ge(s["rows_ready"], n + 1)
                v.wait_ge(s["rest1_ready"], n)
                nc.vector.tensor_copy(p1[:], vrow[:]).then_inc(s["part1_ready"], 1)
                v.wait_ge(s["part1_ready"], n + 1)
                v.wait_ge(s["row_parts_ready"], n)
                stt(rrow[:], p1[:], w("nm12"), vrow[:], ALU.mult, ALU.add).then_inc(s["rest1_ready"], 1)

            def rows_second(n):
                v.wait_ge(s["rest1_ready"], n + 1)
                nc.vector.tensor_copy(p2[:], rrow[:]).then_inc(s["part2_ready"], 1)

            def rows_split(n):
                v.wait_ge(s["part2_ready"], n + 1)
                v.wait_ge(s["scores_product"], n * TYPES)
                stt(Y[:], p2[:], w("nm3"), rrow[:], ALU.mult, ALU.add).then_inc(s["row_parts_ready"], 1)

            def message(n, t, g):
                v.wait_ge(s["message_product"], n + 1)
                stt(MS[:].rearrange("p (b t) -> p b t", b=GB), bank[0][:].rearrange("p (b t) -> p b t", b=GB), w("bv"),
                    pv[:, bass.ds(t, 1), g * GB:(g + 1) * GB].rearrange("p o b -> p b o").broadcast_to((P, GB, S)),
                    ALU.add, ALU.mult).then_inc(s["message_ready"], 1)

            def widen(g):
                for c in range(OC):
                    v.wait_ge(s["win_product"], 4 * g + c + 1)
                    if g:
                        v.wait_ge(s["conv0_step"] if c == 0 else s["conv1_product"], TAPS * g if c == 0 else g)
                    tt(xpad[:, c, :, PAD:], bank[1 + c][:].rearrange("p (b t) -> p b t", b=GB),
                       w("cond", c * B + g * GB, c * B + (g + 1) * GB).rearrange("p (b o) -> p b o", o=1).broadcast_to((P, GB, S)),
                       ALU.add).then_inc(s["widened_ready"], 1)

            def slot(n, t, g, static, ahead=True):
                pg = (g - 1) % NG
                before = not (static and n == 0)

                def choose(k):
                    v.wait_ge(s["scores_product"], n * TYPES + k + 1)
                    v.wait_ge(s["scores_chosen"], n * TYPES + k)
                    passed(v, "passed_dve")
                    nc.vector.copy_predicated(ES[:], MK[:, k, GC[g]], bank[3 + k][:]).then_inc(s["scores_chosen"], 1)

                v.wait_ge(s["v_product"], n + 1)
                tt(Vs[:, g % 2].rearrange("p b d -> p (b d)"), bank[2][:],
                   VL[:, g * GB:(g + 1) * GB, :].rearrange("p b d -> p (b d)"), ALU.add).then_inc(s["v_ready"], 1)
                v.wait_ge(s["base_copied"], n + 1)
                choose(0)
                choose(1)
                if ahead:
                    joint(n + 1, (g + 1) % NG)
                if before:
                    message(n - 1, t if g else t - 1, pg)
                for k in range(2, TYPES):
                    choose(k)
                v.wait_ge(s["scores_chosen"], n * TYPES + TYPES)
                stt(E[:], ES[:], ALPHA, ES[:], ALU.mult, ALU.max).then_inc(s["leaky_ready"], 1)
                v.wait_ge(s["leaky_ready"], n + 1)
                nc.vector.tensor_reduce(nmax[:], E[:].rearrange("p (b t) -> p b t", b=GB), AX.X, ALU.max,
                                        negate=True).then_inc(s["max_ready"], 1)
                if ahead:
                    rows_rest(n + 1)
                    rows_second(n + 1)
                else:
                    v.wait_ge(s["pad_zeroed"], 1)
                    widen(0)
                v.wait_ge(s["exp_ready"], (n + 1) * GB)
                v.wait_ge(s["probs_ready"], n)
                nc.vector.reciprocal(rsum[:], sums[:]).then_inc(s["inverse_ready"], 1)
                if ahead:
                    rows_split(n + 1)
                if before:
                    new_context(n - 1, pg, static and n - 1 >= (T_ITER - 1) * NG)

            v.wait_ge(s["pl_ready"], 1)
            joint(0, 0)
            v.wait_ge(s["adj_loaded"], 16)
            masks(0)
            masks(1)
            rows_rest(0)
            rows_second(0)
            rows_split(0)
            v.wait_ge(s["v_share_product"], 1)
            nc.vector.tensor_copy(VL[:, 0:GB, :].rearrange("p b d -> p (b d)"), bank[3][:]).then_inc(s["v_share_first_kept"], 1)
            masks(2)
            masks(3)
            v.wait_ge(s["v_share_first_kept"], 1)
            v.wait_ge(s["v_share_kept"], NG - 1)
            for g in range(NG):
                v.wait_ge(s["masks_ready"], (TYPES + 1) * (g + 1))
                slot(g, 0, g, True)
            with v.Fori(1, T_ITER - 1) as t:
                for g in range(NG):
                    slot(t * NG + g, t, g, False)
            t = T_ITER - 1
            for g in range(NG):
                slot(t * NG + g, t, g, True, ahead=g < NG - 1)

            nc.vector.tensor_copy(wx[:, :, 0:32], w("wxp").rearrange("p (c n) -> p c n", c=OC)).then_inc(s["xproj_weights_ready"], 1)

            tr = [bank[4 + b // 2][:, (b % 2) * DI:(b % 2 + 1) * DI] for b in range(GB)]

            def convolve(g):
                if g:
                    v.wait_ge(s["silu_ready"], 2 * g)
                v.wait_ge(s["widened_ready"], 2 * g + 1)
                o = cv.rearrange("p (b t) -> p b t", b=GB)
                for k in range(TAPS):
                    wk = w("conv", k, k + 1)
                    src = xpad[:, 0, :, k:k + S]
                    if k == 0:
                        nc.vector.tensor_scalar(o, src, wk, w("bconv", 0, 1), ALU.mult, ALU.add).then_inc(s["conv0_step"], 1)
                    else:
                        v.wait_ge(s["conv0_step"], TAPS * g + k)
                        stt(o, src, wk, o, ALU.mult, ALU.add).then_inc(s["conv0_step"], 1)

            def moments(g):
                v.wait_ge(s["silu_turned"], g + 1)
                for b in range(GB):
                    nc.vector.bn_stats(st[:, b, :], tr[b]).then_inc(s["stats_ready"], 1)
                for b in range(GB):
                    v.wait_ge(s["stats_ready"], GB * g + b + 1)
                    nc.vector.bn_aggr(mv[:, b, :], st[:, b, :]).then_inc(s["moments_ready"], 1)

            def normalize(g):
                if g > 1:
                    v.wait_ge(s["squares_summed"], GB * (g - 1))
                    v.wait_ge(s["xn_rest_ready"], g - 1)
                v.wait_ge(s["moments_ready"], GB * (g + 1))
                for b in range(GB):
                    stt(XN[g % 2][:, b, :], tr[b], mv[:, b, 0:1], rows_sb[:, 0, :], ALU.subtract, ALU.mult).then_inc(s["centred_ready"], 1)
                v.wait_ge(s["deviation_ready"], g + 1)
                nc.vector.reciprocal(rstd[:], sd[:]).then_inc(s["inverse_deviation_ready"], 1)
                v.wait_ge(s["inverse_deviation_ready"], g + 1)
                for b in range(GB):
                    v.wait_ge(s["centred_ready"], GB * g + b + 1)
                    x = stt(XN[g % 2][:, b, :], XN[g % 2][:, b, :], rstd[:, b:b + 1], rows_sb[:, 1, :], ALU.mult, ALU.add)
                x.then_inc(s["xn_ready"], 1)

            def third_part(g):
                v.wait_ge(s["xn_part2_ready"], g + 1)
                v.wait_ge(s["xn_rest_ready"], g + 1)
                bs = slice(g * GB, (g + 1) * GB)
                tt(XP[:, 2, bs, :], RR[:], XP[:, 1, bs, :], ALU.subtract).then_inc(s["xn_part3_ready"], 1)

            v.wait_ge(s["eps_ready"], 1)
            v.wait_ge(s["spread_and_ln_loaded"], 32)
            v.wait_ge(s["pad_zeroed"], 1)
            last = T_ITER * NG - 1
            convolve(0)
            message(last, T_ITER - 1, NG - 1)
            for g in range(NG):
                moments(g)
                if g + 1 < NG:
                    widen(g + 1)
                normalize(g)
                if g == 0:
                    new_context(last, NG - 1, True)
                if g + 1 < NG:
                    convolve(g + 1)
                if g:
                    third_part(g - 1)
            g = NG - 1
            bs = slice(g * GB, (g + 1) * GB)
            v.wait_ge(s["xn_ready"], NG)
            nc.vector.tensor_copy(XP[:, 0, bs, :], XN[g % 2][:]).then_inc(s["xn_part1_ready"], 1)
            v.wait_ge(s["xn_part1_ready"], NG)
            v.wait_ge(s["xn_part3_ready"], NG - 1)
            tt(RR[:], XN[g % 2][:], XP[:, 0, bs, :], ALU.subtract).then_inc(s["xn_rest_ready"], 1)
            v.wait_ge(s["xn_rest_ready"], NG)
            nc.vector.tensor_copy(XP[:, 1, bs, :], RR[:]).then_inc(s["xn_part2_ready"], 1)
            third_part(g)
            v.wait_ge(s["norm_ready"], 1)
            nc.vector.tensor_scalar(nf, nrm[:].rearrange("p (b o) -> p b o", o=1).broadcast_to((P, B, NST)), 1.0, None,
                                    ALU.min).then_inc(s["norm_factor_ready"], 1)

            v.wait_ge(s["tanh_alog_ready"], 1)
            nc.vector.tensor_scalar(nA[:], nA[:], -0.01, None, ALU.mult).then_inc(s["minus_a_ready"], 1)
            v.wait_ge(s["xn_part3_ready"], NG)
            nc.vector.memset(H[:, 3], 0.0).then_inc(s["a_or_h_ready"], 1)
            v.wait_ge(s["abc_loaded"], 16 * 3)
            v.wait_ge(s["norm_rows_product"], 1)
            tt(ABC[:, :, 0, :], ABC[:, :, 0, :], bank[7][:, 0:2 * S].rearrange("p (h t) -> p h t", h=2), ALU.mult).then_inc(s["b_rows_ready"], 1)
            v.wait_ge(s["tanh_dt_ready"], 1)
            v.wait_ge(s["minus_a_ready"], 1)
            nc.vector.tensor_scalar(ABC[:, :, 2, :], ABC[:, :, 2, :], nA[:], 1.0, ALU.mult, ALU.add).then_inc(s["a_or_h_ready"], 1)
            v.wait_ge(s["a_or_h_ready"], 2)

            def blk(nb, j, warm):
                t0 = nb * TB
                v.wait_ge(s["a_of_block"], nb + 1)
                for k in range(TB):
                    t = t0 + k
                    for h in range(2):
                        v.wait_ge(s["d_ready"], 2 * t + h + 1)
                        if not (warm and k == 0):
                            v.wait_ge(s["h_ready"], 2 * t + h - 1)
                        stt(U[:, h, :], H[:, (k + 3) % 4, h, :], ablk[:, j, h, k:k + 1], Dt[:, k % 4, h, :],
                            ALU.mult, ALU.add).then_inc(s["u_ready"], 1)
                    for h in range(2):
                        v.wait_ge(s["u_ready"], 2 * t + h + 1)
                        if not (warm and k < 4):
                            v.wait_ge(s["y_step"], 2 * (t - 3) + h - 1)
                        nc.vector.tensor_scalar(H[:, k % 4, h, :], U[:, h, :], 10.0, -10.0, ALU.min, ALU.max).then_inc(s["h_ready"], 1)
            for nb in range(4):
                blk(nb, nb % 2, nb == 0)
            with v.Fori(1, NBLK // 4) as it:
                for j in range(4):
                    blk(it * 4 + j, j % 2, False)
            gate(v, nc.vector, NBLK - 1)
            result(v, nc.vector, NBLK - 1)

        @block.scalar
        def _(act):
            def a_(o, i, f, bias=0.0, scale=1.0, **k):
                return nc.scalar.activation(o, i, f, bias=bias, scale=scale, **k)

            act.wait_ge(s["question_negative"], 1)
            a_(qexp[:], qneg[:], ACT.Exp).then_inc(s["question_exp"], 1)

            def share_of_pp(g):
                act.wait_ge(s["pl_product"], g + 1)
                a_(grp(PL, g), bank[3 + g][:], ACT.Identity, bias=w("bpl")).then_inc(s["pl_ready"], 1)

            def first_context(g):
                a_(grp(XC, g), grp(MB, g), ACT.Copy, scale=w("init")).then_inc(s["first_context_ready"], 1)

            share_of_pp(0)
            for c in range(3):
                act.wait_ge(s["key_fold_product"], c + 1)
                a_(ak[:, c].rearrange("p t n -> p (t n)"), bank[[1, 7, 0][c]][:, 0:256], ACT.Copy).then_inc(s["key_fold_ready"], 1)
            act.wait_ge(s["mask_first_loaded"], 16)
            first_context(0)
            act.wait_ge(s["row_bias_ready"], 2)

            def rows(n):
                act.wait_ge(s["rows_product"], n + 1)
                act.wait_ge(s["rest1_ready"], n)
                a_(vrow[:], bank[1][:], ACT.Identity, bias=cb[:, bass.ds(n, 1)]).then_inc(s["rows_ready"], 1)

            def slot(n, g, static, more=True, ahead=True):
                if more:
                    if static and n < NG:
                        act.wait_ge(s["masks_ready"], (TYPES + 1) * (n + 1))
                    act.wait_ge(s["leaky_ready"], n)
                    a_(ES[:], BASE[:, GC[g]], ACT.Copy).then_inc(s["base_copied"], 1)
                if not (static and n == 0):
                    act.wait_ge(s["probs_turned"], n)
                    if not (static and n == 1):
                        act.wait_ge(s["message_product"], n - 1)
                    a_(PTs[:], bank[7][:], ACT.Copy).then_inc(s["probs_turned_copied"], 1)
                if more:
                    if ahead:
                        rows(n + 1)
                    act.wait_ge(s["max_ready"], n + 1)
                    act.wait_ge(s["inverse_ready"], n)
                    for b in range(GB):
                        cs = slice(b * S, (b + 1) * S)
                        a_(Pr[:, cs], E[:, cs], ACT.Exp, bias=nmax[:, b:b + 1], accum_out=sums[:, b:b + 1]).then_inc(s["exp_ready"], 1)

            rows(0)
            for g in range(1, NG):
                share_of_pp(g)
            for g in range(1, NG):
                act.wait_ge(s["v_share_product"], g + 1)
                a_(VL[:, g * GB:(g + 1) * GB, :].rearrange("p b d -> p (b d)"), bank[3 + g][:], ACT.Copy).then_inc(s["v_share_kept"], 1)
            act.wait_ge(s["mask_loaded"], 16)
            for g in range(1, NG):
                first_context(g)
            act.wait_ge(s["dt_fold_product"], 1)
            a_(wx[:, :, 32:48], bank[7][:, 0:2 * NST].rearrange("p (c n) -> p c n", c=OC), ACT.Copy).then_inc(s["xproj_weights_ready"], 1)
            a_(w("wmun"), bank[7][:, P:3 * P], ACT.Copy).then_inc(s["xproj_weights_ready"], 1)
            a_(w("bcb"), bank[7][:, 3 * P:3 * P + 1], ACT.Identity, bias=w("bcb")).then_inc(s["xproj_weights_ready"], 1)
            for g in range(NG):
                slot(g, g, True)
            with act.Fori(1, T_ITER - 1) as t:
                for g in range(NG):
                    slot(t * NG + g, g, False)
            for g in range(NG):
                slot((T_ITER - 1) * NG + g, g, True, ahead=g < NG - 1)

            def gates(g):
                for c in range(OC):
                    act.wait_ge(s["win_product"], 4 * g + 2 + c + 1)
                    a_(grp(GATE[:, c], g), bank[(3, 6)[c]][:], ACT.Silu).then_inc(s["gate_ready"], 1)

            def activate(g, c):
                if g:
                    act.wait_ge(s["silu_turned"], g)
                if c == 0:
                    act.wait_ge(s["conv0_step"], TAPS * (g + 1))
                    a_(XS[:, c, :], cv, ACT.Silu).then_inc(s["silu_ready"], 1)
                    a_(warm_in[:], eps[:], ACT.Sqrt).then_inc(s["sqrt_table_in"], 1)
                else:
                    act.wait_ge(s["conv1_product"], g + 1)
                    a_(XS[:, c, :], bank[2][:], ACT.Silu, bias=w("bconv", 1, 2)).then_inc(s["silu_ready"], 1)

            def deviation(g):
                act.wait_ge(s["moments_ready"], GB * (g + 1))
                act.wait_ge(s["inverse_deviation_ready"], g)
                a_(sd[:], mv[:, :, 1], ACT.Sqrt, bias=eps[:]).then_inc(s["deviation_ready"], 1)

            def squares(g):
                act.wait_ge(s["xn_ready"], g + 1)
                for b in range(GB):
                    at = g * GB + b
                    junk = XP[:, 1, at, :] if g < NG - 1 else cv[:, (b % 2) * DI:(b % 2 + 1) * DI]
                    if g == NG - 1 and b > 1:
                        act.wait_ge(s["squares_summed"], GB * g + b - 1)
                    a_(junk, XN[g % 2][:, b, :], ACT.Square, accum_out=ssq[:, at:at + 1]).then_inc(s["squares_summed"], 1)

            def turned(g):
                for c in range(OC):
                    act.wait_ge(s["xn_turned"], 2 * g + c + 1)
                    a_(grp(XNT[:, c], g), bank[4 + c][:], ACT.Copy).then_inc(s["xnt_ready"], 1)

            def first_part(g):
                act.wait_ge(s["xn_ready"], g + 1)
                a_(XP[:, 0, g * GB:(g + 1) * GB, :], XN[g % 2][:], ACT.Copy).then_inc(s["xn_part1_ready"], 1)

            def second_part(g):
                act.wait_ge(s["xn_rest_ready"], g + 1)
                act.wait_ge(s["squares_summed"], GB * (g + 1))
                a_(XP[:, 1, g * GB:(g + 1) * GB, :], RR[:], ACT.Copy).then_inc(s["xn_part2_ready"], 1)

            def projected(g):
                act.wait_ge(s["proj_product"], g + 1)
                a_(PR[:, GC[g]], bank[0][0:48, :], ACT.Copy).then_inc(s["proj_ready"], 1)

            act.wait_ge(s["eps_ready"], 1)
            gates(0)
            slot(T_ITER * NG, 0, True, more=False)
            activate(0, 1)
            activate(0, 0)
            for g in range(NG):
                deviation(g)
                if g + 1 < NG:
                    gates(g + 1)
                if g:
                    second_part(g - 1)
                    projected(g - 1)
                if g + 1 < NG:
                    activate(g + 1, 1)
                    first_part(g)
                    turned(g)
                    activate(g + 1, 0)
                    squares(g)
            turned(NG - 1)
            squares(NG - 1)
            act.wait_ge(s["squares_summed"], GB * NG)
            a_(nrm[:], ssq[:], ACT.Sqrt).then_inc(s["norm_ready"], 1)
            a_(nA[:], w("alog"), ACT.Tanh).then_inc(s["tanh_alog_ready"], 1)
            projected(NG - 1)
            proj_out(act, NG - 1)
            act.wait_ge(s["proj_last_stored"], 16 * 3)
            rows_abc(act, HB + GB, B)
            act.wait_ge(s["abc_loaded"], 16 * 3)
            a_(ABC[:, :, 2, :], ABC[:, :, 2, :], ACT.Tanh, bias=w("bdt")).then_inc(s["tanh_dt_ready"], 1)
            act.wait_ge(s["b_rows_ready"], 1)

            def blk(nb, j, tail, warm):
                t0 = nb * TB
                for k in range(TB):
                    t = t0 + k
                    act.wait_ge(s["x_spread"], t + 1)
                    if not (warm and k < 4):
                        act.wait_ge(s["u_ready"], 2 * (t - 3))
                    for h in range(2):
                        a_(Dt[:, k % 4, h, :], bank[k % 2][:, h * DI:(h + 1) * DI], ACT.Copy,
                           scale=ABC[:, h, 0, bass.ds(t, 1)]).then_inc(s["d_ready"], 1)
                    if tail and k == 0 and not (isinstance(nb, int) and nb == 1):
                        copy_out(nb - 2)
                    if tail and k == 1:
                        copy_y(nb - 1, 1 - j)
                    if tail and k == 4:
                        copy_z(nb - 1)

            def copy_y(nb, j):
                for h in range(2):
                    act.wait_ge(s["y_step"], 2 * (nb + 1) * TB)
                    if not (isinstance(nb, int) and nb == 0):
                        act.wait_ge(s["y_turned"], nb)
                    yb = bank[2 + 2 * j + h][0:TB * HB, 0:DI]
                    a_(YS[0:TB * HB, h, :], yb, ACT.Copy).then_inc(s["y_copied"], 1)

            def copy_z(nb):
                act.wait_ge(s["y_turned"], nb + 1)
                if not (isinstance(nb, int) and nb == 0):
                    act.wait_ge(s["out_product"], nb)
                a_(z.rearrange("p c t b -> p (c t b)"), bank[6][:, 0:OC * TB * B], ACT.Copy).then_inc(s["z_copied"], 1)

            def copy_out(nb):
                act.wait_ge(s["out_product"], nb + 1)
                if not (isinstance(nb, int) and nb == 0):
                    act.wait_ge(s["out_ready"], nb)
                a_(ob, bank[7][:, 0:TB * B], ACT.Copy).then_inc(s["out_copied"], 1)

            blk(0, 0, False, True)
            blk(1, 1, True, False)
            blk(2, 0, True, False)
            blk(3, 1, True, False)
            with act.Fori(2, NBLK // 2) as it:
                blk(it * 2, 0, True, False)
                blk(it * 2 + 1, 1, True, False)
            copy_out(NBLK - 2)
            copy_y(NBLK - 1, 1)
            copy_z(NBLK - 1)
            copy_out(NBLK - 1)

        @block.gpsimd
        def _(pool):
            cp = nc.gpsimd.tensor_copy
            nc.gpsimd.memset(arep[:], 0.0).then_inc(s["zeroed"], 1)
            nc.gpsimd.memset(xpad[:], 0.0).then_inc(s["pad_zeroed"], 1)
            pool.wait_ge(s["zeroed"], 2)
            pool.wait_ge(s["query_fold"], 2)

            def key_cols(t, g):
                src = ak[:, :, bass.ds(t, 1), g * ROWS_OF:(g + 1) * ROWS_OF]
                o = arep[:, :, g, 64:112].rearrange("p c (a n) -> p c a n", n=ROWS_OF)
                return cp(o, src.broadcast_to((P, 3, PARTS, ROWS_OF)))

            for g in range(NG):
                for c in range(3):
                    cp(arep[:, c, g, 0:48].rearrange("p (a k) -> p a k", k=TYPES),
                       aq[:, c, :].rearrange("p (o k) -> p o k", o=1).broadcast_to((P, 12, TYPES)))
                pool.wait_ge(s["key_fold_ready"], 3)
                key_cols(0, g).then_inc(s["row_weights_ready"], 1)
            nc.gpsimd.memset(cmat[:], 0.0).then_inc(s["cmat_zeroed"], 1)

            def slot(n, t, g, final):
                if not final:
                    pool.wait_ge(s["rows_product"], n + 1)
                    passed(pool, "passed_pool")
                    key_cols(t + 1, g).then_inc(s["row_weights_ready"], 1)
                pool.wait_ge(s["inverse_ready"], n + 1)
                p3 = Pr[:].rearrange("p (b t) -> p b t", b=GB)
                nc.gpsimd.tensor_tensor(p3, p3, rsum[:].rearrange("p (b o) -> p b o", o=1).broadcast_to((P, GB, S)),
                                        ALU.mult).then_inc(s["probs_ready"], 1)

            for g in range(NG):
                slot(g, 0, g, False)
            with pool.Fori(1, T_ITER - 1) as t:
                for g in range(NG):
                    slot(t * NG + g, t, g, False)
            for g in range(NG):
                if g == NG - 1:
                    pool.wait_ge(s["rows_product"], T_ITER * NG)
                    for k in range(TAPS):
                        nc.gpsimd.tensor_tensor(diag[:, k, :], w("ident"),
                                                w("conv", TAPS + k, TAPS + k + 1).broadcast_to((P, P)), ALU.mult).then_inc(s["diag_ready"], 1)
                slot((T_ITER - 1) * NG + g, T_ITER - 1, g, True)

            def rest(g):
                pool.wait_ge(s["xn_part1_ready"], g + 1)
                pool.wait_ge(s["xn_part3_ready"], g)
                nc.gpsimd.tensor_tensor(RR[:], XN[g % 2][:], XP[:, 0, g * GB:(g + 1) * GB, :], ALU.subtract).then_inc(s["xn_rest_ready"], 1)

            def skip(g):
                pool.wait_ge(s["proj_product"], g + 1)
                for c in range(OC):
                    nc.gpsimd.tensor_tensor(grp(XNT[:, c], g), grp(XNT[:, c], g),
                                            w("dskip", c, c + 1).broadcast_to((P, GT)), ALU.mult).then_inc(s["skip_done"], 1)

            for g in range(NG - 1):
                rest(g)
                if g:
                    skip(g - 1)
            skip(NG - 2)
            skip(NG - 1)

            pool.wait_ge(s["cmat_zeroed"], 1)
            pool.wait_ge(s["abc_loaded"], 16 * 3)
            pool.wait_ge(s["a_or_h_ready"], 2)

            def fill(nb, j):
                cp(ablk[:, j], ABC[:, :, 2, bass.ds(nb * TB, TB)]).then_inc(s["a_of_block"], 1)
                for h in range(2):
                    o = cmat[:, h, j, :].rearrange("p (k n) -> p k n", k=TB)[:, :, 0:HB]
                    c3 = ABC[:, h, 1, bass.ds(nb * TB, TB)].rearrange("p (t o) -> p t o", o=1).broadcast_to((P, TB, HB))
                    m3 = w("half8").rearrange("p (o b) -> p o b", o=1).broadcast_to((P, TB, HB))
                    nc.gpsimd.tensor_tensor(o, c3, m3, ALU.mult).then_inc(s["c_filled"], 1)

            fill(0, 0)
            fill(1, 1)

            pool.wait_ge(s["skip_done"], OC * NG)
            for nb in range(2):
                pool.wait_ge(s["y_step"], 2 * (nb + 1) * TB)
                fill(nb + 2, nb)
                if nb:
                    result(pool, nc.gpsimd, nb - 1)
                gate(pool, nc.gpsimd, nb)
            with pool.Fori(1, NBLK // 2 - 1) as it:
                for j in range(2):
                    nb = it * 2 + j
                    pool.wait_ge(s["y_step"], 2 * (nb + 1) * TB)
                    fill(nb + 2, j)
                    result(pool, nc.gpsimd, nb - 1)
                    gate(pool, nc.gpsimd, nb)
            result(pool, nc.gpsimd, NBLK - 3)
            gate(pool, nc.gpsimd, NBLK - 2)
            result(pool, nc.gpsimd, NBLK - 2)


def _sel_constants():
    import numpy as np
    one = 0x3F80
    sel = np.zeros((P, 2, ROWS_OF, P), np.uint16)
    for p in range(P):
        if p % 64 < PARTS * ROWS_OF:
            sel[p, p // 64, p % 64 % ROWS_OF, :] = one
    spread = np.zeros((PARTS * B, 2, P), np.uint16)
    for p in range(PARTS * B):
        b = p // (PARTS * GB) * GB + p % GB
        spread[p, b // HB, (b % HB) * NST:(b % HB + 1) * NST] = one
    return sel.reshape(P, -1), spread.reshape(PARTS * B, -1)


def kernel(**inputs):
    import numpy as np
    import concourse.bacc as bacc
    from concourse.bass_utils import run_bass_kernel_spmd

    i = {k: np.asarray(v) for k, v in inputs.items()}
    L0 = {k[8:]: v for k, v in i.items() if k.startswith("L0_cond_")}
    L1 = {k[8:]: v for k, v in i.items() if k.startswith("L1_cond_")}

    def chunks(a):
        return a.reshape(-1, P, a.shape[-1]).transpose(1, 0, 2).reshape(P, -1)

    part = np.arange(P) % 64 // ROWS_OF
    col = lambda a: a.reshape(-1, 1)
    f = {
        "ident": np.eye(P, dtype=np.float32), "wqin": L0["w_qin"].T,
        "wqt": i["fside_BxSxS_0"][:T_ITER].transpose(2, 0, 1).reshape(P, -1),
        "wpl": L0["w_pl"].T, "wpc": L0["w_pc"].T, "wq": L0["w_q"], "wk": L0["w_k"],
        "wv": chunks(L0["w_v"].T), "wpk": L0["w_pk"].T, "wpv": L0["w_pv"].T,
        "wmu": chunks(L0["w_mu"].T), "wmun": L0["w_mu"], "wcb": chunks(L0["w_cb"].T), "win": L1["W_in"].T,
        "wxp": chunks(L1["W_xproj"].T[:, 0:32]), "wout": chunks(L1["W_out"].T),
        "cond": chunks(i["cond_2048"].T), "qenc": i["fside_BxS_0"].T,
        "bqin": col(L0["b_qin"]), "bqt": i["mask_BxS_ff0"][:T_ITER].T, "bpl": col(L0["b_pl"]),
        "bpc": col(L0["b_pc"]), "bq": col(L0["b_q"]), "bk": col(L0["b_k"]), "bv": col(L0["b_v"]),
        "bpk": col(L0["b_pk"]), "bpv": col(L0["b_pv"]), "bmu": col(L0["b_mu"]), "bcb": col(L0["b_cb"]),
        "init": L0["init_mem"].T, "conv": chunks(L1["W_conv"][:, 0, :]), "bconv": chunks(col(L1["b_conv"])),
        "dskip": chunks(col(L1["D"])),
        "bdt": col(np.tile(L1["b_dt"], HB)), "alog": col(np.tile(L1["A_log"], HB)),
        "nm12": col(np.where(part >= 1, -1.0, 0.0).astype(np.float32)),
        "nm3": col(np.where(part >= 2, -1.0, 0.0).astype(np.float32)),
        "half8": np.repeat(np.eye(HB, dtype=np.float32), NST, axis=0),
    }
    w128 = np.concatenate([f[n] for n, _ in COLS], axis=1)
    w16 = np.concatenate([L1["W_xproj"][32:48], L1["W_dt"].T], axis=1)
    sel, spread = _sel_constants()
    arrays = {
        "xT": i["x"].transpose(2, 0, 1).reshape(P, TOK), "adj": i["itok_BxSxS_0_4"].transpose(1, 0, 2).reshape(P, TOK),
        "w128": w128, "w16": w16, "mask": i["mask_BxS_ff1"].reshape(1, TOK),
        "rows": np.concatenate([L1["ln_g"], L1["ln_b"]]).reshape(1, 2 * DI), "sel": sel, "spread": spread,
    }
    arrays = {k: np.ascontiguousarray(v) for k, v in arrays.items()}
    nc = bacc.Bacc("TRN2", target_bir_lowering=False, num_devices=1)
    args = [nc.dram_tensor(k, a.shape, mybir.dt.from_np(a.dtype), kind="ExternalInput").ap() for k, a in arrays.items()]
    out = nc.dram_tensor("outT", (P, TOK), F32, kind="ExternalOutput").ap()
    build_program(nc, *args, out)
    r = run_bass_kernel_spmd(nc, [arrays], core_ids=[0])
    y = np.asarray(r.results[0]["outT"])
    return np.ascontiguousarray(y.reshape(D, S, B).transpose(2, 1, 0))
```
